# Optimizing a Trainium2 kernel written in Bass

```python
import numpy as np
import jax
import jax.numpy as jnp

def _softmax(x, axis=-1):
    return jax.nn.softmax(x, axis=axis)

def _gelu(x):
    return jax.nn.gelu(x, approximate=True)

def _silu(x):
    return jax.nn.silu(x)

def _sigmoid(x):
    return jax.nn.sigmoid(x)

def _layernorm(x, axis=-1, eps=1e-05):
    m = jnp.mean(x, axis=axis, keepdims=True)
    v = jnp.var(x, axis=axis, keepdims=True)
    return (x - m) / jnp.sqrt(v + eps)

def _scatter_add(tgt, idx, src, axis=0):
    return tgt.at[idx].add(src)

def _segment_sum(src, seg, n):
    return jax.ops.segment_sum(src, seg, n)
kernel_name = 'mk_gnn_ffn_d1_gnn_r8_4b72e1'

def setup_inputs(seed: int=0):
    np.random.seed(seed)
    _w = jnp.asarray

    def _rec_inputs():
        import jax
        import jax.numpy as jnp
        _gk = jax.random.key(seed)
        x = -0.0003713 + 1 * jax.random.normal(jax.random.fold_in(_gk, 1), (6250, 256), jnp.float32)
        src = jax.random.randint(jax.random.fold_in(_gk, 2), (100000,), 0, 6250, jnp.int32)
        dst = jnp.minimum((6250 * jax.random.uniform(jax.random.fold_in(_gk, 3), (100000,)) ** 2.0).astype(jnp.int32), 49999)
        _o = jnp.argsort(dst, stable=True)
        src = src[_o]
        dst = dst[_o]
        return (x, src, dst)
    x, src, dst = _rec_inputs()

    def _L0_gnn_setup():
        import jax, jax.numpy as jnp
        import numpy as np
        N_NODES = 6250
        N_EDGES = 100000
        F_IN = 256
        HID = 256

        def _gcn_conv(x, W, b, src, dst, num_nodes):
            h = x @ W
            deg = jax.ops.segment_sum(jnp.ones(src.shape[0], dtype=h.dtype), dst, num_segments=num_nodes)
            dinv = jnp.where(deg > 0, jax.lax.rsqrt(deg), 0.0)
            norm = dinv[src] * dinv[dst]
            msg = h[src] * norm[:, None]
            out = jax.ops.segment_sum(msg, dst, num_segments=num_nodes)
            return out + b
        key = jax.random.key(seed)
        ks = jax.random.split(key, 6)
        x = jax.random.normal(ks[0], (N_NODES, F_IN), dtype=jnp.float32)
        edge_index = jax.random.randint(ks[1], (2, N_EDGES), 0, N_NODES, dtype=jnp.int64)
        W1 = jax.random.normal(ks[2], (F_IN, HID), dtype=jnp.float32) * (1.0 / np.sqrt(F_IN))
        b1 = jnp.zeros((HID,), dtype=jnp.float32)
        W2 = jax.random.normal(ks[3], (HID, HID), dtype=jnp.float32) * (1.0 / np.sqrt(HID))
        b2 = jnp.zeros((HID,), dtype=jnp.float32)
        return {'x': x, 'edge_index': edge_index, 'W1': W1, 'b1': b1, 'W2': W2, 'b2': b2}
    _L0_gnn_all = _L0_gnn_setup()
    _L0_gnn_in = {k: v for k, v in _L0_gnn_all.items() if k in ('W1', 'b1', 'W2', 'b2')}
    del _L0_gnn_all

    def _L0_ffn_setup():
        import jax, jax.numpy as jnp
        import numpy as np
        B, N, D = (16, 512, 256)
        NUM_EXPERTS, TOP_K, HEADS = (4, 2, 4)
        N_EDGES = 131072
        LN_EPS = 1e-05

        def _layernorm(x, g, b):
            mu = x.mean(-1, keepdims=True)
            var = ((x - mu) ** 2).mean(-1, keepdims=True)
            return (x - mu) * jax.lax.rsqrt(var + LN_EPS) * g + b

        def _forward(x, edge_index, W_gat, att_src, att_dst, b_gat, ln_gamma, ln_beta, W1, b1, W2, b2):
            Bc, Nc, Dc = x.shape
            M = Bc * Nc
            x_flat = x.reshape(M, Dc)
            h = (x_flat @ W_gat).reshape(M, HEADS, NUM_EXPERTS)
            loops = jnp.arange(M, dtype=edge_index.dtype)
            src = jnp.concatenate([edge_index[0], loops])
            dst = jnp.concatenate([edge_index[1], loops])
            a_src = (h * att_src).sum(-1)
            a_dst = (h * att_dst).sum(-1)
            e = jax.nn.leaky_relu(a_src[src] + a_dst[dst], negative_slope=0.2)
            e_max = jax.ops.segment_max(e, dst, num_segments=M)
            ee = jnp.exp(e - e_max[dst])
            denom = jax.ops.segment_sum(ee, dst, num_segments=M)
            alpha = ee / (denom[dst] + 1e-16)
            msg = h[src] * alpha[:, :, None]
            agg = jax.ops.segment_sum(msg, dst, num_segments=M).reshape(M, HEADS * NUM_EXPERTS) + b_gat
            scores = _layernorm(agg, ln_gamma, ln_beta).reshape(M, HEADS, NUM_EXPERTS).mean(1)
            scores = scores.reshape(Bc, Nc, NUM_EXPERTS)
            topk_s, topk_i = jax.lax.top_k(scores, TOP_K)
            w = jax.nn.softmax(topk_s, axis=-1)
            out = jnp.zeros_like(x)
            for ei in range(NUM_EXPERTS):
                g = jnp.where(topk_i == ei, w, 0.0).sum(-1)
                hh = jax.nn.gelu(x @ W1[ei] + b1[ei], approximate=False)
                out = out + g[..., None] * (hh @ W2[ei] + b2[ei])
            return out
        key = jax.random.key(seed)
        ks = jax.random.split(key, 8)
        s = 0.05
        return {'x': jax.random.normal(ks[0], (B, N, D), jnp.float32), 'W_gat': jax.random.normal(ks[1], (D, HEADS * NUM_EXPERTS), jnp.float32) * s, 'att_src': jax.random.normal(ks[2], (HEADS, NUM_EXPERTS), jnp.float32) * s, 'att_dst': jax.random.normal(ks[3], (HEADS, NUM_EXPERTS), jnp.float32) * s, 'b_gat': jnp.zeros((HEADS * NUM_EXPERTS,), jnp.float32), 'ln_gamma': jnp.ones((HEADS * NUM_EXPERTS,), jnp.float32), 'ln_beta': jnp.zeros((HEADS * NUM_EXPERTS,), jnp.float32), 'W1': jax.random.normal(ks[4], (NUM_EXPERTS, D, 2 * D), jnp.float32) * s, 'b1': jnp.zeros((NUM_EXPERTS, 2 * D), jnp.float32), 'W2': jax.random.normal(ks[5], (NUM_EXPERTS, 2 * D, D), jnp.float32) * s, 'b2': jnp.zeros((NUM_EXPERTS, D), jnp.float32), 'edge_index': jax.random.randint(ks[6], (2, N_EDGES), 0, B * N, jnp.int32)}
    _L0_ffn_all = _L0_ffn_setup()
    _L0_ffn_in = {k: v for k, v in _L0_ffn_all.items() if k in ('W_gat', 'att_src', 'att_dst', 'b_gat', 'ln_gamma', 'ln_beta', 'W1', 'b1', 'W2', 'b2', 'edge_index')}
    del _L0_ffn_all
    return {'x': x, 'src': src, 'dst': dst, 'L0_gnn_W1': _L0_gnn_in['W1'], 'L0_gnn_b1': _L0_gnn_in['b1'], 'L0_gnn_W2': _L0_gnn_in['W2'], 'L0_gnn_b2': _L0_gnn_in['b2'], 'L0_ffn_W_gat': _L0_ffn_in['W_gat'], 'L0_ffn_att_src': _L0_ffn_in['att_src'], 'L0_ffn_att_dst': _L0_ffn_in['att_dst'], 'L0_ffn_b_gat': _L0_ffn_in['b_gat'], 'L0_ffn_ln_gamma': _L0_ffn_in['ln_gamma'], 'L0_ffn_ln_beta': _L0_ffn_in['ln_beta'], 'L0_ffn_W1': _L0_ffn_in['W1'], 'L0_ffn_b1': _L0_ffn_in['b1'], 'L0_ffn_W2': _L0_ffn_in['W2'], 'L0_ffn_b2': _L0_ffn_in['b2'], 'L0_ffn_edge_index': _L0_ffn_in['edge_index']}

def reference(x, src, dst, L0_gnn_W1, L0_gnn_b1, L0_gnn_W2, L0_gnn_b2, L0_ffn_W_gat, L0_ffn_att_src, L0_ffn_att_dst, L0_ffn_b_gat, L0_ffn_ln_gamma, L0_ffn_ln_beta, L0_ffn_W1, L0_ffn_b1, L0_ffn_W2, L0_ffn_b2, L0_ffn_edge_index):
    import jax
    import jax.numpy as jnp

    def _L0_gnn_ref(x, edge_index, W1, b1, W2, b2):
        import jax, jax.numpy as jnp
        import numpy as np
        N_NODES = 6250
        N_EDGES = 100000
        F_IN = 256
        HID = 256

        def _gcn_conv(x, W, b, src, dst, num_nodes):
            h = x @ W
            deg = jax.ops.segment_sum(jnp.ones(src.shape[0], dtype=h.dtype), dst, num_segments=num_nodes)
            dinv = jnp.where(deg > 0, jax.lax.rsqrt(deg), 0.0)
            norm = dinv[src] * dinv[dst]
            msg = h[src] * norm[:, None]
            out = jax.ops.segment_sum(msg, dst, num_segments=num_nodes)
            return out + b
        num_nodes = x.shape[0]
        loop = jnp.arange(num_nodes, dtype=edge_index.dtype)
        src = jnp.concatenate([edge_index[0], loop])
        dst = jnp.concatenate([edge_index[1], loop])
        h = jax.nn.relu(_gcn_conv(x, W1, b1, src, dst, num_nodes))
        return _gcn_conv(h, W2, b2, src, dst, num_nodes)

    def _L0_ffn_ref(x, W_gat, att_src, att_dst, b_gat, ln_gamma, ln_beta, W1, b1, W2, b2, edge_index):
        import jax, jax.numpy as jnp
        import numpy as np
        B, N, D = (16, 512, 256)
        NUM_EXPERTS, TOP_K, HEADS = (4, 2, 4)
        N_EDGES = 131072
        LN_EPS = 1e-05

        def _layernorm(x, g, b):
            mu = x.mean(-1, keepdims=True)
            var = ((x - mu) ** 2).mean(-1, keepdims=True)
            return (x - mu) * jax.lax.rsqrt(var + LN_EPS) * g + b

        def _forward(x, edge_index, W_gat, att_src, att_dst, b_gat, ln_gamma, ln_beta, W1, b1, W2, b2):
            Bc, Nc, Dc = x.shape
            M = Bc * Nc
            x_flat = x.reshape(M, Dc)
            h = (x_flat @ W_gat).reshape(M, HEADS, NUM_EXPERTS)
            loops = jnp.arange(M, dtype=edge_index.dtype)
            src = jnp.concatenate([edge_index[0], loops])
            dst = jnp.concatenate([edge_index[1], loops])
            a_src = (h * att_src).sum(-1)
            a_dst = (h * att_dst).sum(-1)
            e = jax.nn.leaky_relu(a_src[src] + a_dst[dst], negative_slope=0.2)
            e_max = jax.ops.segment_max(e, dst, num_segments=M)
            ee = jnp.exp(e - e_max[dst])
            denom = jax.ops.segment_sum(ee, dst, num_segments=M)
            alpha = ee / (denom[dst] + 1e-16)
            msg = h[src] * alpha[:, :, None]
            agg = jax.ops.segment_sum(msg, dst, num_segments=M).reshape(M, HEADS * NUM_EXPERTS) + b_gat
            scores = _layernorm(agg, ln_gamma, ln_beta).reshape(M, HEADS, NUM_EXPERTS).mean(1)
            scores = scores.reshape(Bc, Nc, NUM_EXPERTS)
            topk_s, topk_i = jax.lax.top_k(scores, TOP_K)
            w = jax.nn.softmax(topk_s, axis=-1)
            out = jnp.zeros_like(x)
            for ei in range(NUM_EXPERTS):
                g = jnp.where(topk_i == ei, w, 0.0).sum(-1)
                hh = jax.nn.gelu(x @ W1[ei] + b1[ei], approximate=False)
                out = out + g[..., None] * (hh @ W2[ei] + b2[ei])
            return out
        return _forward(x, edge_index, W_gat, att_src, att_dst, b_gat, ln_gamma, ln_beta, W1, b1, W2, b2)
    edge_index = jnp.stack([src, dst])
    x = x + _L0_gnn_ref(_layernorm(x, axis=-1), edge_index, L0_gnn_W1, L0_gnn_b1, L0_gnn_W2, L0_gnn_b2)
    x = x + _L0_ffn_ref(_layernorm(x, axis=-1)[None], L0_ffn_W_gat, L0_ffn_att_src, L0_ffn_att_dst, L0_ffn_b_gat, L0_ffn_ln_gamma, L0_ffn_ln_beta, L0_ffn_W1, L0_ffn_b1, L0_ffn_W2, L0_ffn_b2, L0_ffn_edge_index)[0]
    return x

_drawn_inputs = setup_inputs


def setup_inputs(seed=0):
    import zlib

    import numpy as np

    out = dict(_drawn_inputs(seed))
    spreads = {'L0_gnn_b1': (0.0, 0.1),
     'L0_gnn_b2': (0.0, 0.1),
     'L0_ffn_b_gat': (0.0, 0.1),
     'L0_ffn_ln_gamma': (1.0, 0.2),
     'L0_ffn_ln_beta': (0.0, 0.1),
     'L0_ffn_b1': (0.0, 0.1),
     'L0_ffn_b2': (0.0, 0.1)}
    factors = {'L0_ffn_att_dst': 2.907}
    for name, (base, spread) in spreads.items():
        noise = np.random.default_rng([zlib.crc32(name.encode()), seed]).standard_normal(out[name].shape)
        drawn = base * np.exp(spread * noise) if base else spread * noise
        out[name] = jnp.asarray(drawn.astype(out[name].dtype))
    for name, factor in factors.items():
        out[name] = (out[name] * factor).astype(out[name].dtype)
    return out
```

```python
import numpy as np
import concourse.bass as bass
from concourse import mybir
from contextlib import ExitStack

F32, I32, F16, BF16 = mybir.dt.float32, mybir.dt.int32, mybir.dt.float16, mybir.dt.bfloat16
U16, I16 = mybir.dt.uint16, mybir.dt.int16
ALU = mybir.AluOpType
ACT = mybir.ActivationFunctionType
AX = mybir.AxisListType

P = 128
N = 6250
D = 256
NBIN = -(-N // P)
LAST = N - (NBIN - 1) * P
U = 4
NBP = -(-NBIN // U) * U
STEPS = NBP // U
ROWS = NBP * P
EXPERTS, HEADS, HID = 4, 4, 512
HE = HEADS * EXPERTS
REC = HE + HEADS
SEL = 24
G = 8
LN_EPS = 1e-5
BIG = float(2.0 ** 126)
KC = D // P
HC = HID // P


def tiles_bound(edges):
    most = (edges + NBIN * (P - 1)) // P
    return -(-most // (2 * G)) * 2 * G


class Counter:

    def __init__(self, eng, sem, base=0):
        self.eng, self.sem, self.base, self.n = eng, sem, base, 0

    def inc(self, ins):
        ins.then_inc(self.sem, 1)
        self.n += 1

    def wait(self):
        self.eng.wait_ge(self.sem, self.base + self.n)

    def step(self, ins):
        self.inc(ins)
        self.wait()


class Graph:
    def __init__(self, name, edges, src, dst, parts, with_degree, row_stride):
        self.name, self.src, self.dst = name, src, dst
        self.EP, self.T = parts, edges // parts
        self.NT = tiles_bound(edges)
        self.with_degree, self.row_stride = with_degree, row_stride
        w = -(-self.NT // 3)
        w += w % 2
        self.chunks = [(c * w, min(w, self.NT - c * w)) for c in range(3)]


def build(nc, x, src, dst, gW1, gb1, gW2, gb2, W_gat, att_src, att_dst, b_gat, ln_g, ln_b,
          W1, b1, W2, b2, edge_index, out):
    E1, E2 = src.shape[0], edge_index.shape[1]
    e1_parts = max(p for p in range(1, P + 1) if E1 % p == 0 and (E1 // p) % 4 == 0)
    g1 = Graph("gcn", E1, src, dst, e1_parts, True, D)
    g2 = Graph("gat", E2, edge_index[0, :], edge_index[1, :], P, False, SEL)
    TMAX = 1088
    assert max(g1.NT, g2.NT, g1.T, g2.T) <= TMAX and g2.T % 4 == 0

    def dram(name, shape, dt):
        return nc.dram_tensor(name, shape, dt, kind="Internal").ap()

    G1 = dram("gcn_table_1", (ROWS, D), F32)
    G2 = dram("gcn_table_2", (ROWS, D), F32)
    X2 = dram("x_after_gcn", (ROWS, D), F32)
    AT = dram("ffn_in_t", (KC * P, ROWS), F32)
    TR = dram("gat_table", (ROWS, REC), F32)
    Y = dram("expert_out", (ROWS, EXPERTS * D), F32)

    with ExitStack() as ctx:
        def sb(name, shape, dt):
            return ctx.enter_context(nc.sbuf_tensor(name, shape, dt))

        def sem(name):
            return ctx.enter_context(nc.semaphore(name))

        ACCF = NBP * D
        R = sb("big", [P, max(ACCF + 9 * TMAX, g2.NT * REC)], F32)
        acc = R[:, 0:ACCF]
        gat_rows = R[:, 0:g2.NT * REC].rearrange("p (t r) -> p t r", r=REC)

        def tmp(k, dt=F32):
            v = R[:, ACCF + k * TMAX:ACCF + (k + 1) * TMAX]
            return v if dt == F32 else v.bitcast(dt)

        src_i, dst_i, valA, valB = tmp(0, I32), tmp(1, I32), tmp(2), tmp(3)
        pos, run, plo, phi = tmp(4), tmp(5), tmp(6), tmp(7)
        bin16 = tmp(8, F16)[:, 0:TMAX]
        mask = tmp(8, U16)[:, TMAX:2 * TMAX]

        UN = sb("phase", [P, 6144], F32)
        oh_hi = UN[:, 0:4 * TMAX // 2].bitcast(F16).rearrange("p (k t) -> p k t", k=4)
        oh_lo = UN[:, 2 * TMAX:2 * TMAX + 4 * 3 * P // 2].bitcast(F16).rearrange(
            "p (k j n) -> p k j n", k=4, j=3)
        oh_bin = UN[:, 3072:3072 + 4 * 64 // 2].bitcast(F16).rearrange("p (k n) -> p k n", k=4)
        msg = UN[:, 0:G * D].rearrange("p (k n) -> p k n", k=G)
        at_in = UN[:, 0:KC * 512].rearrange("p (k n) -> p k n", k=KC)
        hid = UN[:, 1024:1024 + HC * 512].rearrange("p (c n) -> p c n", c=HC)
        y_sb = UN[:, 3072:3072 + 4 * D].rearrange("p (s n) -> p s n", s=4)
        y_in = UN[:, 0:U * EXPERTS * D].rearrange("p (u e n) -> p u e n", u=U, e=EXPERTS)
        x2_in = UN[:, 4096:4096 + U * D].rearrange("p (u n) -> p u n", u=U)
        o_sb = UN[:, 5120:5120 + U * D].rearrange("p (u n) -> p u n", u=U)

        for g in (g1, g2):
            g.idx = sb(g.name + "_idx", [P, g.NT], I32)
            g.dlo = sb(g.name + "_dlo", [P, g.NT], F16)
            g.row = sb(g.name + "_row", [1, g.NT], I16)
        stage = sb("stage", [P, 2, G], I32)
        ring = sb("ring", [P, 2, G * REC], F32)
        S = sb("sel", [P, G, P], F32)
        ST = sb("sel_t", [P, G, P], BF16)
        Z = sb("z", [P, G, 48], BF16)
        V = sb("v", [12, 2, 512], BF16)
        tiles = sb("node_tiles", [P, 4 * U * D], F32)
        xt, xn, x2t = [tiles[:, k * U * D:(k + 1) * U * D].rearrange("p (u n) -> p u n", u=U) for k in range(3)]
        aT = tiles[:, 3 * U * D:4 * U * D].rearrange("p (u k n) -> p u k n", u=U, k=KC)
        big = tiles[:, 0:2 * NBP * HE].rearrange("p (j t n) -> p j t n", j=2, t=NBP)
        v8 = tiles[:, 2 * NBP * HE:2 * NBP * HE + NBP * 8].rearrange("p (t n) -> p t n", n=8)
        r8 = tiles[:, 2 * NBP * HE + NBP * 8:2 * NBP * HE + NBP * 16].rearrange("p (t n) -> p t n", n=8)
        wg = [sb(f"gcn_w{i}", [P, KC, D], F32) for i in range(2)]
        wgat = sb("gat_w", [P, KC, HE], F32)
        w1s = sb("ffn_w1", [P, KC, HID], F32)
        w2s = sb("ffn_w2", [P, HC, D], F32)
        b1s = sb("ffn_b1", [P, EXPERTS * HC], F32)
        b2s = sb("ffn_b2", [P, EXPERTS * D], F32)
        bias = [sb(f"gcn_b{i}", [P, D], F32) for i in range(2)]
        vecs = sb("gat_vecs", [P, 5, HE], F32)
        st6 = sb("bn", [P, U, 6], F32)
        mv = sb("mean_var", [P, U, 4], F32)
        dinv = sb("dinv", [P, NBP], F32)
        iota16 = sb("iota16", [P, TMAX], F16)
        iota32 = sb("iota32", [P, P], F32)
        iobin = sb("iobin", [P, 64], F32)
        ident = sb("ident", [P, P], F32)
        ident16 = sb("ident16", [P, P], BF16)
        ones = sb("ones", [P, P], F32)
        ones16 = sb("ones16", [P, P], BF16)
        onesf16 = sb("onesf16", [P, 1], F16)
        zero16 = sb("zero16", [P, 512], F16)
        tri = sb("tri", [P, P], F32)
        H = sb("hist", [P, 64], F32)
        bn = sb("bin_small", [P, 6, 64], F32)
        bni = sb("bin_small_i", [P, 64], I32)
        tg = sb("gat_rec", [P, NBP, REC], F32)
        adst = sb("a_dst", [P, NBP, HEADS], F32)
        sc = [sb(f"score{k}", [P, NBP, EXPERTS], F32) for k in range(3)]
        one = [sb(f"one{k}", [P, NBP], F32) for k in range(2)]
        mx = sb("max_src", [P, NBP * SEL], F32)
        adp = sb("ad_parts", [P, NBP * SEL], BF16)
        acc2 = sb("gat_acc", [P, NBP * SEL], F32)
        gate = sb("gate", [P, NBP * EXPERTS], F32)
        red = sb("red", [P, G, HEADS], F32)
        asr = sb("as_res", [P, 2, G, HEADS], F32)
        ssel = sb("sel_vals", [P, G, SEL], F32)
        q8 = sb("q8", [P, G, 8], F32)
        ee = sb("ee", [P, 3, G, HEADS], F32)
        pay = sb("payload", [P, G, REC], F32)

        PS = [ctx.enter_context(nc.psum_tensor(f"ps{k}", [P, 512], F32)) for k in range(8)]

        s_const = sem("s_const")
        s_alone = sem("s_alone")
        s_w = sem("s_weights")
        s_vc = sem("s_vec_chain")
        for g in (g1, g2):
            g.s_in = sem(g.name + "_in")
            g.s_hist = sem(g.name + "_hist")
            g.s_pre = sem(g.name + "_prefix")
            g.s_scan = sem(g.name + "_scan")
            g.s_oh = sem(g.name + "_onehots")
            g.s_pl = sem(g.name + "_placed")
            g.s_done = sem(g.name + "_placed_all")
            g.s_cmp = sem(g.name + "_cmp")
            g.s_row = sem(g.name + "_rowps")
            g.s_ready = sem(g.name + "_ready")
        s_deg = sem("s_deg")
        s_degq = sem("s_degq")
        ph = []
        for k in range(3):
            names = ["dv", "xn", "tp", "at", "mm", "ev"]
            names += {0: ["var", "sq", "st"], 1: ["st"],
                      2: ["var", "sq", "x2", "free"]}[k]
            s = {n: sem(f"p{k}_{n}") for n in names}
            if k != 1:
                s["x"] = [sem(f"p{k}_xin{u}") for u in range(U)]
            ph.append(s)
        s_ss = [[sem(f"s_st{a}{u}") for u in range(U)] for a in range(2)]
        cv = []
        for k in range(2):
            cv.append(dict(g=[sem(f"c{k}_gath{j}") for j in range(G)],
                           ix=sem(f"c{k}_ix"),
                           s=sem(f"c{k}_sel"),
                           used=sem(f"c{k}_used"),
                           add=sem(f"c{k}_add")))
        s_ix = sem("s_ix")
        s_rec, s_recst = sem("s_rec"), sem("s_recst")
        s_gr = [sem(f"s_gr{h}") for h in range(2)]
        s_pc = sem("s_pc")
        s_fw, s_ai, s_hm, s_hg, s_ym, s_ye = [sem("e_" + n) for n in ("w", "in", "hm", "hg", "ym", "ye")]
        s_ys = [sem(f"e_ys{j}") for j in range(4)]
        a_s, a_z, a_t, a_nm, a_zv, a_v, a_m, a_r, a_c = [sem("a_" + n) for n in
            ("s", "z", "t", "nm", "zv", "v", "m", "r", "c")]
        s_adp = sem("s_adp")
        b_s, b_t, b_st, b_sel, b_sc, b_e, b_x, b_p, b_o, b_a, b_c = [sem("b_" + n) for n in
            ("s", "t", "st", "sel", "sc", "e", "x", "p", "o", "a", "c")]
        s_ex, s_sx, s_gate = sem("s_ex"), sem("s_sx"), sem("s_gate")
        f_in = [sem(f"f_in{u}") for u in range(U)]
        f_c, f_o, f_free = sem("f_c"), sem("f_o"), sem("f_free")
        f_st = [sem(f"f_st{u}") for u in range(U)]

        RT = g2.NT // G
        NCONST, NLOADS = 12, 12
        CH = ROWS // 512

        def alone(eng):
            eng.sem_inc(s_alone, 1)

        block = ctx.enter_context(nc.Block())

        @block.sync
        def _(sp):
            def load_edges(g):
                sp.dma_start(src_i[0:g.EP, 0:g.T], g.src.rearrange("(p t) -> p t", t=g.T)).then_inc(g.s_in, 16)
                sp.dma_start(dst_i[0:g.EP, 0:g.T], g.dst.rearrange("(p t) -> p t", t=g.T)).then_inc(g.s_in, 16)

            load_edges(g1)
            for k, w in enumerate((gW1, gW2)):
                sp.dma_start(wg[k][:, :, :], w.rearrange("(k p) n -> p k n", p=P)).then_inc(s_w, 16)
            sp.dma_start(wgat[:, :, :], W_gat.rearrange("(k p) n -> p k n", p=P)).then_inc(s_w, 16)
            for k, b in enumerate((gb1, gb2)):
                sp.dma_start(bias[k][:, :], b.partition_broadcast(P)).then_inc(s_w, 16)
            for k, b in enumerate((att_src.rearrange("a b -> (a b)"), att_dst.rearrange("a b -> (a b)"),
                                   b_gat, ln_g, ln_b)):
                sp.dma_start(vecs[:, k, :], b.partition_broadcast(P)).then_inc(s_w, 16)
            sp.dma_start(b2s[:, :], b2.rearrange("e n -> (e n)").partition_broadcast(P)).then_inc(s_w, 16)
            with nc.allow_non_contiguous_dma(reason="bias as a column per hidden chunk"):
                sp.dma_start(b1s[:, :], b1.rearrange("e (c p) -> p (e c)", p=P)).then_inc(s_w, 16)

            def load_x(s, i, tail):
                for u in range(U):
                    sp.wait_ge(s["xn"], i * U + u + 1)
                    rows = LAST if tail and u == 0 else P
                    view = x[(NBIN - 1) * P:N, :] if tail and u == 0 else (
                        x[0:P, :] if tail else x[bass.ds((i * U + u) * P, P), :])
                    sp.dma_start(xt[0:rows, u, :], view).then_inc(s["x"][u], 16)

            def store_table(s, table, i):
                sp.wait_ge(s["ev"], 2 + (i + 1) * U)
                sp.dma_start(table[bass.ds(i * U * P, U * P), :].rearrange("(u p) n -> p u n", p=P),
                             acc[:, bass.ds(i * U * D, U * D)].rearrange("p (u n) -> p u n", u=U)).then_inc(s["st"], 16)

            with sp.Fori(0, STEPS - 1) as i:
                load_x(ph[0], i, False)
                store_table(ph[0], G1, i)
            load_x(ph[0], STEPS - 1, True)
            store_table(ph[0], G1, STEPS - 1)
            load_edges(g2)
            with sp.Fori(0, STEPS) as i:
                store_table(ph[1], G2, i)
            s = ph[2]
            sp.sem_inc(s["free"], U)
            with sp.Fori(0, STEPS) as i:
                for u in range(U):
                    sp.wait_ge(s["x2"], U + i * U + u + 1)
                    sp.dma_start(X2[bass.ds((i * U + u) * P, P), :], x2t[:, u, :]).then_inc(s_ss[0][u], 16)
                    sp.wait_ge(s["at"], 2 + i * U + u + 1)
                    alone(sp)
                    sp.dma_start(AT[:, bass.ds((i * U + u) * P, P)].rearrange("(k p) n -> p k n", p=P),
                                 aT[:, u, :, :]).then_inc(s_ss[1][u], 16)
                for u in range(U):
                    sp.wait_ge(s_ss[0][u], (i + 1) * 16)
                    sp.wait_ge(s_ss[1][u], (i + 1) * 16)
                    sp.sem_inc(s["free"], 1)
            sp.wait_ge(s_rec, 1)
            sp.dma_start(TR.rearrange("(t p) r -> p t r", p=P), tg[:, :, :]).then_inc(s_recst, 16)

            for j in range(4):
                sp.dma_start(y_sb[:, j, :], b2[0, :].partition_broadcast(P)).then_inc(s_ys[j], 16)
            with sp.Fori(0, EXPERTS) as e:
                sp.wait_ge(s_ym, e * (CH * 4) + 1)
                sp.dma_start(w1s[:, :, :], W1[bass.ds(e, 1), :, :].rearrange("o (k p) n -> p (o k) n", p=P)).then_inc(s_fw, 16)
                sp.dma_start(w2s[:, :, :], W2[bass.ds(e, 1), :, :].rearrange("o (k p) n -> p (o k) n", p=P)).then_inc(s_fw, 16)
                with sp.Fori(0, CH) as c:
                    sp.wait_ge(s_hm, (e * CH + c + 1) * HC)
                    sp.dma_start(at_in[:, :, :], AT[:, bass.ds(c * 512, 512)]
                                 .rearrange("(k p) n -> p k n", p=P)).then_inc(s_ai, 16)

            sp.sem_inc(f_free, U)
            sp.wait_ge(b_a, 1 + RT)
            for j in range(4):
                sp.wait_ge(s_ys[j], 16 * (1 + EXPERTS * CH))

            def final_in(i, us):
                for u in us:
                    sp.wait_ge(f_o, i * U + u + 1)
                    sp.dma_start(x2_in[:, u, :], X2[bass.ds((i * U + u) * P, P), :]).then_inc(f_in[u], 16)
                    sp.dma_start(y_in[:, u, :, :], Y[bass.ds((i * U + u) * P, P), :]
                                 .rearrange("p (e n) -> p e n", e=EXPERTS)).then_inc(f_in[u], 16)

            def final_out(i, us, rows):
                for u in us:
                    sp.wait_ge(f_o, U + i * U + u + 1)
                    sp.dma_start(out[bass.ds((i * U + u) * P, rows), :], o_sb[0:rows, u, :]).then_inc(f_st[u], 16)

            with sp.Fori(0, STEPS - 1) as i:
                final_in(i, range(U))
                final_out(i, range(U), P)
                for u in range(U):
                    sp.wait_ge(f_st[u], (i + 1) * 16)
                    sp.sem_inc(f_free, 1)
            final_in(STEPS - 1, [0])
            final_out(STEPS - 1, [0], LAST)
            sp.wait_ge(f_st[0], STEPS * 16)

        @block.gpsimd
        def _(pool):
            pool.iota(iota16[:, :], [[1, TMAX]], base=0, channel_multiplier=0,
                      allow_small_or_imprecise_dtypes=True).then_inc(s_const, 1)
            pool.iota(iota32[:, :], [[1, P]], base=0, channel_multiplier=0,
                      allow_small_or_imprecise_dtypes=True).then_inc(s_const, 1)
            pool.iota(iobin[:, :], [[1, 64]], base=0, channel_multiplier=0,
                      allow_small_or_imprecise_dtypes=True).then_inc(s_const, 1)
            pool.memset(ones[:, :], 1.0).then_inc(s_const, 1)
            pool.memset(ones16[:, :], 1.0).then_inc(s_const, 1)
            pool.memset(onesf16[:, :], 1.0).then_inc(s_const, 1)
            pool.memset(zero16[:, :], 0.0).then_inc(s_const, 1)
            pool.memset(Z[:, :, :], 0.0).then_inc(s_const, 1)
            pool.memset(xt[:, :, :], 0.0).then_inc(s_const, 1)
            pool.memset(dinv[:, :], 1.0).then_inc(s_const, 1)
            pool.wait_ge(s_const, 10)
            pool.affine_select(out=ident[:, :], in_=ones[:, :], compare_op=ALU.is_equal, fill=0.0,
                               base=0, pattern=[[-1, P]], channel_multiplier=1).then_inc(s_const, 1)
            pool.affine_select(out=tri[:, :], in_=ones[:, :], compare_op=ALU.is_gt, fill=0.0,
                               base=0, pattern=[[1, P]], channel_multiplier=-1).then_inc(s_const, 1)

            def conv(c, g, table, s):
                pool.wait_ge(s["st"], 16 * STEPS)
                with pool.Fori(0, g.NT // (2 * G)) as i:
                    for h in range(2):
                        j = i * 2 + h
                        pool.wait_ge(c["used"], j * G + 1)
                        pool.tensor_copy(stage[:, h, :], g.idx[:, bass.ds(j * G, G)]).then_inc(c["ix"], 1)
                        pool.wait_ge(c["ix"], j + 1)
                        for k in range(G):
                            pool.wait_ge(c["used"], j * G + k + 1)
                            alone(pool)
                            pool.indirect_dma_start(
                                out=msg[:, k, :], out_offset=None, in_=table[:, :],
                                in_offset=bass.IndirectOffsetOnAxis(ap=stage[:, h, k:k + 1], axis=0),
                            ).then_inc(c["g"][k], 16)

            pool.wait_ge(g1.s_ready, 1)
            pool.wait_ge(g2.s_ready, 1)
            conv(cv[0], g1, G1, ph[0])
            conv(cv[1], g1, G2, ph[1])

            def load_x(s, i, tail):
                for u in range(U):
                    pool.wait_ge(s["x2"], i * U + u + 1)
                    rows = LAST if tail and u == 0 else P
                    view = x[(NBIN - 1) * P:N, :] if tail and u == 0 else (
                        x[0:P, :] if tail else x[bass.ds((i * U + u) * P, P), :])
                    pool.dma_start(xt[0:rows, u, :], view).then_inc(s["x"][u], 16)

            with pool.Fori(0, STEPS - 1) as i:
                load_x(ph[2], i, False)
            load_x(ph[2], STEPS - 1, True)

            pool.wait_ge(s_recst, 16)

            def gather(j, h):
                pool.tensor_copy(stage[:, h, :], g2.idx[:, bass.ds(j * G, G)]).then_inc(s_ix, 1)
                pool.wait_ge(s_ix, j + 1)
                alone(pool)
                for k in range(G):
                    pool.indirect_dma_start(
                        out=ring[:, h, k * REC:(k + 1) * REC], out_offset=None, in_=TR[:, :],
                        in_offset=bass.IndirectOffsetOnAxis(ap=stage[:, h, k:k + 1], axis=0),
                    ).then_inc(s_gr[h], 16)

            def place(j, h):
                pool.wait_ge(s_gr[h], (j - h + 2) * (G * 8))
                pool.tensor_copy(R[:, bass.ds(j * (G * REC), G * REC)], ring[:, h, :]).then_inc(s_pc, 1)
                pool.wait_ge(s_pc, j + 1)

            gather(0, 0)
            with pool.Fori(0, RT // 2 - 1) as i:
                gather(i * 2 + 1, 1)
                place(i * 2, 0)
                gather(i * 2 + 2, 0)
                place(i * 2 + 1, 1)
            gather(RT - 1, 1)
            place(RT - 2, 0)
            place(RT - 1, 1)

        @block.tensor
        def _(pe):
            mm = nc.tensor.matmul
            pe.wait_ge(s_const, NCONST)
            pe.wait_ge(s_w, 16 * NLOADS)

            def sort(g):
                pe.sem_inc(g.s_pl, 4)
                pe.wait_ge(g.s_hist, NBIN)
                mm(PS[7][:, 0:NBIN], ones[0:g.EP, :], H[0:g.EP, 0:NBIN], start=True, stop=True)
                mm(PS[7][:, 64:64 + NBIN], tri[0:g.EP, :], H[0:g.EP, 0:NBIN], start=True, stop=True,
                   skip_group_check=True).then_inc(g.s_pre, 1)
                outs = [(3 * j + c, at, w, j) for j in range(2) for c, (at, w) in enumerate(g.chunks)]

                def edge(start, stop):
                    for b, _, w, _ in outs:
                        last = mm(PS[b][:, 0:w], zero16[:, 0:P], zero16[:, 0:w], start=start, stop=stop)
                    if g.with_degree:
                        last = mm(PS[6][:, 0:NBIN], zero16[:, 0:P], zero16[:, 0:NBIN], start=start, stop=stop)
                    return last

                edge(True, False)
                with pe.Fori(0, g.T // 4) as i:
                    for k in range(4):
                        pe.wait_ge(g.s_oh, i * 4 + k + 1)
                        for b, at, w, j in outs:
                            last = mm(PS[b][:, 0:w], oh_lo[0:g.EP, k, j, :], oh_hi[0:g.EP, k, at:at + w],
                                      start=False, stop=False)
                        if g.with_degree:
                            last = mm(PS[6][:, 0:NBIN], oh_lo[0:g.EP, k, 2, :], oh_bin[0:g.EP, k, 0:NBIN],
                                      start=False, stop=False)
                        last.then_inc(g.s_pl, 1)
                edge(False, True).then_inc(g.s_done, 1)
                pe.wait_ge(g.s_cmp, 1)
                for c, (at, w) in enumerate(g.chunks):
                    last = mm(PS[c][0:1, 0:w], onesf16[0:NBIN, 0:1], oh_hi[0:NBIN, 0, at:at + w],
                              start=True, stop=True)
                last.then_inc(g.s_row, 1)

            def phase(s, w, n):
                pe.sem_inc(s["tp"], U)
                pe.sem_inc(s["mm"], U)
                with pe.Fori(0, STEPS) as i:
                    for pair in range(0, U, 2):
                        for u in (pair, pair + 1):
                            pe.wait_ge(s["xn"], U + i * U + u + 1)
                            pe.wait_ge(s["at"], i * U + u + 1)
                            for c in range(KC):
                                last = nc.tensor.transpose(PS[u % 2][:, c * P:(c + 1) * P],
                                                           xn[:, u, c * P:(c + 1) * P], ident[:, :])
                            last.then_inc(s["tp"], 1)
                        for u in (pair, pair + 1):
                            pe.wait_ge(s["at"], 2 + i * U + u + 1)
                            pe.wait_ge(s["ev"], i * U + u + 1)
                            for c in range(KC):
                                last = mm(PS[2 + u % 2][:, 0:n], aT[:, u, c, :], w[:, c, :],
                                          start=c == 0, stop=c == KC - 1)
                            last.then_inc(s["mm"], 1)

            def conv(c, g):
                pe.sem_inc(c["used"], G)
                with pe.Fori(0, g.NT // G) as i:
                    for k in range(G):
                        pe.wait_ge(c["s"], i * G + k + 1)
                        pe.wait_ge(c["g"][k], (i + 1) * 16)
                        pe.wait_ge(c["add"], i * G + k + 1)
                        mm(PS[4 + k % 4][:, 0:D], S[:, k, :], msg[:, k, :], start=True, stop=True).then_inc(c["used"], 1)

            sort(g1)
            phase(ph[0], wg[0], D)
            sort(g2)
            conv(cv[0], g1)
            phase(ph[1], wg[1], D)
            conv(cv[1], g1)
            phase(ph[2], wgat, HE)

            pe.sem_inc(s_ym, 1)
            pe.sem_inc(s_hm, HC)
            with pe.Fori(0, EXPERTS) as e:
                pe.wait_ge(s_fw, (e + 1) * 32)
                alone(pe)
                with pe.Fori(0, CH) as c:
                    n = e * CH + c
                    pe.wait_ge(s_ai, (n + 1) * 16)
                    for q in range(HC):
                        pe.wait_ge(s_hg, n * HC + q + 1)
                        for k in range(KC):
                            last = mm(PS[q % 2][:, :], w1s[:, k, q * P:(q + 1) * P],
                                      at_in[:, k, :], start=k == 0, stop=k == KC - 1)
                        last.then_inc(s_hm, 1)
                    pe.wait_ge(s_hg, 2 + (n + 1) * HC)
                    for j in range(4):
                        pe.wait_ge(s_ye, n * 4 + j + 1)
                        for q in range(HC):
                            last = mm(PS[2 + j % 2][:, 0:D], hid[:, q, j * P:(j + 1) * P], w2s[:, q, :],
                                      start=q == 0, stop=q == HC - 1)
                        last.then_inc(s_ym, 1)

            pe.wait_ge(s_ye, 2 + EXPERTS * CH * 4)
            pe.sem_inc(a_m, G)
            with pe.Fori(0, RT) as i:
                for half in range(2):
                    four = range(4 * half, 4 * half + 4)
                    for k in four:
                        pe.wait_ge(a_s, i * G + k + 1)
                        pe.wait_ge(a_nm, i * 2 + half + 1)
                        last = nc.tensor.transpose(PS[4][:, (k % 4) * P:(k % 4 + 1) * P], S[:, k, :], ident[:, :])
                    last.then_inc(a_t, 1)
                    pe.wait_ge(a_z, i + 1)
                    for k in four:
                        pe.wait_ge(a_v, i * G + k + 1)
                        for h in range(HEADS):
                            last = mm(PS[(3, 5)[k % 2]][0:12, h * P:(h + 1) * P], Z[:, k, h * 12:(h + 1) * 12],
                                      ident16[:, :], start=True, stop=True, skip_group_check=True)
                        last.then_inc(a_zv, 1)
                        pe.wait_ge(a_nm, 1 + i * 2 + half + 1)
                        pe.wait_ge(a_v, 2 + i * G + k + 1)
                        pe.wait_ge(a_r, i * G + k + 1)
                        mm(PS[6 + k % 2][:, :], ones16[0:12, :], V[:, k % 2, :], start=True, stop=False)
                        mm(PS[6 + k % 2][:, :], ident16[:, :], ST[:, k, :].unsqueeze(1).to_broadcast([P, HEADS, P]),
                           start=False, stop=True).then_inc(a_m, 1)

            row_regs = [pe.alloc_register(f"pe_bin{k}") for k in range(G)]
            pe.wait_ge(s_adp, 1)
            with pe.Fori(0, RT) as i:
                for half in range(2):
                    for k in range(4 * half, 4 * half + 4):
                        pe.wait_ge(b_s, i * G + k + 1)
                        pe.wait_ge(b_st, i * 2 + half + 1)
                        last = nc.tensor.transpose(PS[3 + half][:, (k % 4) * P:(k % 4 + 1) * P], S[:, k, :], ident[:, :])
                    last.then_inc(b_t, 1)
                pe.load(row_regs, g2.row[0:1, bass.ds(i * G, G)])
                offs = [pe.snap(r, min_val=0, max_val=NBIN * SEL) for r in row_regs]
                pe.wait_ge(b_sc, i + 1)
                for k in range(G):
                    pe.wait_ge(b_st, 2 + i * 2 + k // 4 + 1)
                    last = mm(PS[5][:, k * SEL:(k + 1) * SEL], ST[:, k, :], adp[:, bass.ds(offs[k], SEL)],
                              start=True, stop=True, skip_group_check=True)
                last.then_inc(b_sel, 1)
                pe.wait_ge(b_p, i + 1)
                pe.wait_ge(b_a, i + 1)
                for k in range(G):
                    last = mm(PS[6][:, k * REC:(k + 1) * REC], S[:, k, :], pay[:, k, :],
                              start=True, stop=True, skip_group_check=True)
                last.then_inc(b_o, 1)

        @block.scalar
        def _(act):
            act.wait_ge(s_const, NCONST)
            copy = lambda o, i: nc.scalar.activation(o, i, ACT.Copy)
            act.wait_ge(s_deg, 1)
            nc.scalar.activation(one[1][:, 0:NBIN], one[0][:, 0:NBIN], ACT.Sqrt).then_inc(s_degq, 1)

            def phase(k, s, n):
                act.sem_inc(s["at"], 2)
                act.sem_inc(s["ev"], 2)
                with act.Fori(0, STEPS) as i:
                    if k != 1:
                        act.wait_ge(s["var"], i + 1)
                        nc.scalar.activation(mv[:, :, 3], mv[:, :, 2], ACT.Sqrt).then_inc(s["sq"], 1)
                    for pair in range(0, U, 2):
                        for u in (pair, pair + 1):
                            act.wait_ge(s["tp"], U + i * U + u + 1)
                            act.wait_ge(s["mm"], i * U + u + 1)
                            if k == 2:
                                act.wait_ge(s["free"], i * U + u + 1)
                            copy(aT[:, u, :, :], PS[u % 2][:, 0:D].rearrange("p (k n) -> p k n", k=KC)).then_inc(s["at"], 1)
                        for u in (pair, pair + 1):
                            act.wait_ge(s["mm"], U + i * U + u + 1)
                            alone(act)
                            if k == 2:
                                copy(tg[:, bass.ds(i * U + u, 1), 0:HE],
                                     PS[2 + u % 2][:, 0:HE].unsqueeze(1)).then_inc(s["ev"], 1)
                            else:
                                nc.scalar.activation(acc[:, bass.ds((i * U + u) * D, D)], PS[2 + u % 2][:, 0:D], ACT.Copy,
                                                     scale=dinv[:, bass.ds(i * U + u, 1)]).then_inc(s["ev"], 1)

            act.wait_ge(g1.s_ready, 1)
            phase(0, ph[0], D)
            phase(1, ph[1], D)
            phase(2, ph[2], HE)

            act.sem_inc(s_hg, 2)

            def gelu(e, c):
                for q in range(HC):
                    act.wait_ge(s_hm, HC + (e * CH + c) * HC + q + 1)
                    alone(act)
                    nc.scalar.activation(hid[:, q, :], PS[q % 2][:, :], ACT.Gelu,
                                         bias=b1s[:, bass.ds(e * HC + q, 1)]).then_inc(s_hg, 1)

            def store_y(e, c):
                for j in range(4):
                    act.wait_ge(s_ye, 2 + (e * CH + c) * 4 + j + 1)
                    act.dma_start(Y[bass.ds((c * 4 + j) * P, P), bass.ds(e * D, D)],
                                  y_sb[:, j, :]).then_inc(s_ys[j], 16)

            with act.Fori(0, EXPERTS) as e:
                gelu(e, 0)
                with act.Fori(1, CH) as c:
                    gelu(e, c)
                    store_y(e, c - 1)
                store_y(e, CH - 1)

            act.sem_inc(a_nm, 1)
            act.sem_inc(a_v, 2)
            with act.Fori(0, RT) as i:
                for half in range(2):
                    act.wait_ge(a_t, i * 2 + half + 1)
                    act.wait_ge(a_m, i * G + 4 * half + 4)
                    nc.scalar.activation(ST[:, 4 * half:4 * half + 4, :], PS[4][:, :].rearrange("p (k n) -> p k n", k=4),
                                         ACT.Copy, scale=BIG, bias=-BIG).then_inc(a_nm, 1)
                    for k in range(4 * half, 4 * half + 4):
                        act.wait_ge(a_zv, i * G + k + 1)
                        act.wait_ge(a_m, G + i * G + k - 1)
                        copy(V[:, k % 2, :], PS[(3, 5)[k % 2]][0:12, :]).then_inc(a_v, 1)

            act.wait_ge(s_ex, 1)
            acc2v = acc2[:, :].rearrange("p (t s) -> p t s", s=SEL)
            nc.scalar.activation(acc2v[:, :, HE:REC], big[:, 1, :, 0:HEADS], ACT.Exp).then_inc(s_sx, 1)
            act.sem_inc(b_st, 2)
            act.sem_inc(b_sc, 1)
            with act.Fori(0, RT) as i:
                for half in range(2):
                    act.wait_ge(b_t, i * 2 + half + 1)
                    copy(ST[:, 4 * half:4 * half + 4, :], PS[3 + half][:, :].rearrange("p (k n) -> p k n", k=4)).then_inc(b_st, 1)
                act.wait_ge(b_sel, i + 1)
                copy(ssel[:, :, :], PS[5][:, 0:G * SEL].rearrange("p (k n) -> p k n", k=G)).then_inc(b_sc, 1)
                act.wait_ge(b_e, i + 1)
                nc.scalar.activation(pay[:, :, HE:REC], ee[:, 2, :, :], ACT.Exp).then_inc(b_x, 1)
            act.wait_ge(s_ex, 2)
            nc.scalar.activation(one[1][:, :], one[0][:, :], ACT.Sqrt).then_inc(s_sx, 1)
            act.wait_ge(s_ex, 3)
            nc.scalar.activation(sc[1][:, :, :], sc[2][:, :, :], ACT.Exp).then_inc(s_sx, 1)

        @block.vector
        def _(vec):
            v = nc.vector
            ch = Counter(vec, s_vc)
            vec.wait_ge(s_const, NCONST)
            vec.wait_ge(s_w, 16 * NLOADS)
            ch.step(v.tensor_copy(ident16[:, :], ident[:, :]))

            def sort(g):
                p, t = g.EP, g.T
                vec.wait_ge(g.s_in, 32)
                si, di, a_f, b_f = src_i[0:p, 0:t], dst_i[0:p, 0:t], valA[0:p, 0:t], valB[0:p, 0:t]
                lo_f = tmp(0)[0:p, 0:t]
                pos_f, pos_i = pos[0:p, 0:t], tmp(4, I32)[0:p, 0:t]
                run_f, run_i = run[0:p, 0:t], tmp(5, I32)[0:p, 0:t]
                plo_f, plo_i = plo[0:p, 0:t], tmp(6, I32)[0:p, 0:t]
                phi_f = phi[0:p, 0:t]
                b16, mk = bin16[0:p, 0:t], mask[0:p, 0:t]
                ch.step(v.tensor_scalar(si, si, float(N - 1), None, ALU.min))
                ch.step(v.tensor_scalar(plo_i, si, 3, None, ALU.arith_shift_right))
                ch.step(v.tensor_copy(a_f, plo_i))
                ch.step(v.tensor_scalar(plo_i, si, 7, None, ALU.bitwise_and))
                ch.step(v.tensor_scalar(run_i, di, P - 1, None, ALU.bitwise_and))
                ch.step(v.tensor_copy(lo_f, run_i))
                ch.step(v.tensor_scalar(b_f, plo_i, 256.0, 1.0, ALU.mult, ALU.add))
                ch.step(v.tensor_tensor(b_f, b_f, lo_f, ALU.add))
                ch.step(v.tensor_scalar(plo_i, di, 7, None, ALU.arith_shift_right))
                ch.step(v.tensor_scalar(phi_f, di, float(N), 64.0, ALU.is_ge, ALU.mult))
                ch.step(v.tensor_tensor(b16, phi_f, plo_i, ALU.add))
                with v.Fori(0, NBIN) as b:
                    v.tensor_scalar(mk, b16, iobin[0:p, bass.ds(b, 1)], None, ALU.is_equal, ALU.add,
                                    accum_out=H[0:p, bass.ds(b, 1)]).then_inc(g.s_hist, 1)
                    vec.wait_ge(g.s_hist, b + 1)
                vec.wait_ge(g.s_pre, 1)
                nb = slice(0, NBIN)
                ch.step(v.tensor_scalar(bni[:, nb], PS[7][:, nb], float(P - 1), None, ALU.add))
                ch.step(v.tensor_scalar(bni[:, nb], bni[:, nb], 7, None, ALU.arith_shift_right))
                ch.step(v.tensor_copy(bn[:, 0, nb], bni[:, nb]))
                ch.step(v.tensor_tensor_scan(bn[:, 1, nb], bn[:, 0, nb], bn[:, 0, nb], 0.0, ALU.add, ALU.max))
                ch.step(v.tensor_tensor(bn[:, 2, nb], bn[:, 1, nb], bn[:, 0, nb], ALU.subtract))
                ch.step(v.scalar_tensor_tensor(bn[:, 3, nb], bn[:, 2, nb], float(P), PS[7][:, 64:64 + NBIN],
                                               ALU.mult, ALU.add))
                ch.step(v.memset(pos_f, float(1 << 20)))
                with v.Fori(0, NBIN) as b:
                    lc = Counter(vec, g.s_scan, base=b * 3)
                    lc.step(v.tensor_scalar(mk, b16, iobin[0:p, bass.ds(b, 1)], None, ALU.is_equal))
                    lc.step(v.tensor_tensor_scan(run_f, mk, mk, bn[0:p, 3, bass.ds(b, 1)], ALU.add, ALU.max))
                    alone(vec)
                    lc.step(v.copy_predicated(pos_f, mk, run_f))
                ch.step(v.tensor_scalar(run_i, pos_f, -1.0, None, ALU.add))
                ch.step(v.tensor_scalar(pos_i, run_i, 7, None, ALU.arith_shift_right))
                ch.step(v.tensor_copy(phi_f, pos_i))
                ch.step(v.tensor_scalar(pos_i, run_i, P - 1, None, ALU.bitwise_and))
                ch.step(v.tensor_copy(plo_f, pos_i))
                with v.Fori(0, t // 4) as i:
                    for k in range(4):
                        at = lambda a: a[:, bass.ds(i * 4 + k, 1)]
                        vec.wait_ge(g.s_pl, i * 4 + k + 1)
                        v.tensor_scalar(oh_hi[0:p, k, 0:g.NT], iota16[0:p, 0:g.NT], at(phi_f), None, ALU.is_equal)
                        v.tensor_scalar(oh_lo[0:p, k, 0, :], iota16[0:p, 0:P], at(plo_f), at(a_f), ALU.is_equal, ALU.mult)
                        last = v.tensor_scalar(oh_lo[0:p, k, 1, :], iota16[0:p, 0:P], at(plo_f), at(b_f), ALU.is_equal, ALU.mult)
                        if g.with_degree:
                            v.tensor_scalar(oh_lo[0:p, k, 2, :], iota16[0:p, 0:P], at(lo_f), None, ALU.is_equal)
                            last = v.tensor_scalar(oh_bin[0:p, k, 0:NBIN], iota16[0:p, 0:NBIN], at(b16), None, ALU.is_equal)
                        last.then_inc(g.s_oh, 1)
                vec.wait_ge(g.s_done, 1)
                for c, (at, w) in enumerate(g.chunks):
                    bi, hi = tmp(0, I32)[:, at:at + w], tmp(1, I32)[:, at:at + w]
                    ch.step(v.tensor_copy(bi, PS[3 + c][:, 0:w]))
                    ch.step(v.tensor_scalar(hi, bi, 8, None, ALU.arith_shift_right))
                    ch.step(v.scalar_tensor_tensor(g.idx[:, at:at + w], PS[c][:, 0:w], 8.0, hi, ALU.mult, ALU.add))
                    ch.step(v.tensor_scalar(hi, bi, 255, None, ALU.bitwise_and))
                    ch.step(v.tensor_scalar(g.dlo[:, at:at + w], hi, -1.0, None, ALU.add))
                ch.step(v.tensor_tensor(bn[:, 4, nb], bn[:, 1, nb], ident[:, nb], ALU.mult))
                ch.step(v.reduce_sum(bn[:, 5, 0:1], bn[:, 4, nb], axis=AX.X))
                v.tensor_scalar(oh_hi[0:NBIN, 0, 0:g.NT], iota16[0:NBIN, 0:g.NT], bn[0:NBIN, 5, 0:1], None,
                                ALU.is_ge).then_inc(g.s_cmp, 1)
                vec.wait_ge(g.s_row, 1)
                for c, (at, w) in enumerate(g.chunks):
                    last = v.tensor_scalar(g.row[0:1, at:at + w], PS[c][0:1, 0:w], float(g.row_stride), None, ALU.mult)
                ch.step(last)
                if g.with_degree:
                    v.tensor_scalar(one[0][:, nb], PS[6][:, nb], 1.0, None, ALU.add).then_inc(s_deg, 1)
                    vec.wait_ge(s_degq, 1)
                    ch.step(v.reciprocal(dinv[:, nb], one[1][:, nb]))
                vec.sem_inc(g.s_ready, 1)

            def phase(k, s, first):
                vec.sem_inc(s["xn"], U)
                if k == 2:
                    vec.sem_inc(s["x2"], U)
                with v.Fori(0, STEPS) as i:
                    per = 1 if k == 1 else 4
                    lc = Counter(vec, s["dv"], base=i * {0: 10, 1: 4, 2: 14}[k])
                    tile = lambda u: acc[:, bass.ds((i * U + u) * D, D)]
                    dcol = lambda u: dinv[:, bass.ds(i * U + u, 1)]
                    if k == 1:
                        for u in range(U):
                            lc.inc(v.scalar_tensor_tensor(x2t[:, u, :], tile(u), dcol(u), bias[0][:, :], ALU.mult, ALU.add))
                        lc.wait()
                        for u in range(U):
                            vec.wait_ge(s["tp"], i * U + u + 1)
                            v.tensor_scalar(xn[:, u, :], x2t[:, u, :], 0.0, None, ALU.max).then_inc(s["xn"], 1)
                        vec.wait_ge(s["xn"], U + (i + 1) * U)
                        continue_ = True
                    else:
                        srct = xt
                        if k == 2:
                            for u in range(U):
                                vec.wait_ge(s["x"][u], (i + 1) * 16)
                                vec.wait_ge(s["free"], i * U + u + 1)
                                lc.inc(v.scalar_tensor_tensor(x2t[:, u, :], tile(u), dcol(u), xt[:, u, :], ALU.mult, ALU.add))
                            lc.wait()
                            for u in range(U):
                                v.tensor_tensor(x2t[:, u, :], x2t[:, u, :], bias[1][:, :], ALU.add).then_inc(s["x2"], 1)
                            vec.wait_ge(s["x2"], U + (i + 1) * U)
                            srct = x2t
                        for u in range(U):
                            if k == 0:
                                vec.wait_ge(s["x"][u], (i + 1) * 16)
                            lc.inc(v.bn_stats(st6[:, u, :], srct[:, u, :]))
                        lc.wait()
                        alone(vec)
                        for u in range(U):
                            lc.inc(v.bn_aggr(mv[:, u, 0:2], st6[:, u, :]))
                        lc.wait()
                        v.tensor_scalar(mv[:, :, 2], mv[:, :, 1], LN_EPS, None, ALU.add).then_inc(s["var"], 1)
                        vec.wait_ge(s["sq"], i + 1)
                        lc.step(v.reciprocal(mv[:, :, 2], mv[:, :, 3]))
                        for u in range(U):
                            vec.wait_ge(s["tp"], i * U + u + 1)
                            v.tensor_scalar(xn[:, u, :], srct[:, u, :], mv[:, u, 0:1], mv[:, u, 2:3],
                                            ALU.subtract, ALU.mult).then_inc(s["xn"], 1)
                        lc.step(v.tensor_copy(one[0][:, 0:1], mv[:, 0, 0:1]))
                    assert lc.n == {0: 10, 1: 4, 2: 14}[k]

            def one_hot(g, k, i):
                return v.tensor_scalar(S[:, k, :], iota32[:, :], g.dlo[:, bass.ds(i * G + k, 1)], None, ALU.is_equal)

            row_regs = [vec.alloc_register(f"dve_bin{k}") for k in range(G)]

            def bins(g, i, top):
                vec.load(row_regs, g.row[0:1, bass.ds(i * G, G)])
                return [vec.snap(r, min_val=0, max_val=top) for r in row_regs]

            def conv(c, g):
                vec.sem_inc(c["add"], 4)
                with v.Fori(0, g.NT // G) as i:
                    offs = bins(g, i, NBIN * D)
                    for k in range(G):
                        one_hot(g, k, i).then_inc(c["s"], 1)
                    for k in range(G):
                        vec.wait_ge(c["used"], G + i * G + k + 1)
                        vec.wait_ge(c["add"], 4 + i * G + k)
                        a = acc[:, bass.ds(offs[k], D)]
                        v.tensor_tensor(a, a, PS[4 + k % 4][:, 0:D], ALU.add).then_inc(c["add"], 1)
                vec.wait_ge(c["add"], 4 + g.NT)

            sort(g1)
            phase(0, ph[0], True)
            sort(g2)
            vec.wait_ge(ph[0]["st"], 16 * STEPS)
            conv(cv[0], g1)
            phase(1, ph[1], False)
            vec.wait_ge(ph[1]["st"], 16 * STEPS)
            conv(cv[1], g1)
            phase(2, ph[2], False)

            bc = lambda k: vecs[:, k, :].unsqueeze(1).to_broadcast([P, NBP, HE])
            he = lambda a: a.rearrange("p t (h e) -> p t h e", h=HEADS)
            hb = lambda a: a.unsqueeze(3).to_broadcast([P, NBP, HEADS, EXPERTS])
            w0, w1 = big[:, 0, :, :], big[:, 1, :, :]
            h4 = slice(0, HEADS)
            vec.wait_ge(ph[2]["ev"], 2 + NBP)
            ch.step(v.tensor_tensor(w0, tg[:, :, 0:HE], bc(0), ALU.mult))
            ch.step(v.tensor_tensor(w1, tg[:, :, 0:HE], bc(1), ALU.mult))
            ch.step(v.reduce_sum(adst[:, :, :], he(w1), axis=AX.X))
            v.reduce_sum(tg[:, :, HE:REC], he(w0), axis=AX.X).then_inc(s_rec, 1)
            vec.wait_ge(s_rec, 1)
            mxv = mx[:, :].rearrange("p (t s) -> p t s", s=SEL)
            ch.step(v.tensor_copy(mxv[:, :, 0:HEADS], tg[:, :, HE:REC]))

            vec.sem_inc(s_ye, 2)
            with v.Fori(0, EXPERTS) as e:
                with v.Fori(0, CH) as c:
                    for j in range(4):
                        n = e * CH + c
                        vec.wait_ge(s_ym, 1 + n * 4 + j + 1)
                        vec.wait_ge(s_ys[j], (n + 1) * 16)
                        v.tensor_tensor(y_sb[:, j, :], PS[2 + j % 2][:, 0:D], b2s[:, bass.ds(e * D, D)],
                                        ALU.add).then_inc(s_ye, 1)

            vec.sem_inc(a_r, 2)
            with v.Fori(0, RT) as i:
                offs = bins(g2, i, NBIN * SEL)
                for k in range(G):
                    one_hot(g2, k, i).then_inc(a_s, 1)
                vec.wait_ge(s_pc, i + 1)
                rec = R[:, bass.ds(i * (G * REC), G * REC)].rearrange("p (k r) -> p k r", k=G)
                a_src = rec[:, :, HE:REC]
                part = [Z[:, :, 4 * p:4 * p + 40:13] for p in range(3)]
                lc = Counter(vec, a_c, base=i * (4 + G))
                lc.step(v.tensor_copy(part[0], a_src))
                lc.step(v.tensor_tensor(asr[:, 0, :, :], a_src, part[0], ALU.subtract))
                lc.step(v.tensor_copy(part[1], asr[:, 0, :, :]))
                lc.step(v.tensor_tensor(asr[:, 1, :, :], asr[:, 0, :, :], part[1], ALU.subtract))
                v.tensor_copy(part[2], asr[:, 1, :, :]).then_inc(a_z, 1)
                for k in range(G):
                    vec.wait_ge(a_m, G + i * G + k + 1)
                    v.tensor_reduce(red[:, k, :], PS[6 + k % 2][:, :].rearrange("p (h n) -> p h n", h=HEADS),
                                    AX.X, ALU.max).then_inc(a_r, 1)
                    vec.wait_ge(a_r, 2 + i * G + k + 1)
                    m = mx[:, bass.ds(offs[k], HEADS)]
                    lc.step(v.tensor_tensor(m, m, red[:, k, :], ALU.max))

            ch.step(v.tensor_copy(v8[:, :, h4], adst[:, :, :]))
            ch.step(v.tensor_tensor(r8[:, :, h4], mxv[:, :, h4], adst[:, :, :], ALU.add))
            ch.step(v.scalar_tensor_tensor(v8[:, :, 4:8], r8[:, :, h4], 0.2, r8[:, :, h4], ALU.mult, ALU.max))
            adpv = adp[:, :].rearrange("p (t s) -> p t s", s=SEL)
            ch.step(v.tensor_copy(adpv[:, :, 0:8], v8[:, :, :]))
            ch.step(v.tensor_tensor(r8[:, :, :], v8[:, :, :], adpv[:, :, 0:8], ALU.subtract))
            ch.step(v.tensor_copy(adpv[:, :, 8:16], r8[:, :, :]))
            ch.step(v.tensor_tensor(r8[:, :, :], r8[:, :, :], adpv[:, :, 8:16], ALU.subtract))
            v.tensor_copy(adpv[:, :, 16:24], r8[:, :, :]).then_inc(s_adp, 1)
            ch.step(v.tensor_tensor(w0[:, :, h4], tg[:, :, HE:REC], adst[:, :, :], ALU.add))
            ch.step(v.scalar_tensor_tensor(w1[:, :, h4], w0[:, :, h4], 0.2, w0[:, :, h4], ALU.mult, ALU.max))
            v.tensor_tensor(w1[:, :, h4], w1[:, :, h4], v8[:, :, 4:8], ALU.subtract).then_inc(s_ex, 1)
            vec.wait_ge(s_sx, 1)
            acc2v = acc2[:, :].rearrange("p (t s) -> p t s", s=SEL)
            ch.step(v.tensor_tensor(he(acc2v[:, :, 0:HE]), he(tg[:, :, 0:HE]), hb(acc2v[:, :, HE:REC]), ALU.mult))

            vec.sem_inc(b_a, 1)
            with v.Fori(0, RT) as i:
                offs = bins(g2, i, NBIN * SEL)
                for k in range(G):
                    one_hot(g2, k, i).then_inc(b_s, 1)
                lc = Counter(vec, b_c, base=i * (4 + G - 1))
                vec.wait_ge(b_sc, 1 + i + 1)
                lc.step(v.tensor_tensor(q8[:, :, :], ssel[:, :, 0:8], ssel[:, :, 8:16], ALU.add))
                lc.step(v.tensor_tensor(q8[:, :, :], q8[:, :, :], ssel[:, :, 16:24], ALU.add))
                rec = R[:, bass.ds(i * (G * REC), G * REC)].rearrange("p (k r) -> p k r", k=G)
                lc.step(v.tensor_tensor(ee[:, 0, :, :], rec[:, :, HE:REC], q8[:, :, h4], ALU.add))
                lc.step(v.scalar_tensor_tensor(ee[:, 1, :, :], ee[:, 0, :, :], 0.2, ee[:, 0, :, :], ALU.mult, ALU.max))
                v.tensor_tensor(ee[:, 2, :, :], ee[:, 1, :, :], q8[:, :, 4:8], ALU.subtract).then_inc(b_e, 1)
                vec.wait_ge(b_x, i + 1)
                v.tensor_tensor(pay[:, :, 0:HE].rearrange("p k (h e) -> p k h e", h=HEADS),
                                rec[:, :, 0:HE].rearrange("p k (h e) -> p k h e", h=HEADS),
                                pay[:, :, HE:REC].unsqueeze(3).to_broadcast([P, G, HEADS, EXPERTS]),
                                ALU.mult).then_inc(b_p, 1)
                vec.wait_ge(b_o, i + 1)
                for k in range(G):
                    a = acc2[:, bass.ds(offs[k], REC)]
                    ins = v.tensor_tensor(a, a, PS[6][:, k * REC:(k + 1) * REC], ALU.add)
                    if k < G - 1:
                        lc.step(ins)
                    else:
                        ins.then_inc(b_a, 1)
                        vec.wait_ge(b_a, 1 + i + 1)

            c16 = lambda a: a.unsqueeze(2).to_broadcast([P, NBP, HE])
            c4 = lambda a: a.unsqueeze(2).to_broadcast([P, NBP, EXPERTS])
            o0, o1 = one[0][:, :], one[1][:, :]
            ch.step(v.tensor_scalar(r8[:, :, h4], acc2v[:, :, HE:REC], 1e-16, None, ALU.add))
            ch.step(v.reciprocal(r8[:, :, 4:8], r8[:, :, h4]))
            ch.step(v.tensor_tensor(he(w0), he(acc2v[:, :, 0:HE]), hb(r8[:, :, 4:8]), ALU.mult))
            ch.step(v.tensor_tensor(w0, w0, bc(2), ALU.add))
            ch.step(v.reduce_sum(o0, w0, axis=AX.X))
            ch.step(v.tensor_scalar(o0, o0, 1.0 / HE, None, ALU.mult))
            ch.step(v.tensor_tensor(w0, w0, c16(o0), ALU.subtract))
            ch.step(v.tensor_tensor(w1, w0, w0, ALU.mult))
            ch.step(v.reduce_sum(o0, w1, axis=AX.X))
            v.tensor_scalar(o0, o0, 1.0 / HE, LN_EPS, ALU.mult, ALU.add).then_inc(s_ex, 1)
            vec.wait_ge(s_sx, 2)
            ch.step(v.reciprocal(o0, o1))
            ch.step(v.tensor_tensor(w0, w0, c16(o0), ALU.mult))
            ch.step(v.tensor_tensor(w0, w0, bc(3), ALU.mult))
            ch.step(v.tensor_tensor(w0, w0, bc(4), ALU.add))
            ch.step(v.reduce_sum(sc[0][:, :, :], w0.rearrange("p t (h e) -> p t e h", h=HEADS), axis=AX.X))
            ch.step(v.tensor_scalar(sc[0][:, :, :], sc[0][:, :, :], 1.0 / HEADS, None, ALU.mult))
            ch.step(v.tensor_reduce(o0, sc[0][:, :, :], AX.X, ALU.max))
            v.tensor_tensor(sc[2][:, :, :], sc[0][:, :, :], c4(o0), ALU.subtract).then_inc(s_ex, 1)
            rank, cmpv = w0[:, :, 0:EXPERTS], w1
            n = 0
            for e in range(EXPERTS):
                for j in range(EXPERTS):
                    if j != e:
                        ch.inc(v.tensor_tensor(cmpv[:, :, n:n + 1], sc[0][:, :, j:j + 1], sc[0][:, :, e:e + 1],
                                               ALU.is_ge if j < e else ALU.is_gt))
                        n += 1
            ch.wait()
            ch.step(v.reduce_sum(rank, w1[:, :, 0:12].rearrange("p t (e j) -> p t e j", e=EXPERTS), axis=AX.X))
            vec.wait_ge(s_sx, 3)
            ch.step(v.scalar_tensor_tensor(sc[2][:, :, :], rank, 2.0, sc[1][:, :, :], ALU.is_lt, ALU.mult))
            ch.step(v.reduce_sum(o0, sc[2][:, :, :], axis=AX.X))
            ch.step(v.reciprocal(o1, o0))
            ch.step(v.tensor_tensor(gate[:, :].rearrange("p (t e) -> p t e", e=EXPERTS), sc[2][:, :, :], c4(o1), ALU.mult))

            vec.sem_inc(f_o, U)

            def final(i, us, base):
                lc = Counter(vec, f_c, base=base)
                for u in us:
                    vec.wait_ge(f_in[u], (i + 1) * 32)
                    vec.wait_ge(f_free, i * U + u + 1)
                for e in range(EXPERTS):
                    for u in us:
                        other = x2_in[:, u, :] if e == 0 else o_sb[:, u, :]
                        ins = v.scalar_tensor_tensor(o_sb[:, u, :], y_in[:, u, e, :],
                                                     gate[:, bass.ds((i * U + u) * EXPERTS + e, 1)], other,
                                                     ALU.mult, ALU.add)
                        if e < EXPERTS - 1:
                            lc.inc(ins)
                        else:
                            ins.then_inc(f_o, 1)
                    lc.wait()

            with v.Fori(0, STEPS - 1) as i:
                final(i, range(U), i * (EXPERTS - 1) * U)
            final(STEPS - 1, [0], (STEPS - 1) * (EXPERTS - 1) * U)


_INS = ['x', 'src', 'dst', 'L0_gnn_W1', 'L0_gnn_b1', 'L0_gnn_W2', 'L0_gnn_b2', 'L0_ffn_W_gat',
        'L0_ffn_att_src', 'L0_ffn_att_dst', 'L0_ffn_b_gat', 'L0_ffn_ln_gamma', 'L0_ffn_ln_beta',
        'L0_ffn_W1', 'L0_ffn_b1', 'L0_ffn_W2', 'L0_ffn_b2', 'L0_ffn_edge_index']


def kernel(**inputs):
    import numpy as _np
    import concourse.bacc as _bacc
    from concourse import mybir as _mybir
    from concourse.bass_utils import run_bass_kernel_spmd as _run

    nc = _bacc.Bacc("TRN2", target_bir_lowering=False, num_devices=1)
    arrays, args = {}, []
    for name in _INS:
        a = _np.ascontiguousarray(inputs[name])
        arrays[f"in_{name}_dram"] = a
        args.append(nc.dram_tensor(f"in_{name}_dram", a.shape, _mybir.dt.from_np(a.dtype), kind="ExternalInput").ap())
    args.append(nc.dram_tensor("out_0_dram", (N, D), _mybir.dt.float32, kind="ExternalOutput").ap())
    build(nc, *args)
    r = _run(nc, [arrays], core_ids=[0])
    return r.results[0]["out_0_dram"]
```

```python
import numpy as np
import concourse.bass as bass
from concourse import mybir
from contextlib import ExitStack

F32, I32, F16, BF16 = mybir.dt.float32, mybir.dt.int32, mybir.dt.float16, mybir.dt.bfloat16
U16, I16 = mybir.dt.uint16, mybir.dt.int16
ALU = mybir.AluOpType
ACT = mybir.ActivationFunctionType
AX = mybir.AxisListType

P = 128
N = 6250
D = 256
NBIN = -(-N // P)
LAST = N - (NBIN - 1) * P
U = 4
NBP = -(-NBIN // U) * U
STEPS = NBP // U
ROWS = NBP * P
EXPERTS, HEADS, HID = 4, 4, 512
HE = HEADS * EXPERTS
REC = HE + HEADS
SEL = 24
G = 8
LN_EPS = 1e-5
ZR = 3 * HEADS * G + 3 * G + 2
PEN = float(2.0 ** 110)
KC = D // P
HC = HID // P


def tiles_bound(edges):
    most = (edges + NBIN * (P - 1)) // P
    return -(-most // (2 * G)) * 2 * G


class Counter:

    def __init__(self, eng, sem, base=0):
        self.eng, self.sem, self.base, self.n = eng, sem, base, 0

    def inc(self, ins):
        ins.then_inc(self.sem, 1)
        self.n += 1

    def wait(self):
        self.eng.wait_ge(self.sem, self.base + self.n)

    def step(self, ins):
        self.inc(ins)
        self.wait()


class Graph:
    def __init__(self, name, edges, src, dst, parts, with_degree, row_stride):
        self.name, self.src, self.dst = name, src, dst
        self.EP, self.T = parts, edges // parts
        self.NT = tiles_bound(edges)
        self.with_degree, self.row_stride = with_degree, row_stride
        w = -(-self.NT // 3)
        w += w % 2
        self.chunks = [(c * w, min(w, self.NT - c * w)) for c in range(3)]


def build(nc, x, src, dst, gW1, gb1, gW2, gb2, W_gat, att_src, att_dst, b_gat, ln_g, ln_b,
          W1, b1, W2, b2, edge_index, out):
    E1, E2 = src.shape[0], edge_index.shape[1]
    e1_parts = max(p for p in range(1, P + 1) if E1 % p == 0 and (E1 // p) % 4 == 0)
    g1 = Graph("gcn", E1, src, dst, e1_parts, True, D)
    g2 = Graph("gat", E2, edge_index[0, :], edge_index[1, :], P, False, SEL)
    TMAX = 1088
    assert max(g1.NT, g2.NT, g1.T, g2.T) <= TMAX and g2.T % 4 == 0

    def dram(name, shape, dt):
        return nc.dram_tensor(name, shape, dt, kind="Internal").ap()

    G1 = dram("gcn_table_1", (ROWS, D), F32)
    G2 = dram("gcn_table_2", (ROWS, D), F32)
    X2 = dram("x_after_gcn", (ROWS, D), F32)
    AT = dram("ffn_in_t", (KC * P, ROWS), F32)
    TR = dram("gat_table", (ROWS, REC), F32)
    Y = dram("expert_out", (ROWS, EXPERTS * D), F32)

    with ExitStack() as ctx:
        def sb(name, shape, dt):
            return ctx.enter_context(nc.sbuf_tensor(name, shape, dt))

        def sem(name):
            return ctx.enter_context(nc.semaphore(name))

        ACCF = NBP * D
        R = sb("big", [P, max(ACCF + 9 * TMAX, g2.NT * REC)], F32)
        acc = R[:, 0:ACCF]
        gat_rows = R[:, 0:g2.NT * REC].rearrange("p (t r) -> p t r", r=REC)

        def tmp(k, dt=F32):
            v = R[:, ACCF + k * TMAX:ACCF + (k + 1) * TMAX]
            return v if dt == F32 else v.bitcast(dt)

        src_i, dst_i, valA, valB = tmp(0, I32), tmp(1, I32), tmp(2), tmp(3)
        pos, run, plo, phi = tmp(4), tmp(5), tmp(6), tmp(7)
        bin16 = tmp(8, F16)[:, 0:TMAX]
        mask = tmp(8, U16)[:, TMAX:2 * TMAX]
        zd = R[:, g2.NT * REC:g2.NT * REC + g2.NT * 3 // 2].bitcast(BF16).rearrange("p (t q) -> p t q", q=3)
        assert g2.NT * REC >= ACCF + 6 * TMAX and g2.NT * REC + g2.NT * 3 // 2 <= ACCF + 9 * TMAX

        UN = sb("phase", [P, 6144], F32)
        def onehot_slots(base, n):
            hi = base[:, 0:2 * TMAX].bitcast(F16).rearrange("p (k t) -> p k t", k=4)
            lo = base[:, 2 * TMAX:2 * TMAX + 2 * n * P].bitcast(F16).rearrange("p (k j n) -> p k j n", k=4, j=n)
            return hi, lo

        g1.oh_hi, g1.oh_lo = onehot_slots(UN, 4)
        oh_bin = UN[:, 3328:3328 + 4 * 64 // 2].bitcast(F16).rearrange("p (k n) -> p k n", k=4)
        msg = UN[:, 0:G * D].rearrange("p (k n) -> p k n", k=G)
        SC, SB = [UN[:, at:at + 2 * G * P].rearrange("p (h k n) -> p h k n", h=2, k=G)
                  for at in (G * D, 0)]
        LV = UN[:, 4096:6144].bitcast(BF16).rearrange("p (k h n) -> p k h n", k=G, h=HEADS)
        at_in = UN[:, 0:KC * 512].rearrange("p (k n) -> p k n", k=KC)
        hid = UN[:, 1024:1024 + HC * 512].rearrange("p (c n) -> p c n", c=HC)
        y_sb = UN[:, 3072:3072 + 4 * D].rearrange("p (s n) -> p s n", s=4)
        y_in = UN[:, 0:U * EXPERTS * D].rearrange("p (u e n) -> p u e n", u=U, e=EXPERTS)
        x2_in = UN[:, 4096:4096 + U * D].rearrange("p (u n) -> p u n", u=U)
        o_sb = UN[:, 5120:5120 + U * D].rearrange("p (u n) -> p u n", u=U)

        for g in (g1, g2):
            g.idx = sb(g.name + "_idx", [P, g.NT], I32)
            g.dlo = sb(g.name + "_dlo", [P, g.NT], F16)
            g.row = sb(g.name + "_row", [1, g.NT], I16)
        stage = sb("stage", [P, 2, G], I32)
        ring = sb("ring", [P, 2, G * REC], F32)
        ST = sb("sel_t", [P, G, P], BF16)
        Z = sb("z", [P, 2, P], BF16)
        VT = sb("z_t", [P, 2, P], BF16)
        LC = sb("mask_factors", [P, 4, G], F32)
        LM = sb("mask_matrix", [P, G, P], BF16)
        tiles = sb("node_tiles", [P, 4 * U * D], F32)
        xt, xn, x2t = [tiles[:, k * U * D:(k + 1) * U * D].rearrange("p (u n) -> p u n", u=U) for k in range(3)]
        aT = tiles[:, 3 * U * D:4 * U * D].rearrange("p (u k n) -> p u k n", u=U, k=KC)
        g2.oh_hi, g2.oh_lo = onehot_slots(tiles[:, U * D:4 * U * D], 3)
        big = tiles[:, 0:2 * NBP * HE].rearrange("p (j t n) -> p j t n", j=2, t=NBP)
        v8 = tiles[:, 2 * NBP * HE:2 * NBP * HE + NBP * 8].rearrange("p (t n) -> p t n", n=8)
        r8 = tiles[:, 2 * NBP * HE + NBP * 8:2 * NBP * HE + NBP * 16].rearrange("p (t n) -> p t n", n=8)
        wg = [sb(f"gcn_w{i}", [P, KC, D], F32) for i in range(2)]
        wgat = sb("gat_w", [P, KC, HE], F32)
        w1s = sb("ffn_w1", [P, KC, HID], F32)
        w2s = sb("ffn_w2", [P, HC, D], F32)
        b1s = sb("ffn_b1", [P, EXPERTS * HC], F32)
        b2s = sb("ffn_b2", [P, EXPERTS * D], F32)
        bias = [sb(f"gcn_b{i}", [P, D], F32) for i in range(2)]
        vecs = sb("gat_vecs", [P, 5, HE], F32)
        st6 = sb("bn", [P, U, 6], F32)
        mv = sb("mean_var", [P, U, 4], F32)
        dinv = sb("dinv", [P, NBP], F32)
        iota16 = sb("iota16", [P, TMAX], F16)
        iota32 = sb("iota32", [P, P], F32)
        iobin = sb("iobin", [P, 64], F32)
        ident = sb("ident", [P, P], F32)
        ident16 = sb("ident16", [P, P], BF16)
        ones = sb("ones", [P, P], F32)
        onesf16 = sb("onesf16", [P, 1], F16)
        zero16 = sb("zero16", [P, 512], F16)
        tri = sb("tri", [P, P], F32)
        H = sb("hist", [P, 64], F32)
        bn = sb("bin_small", [P, 6, 64], F32)
        bni = sb("bin_small_i", [P, 64], I32)
        tg = sb("gat_rec", [P, NBP, REC], F32)
        adst = sb("a_dst", [P, NBP, HEADS], F32)
        sc = [sb(f"score{k}", [P, NBP, EXPERTS], F32) for k in range(3)]
        one = [sb(f"one{k}", [P, NBP], F32) for k in range(2)]
        mx = sb("max_src", [P, NBP * SEL], F32)
        adp = sb("ad_parts", [P, NBP * SEL], BF16)
        acc2 = sb("gat_acc", [P, NBP * SEL], F32)
        gate = sb("gate", [P, NBP * EXPERTS], F32)
        red = sb("red", [P, G, HEADS], F32)
        asr = sb("as_res", [P, 2, G, HEADS], F32)
        ssel = sb("sel_vals", [P, G, SEL], F32)
        q8 = sb("q8", [P, G, 8], F32)
        ee = sb("ee", [P, 3, G, HEADS], F32)
        pay = sb("payload", [P, G, REC], F32)

        PS = [ctx.enter_context(nc.psum_tensor(f"ps{k}", [P, 512], F32)) for k in range(8)]

        s_const = sem("s_const")
        s_alone = sem("s_alone")
        s_w = sem("s_weights")
        s_vc = sem("s_vec_chain")
        for g in (g1, g2):
            g.s_in = sem(g.name + "_in")
            g.s_hist = sem(g.name + "_hist")
            g.s_pre = sem(g.name + "_prefix")
            g.s_scan = sem(g.name + "_scan")
            g.s_oh = sem(g.name + "_onehots")
            g.s_ab = sem(g.name + "_payloads")
            g.s_pl = sem(g.name + "_placed")
            g.s_done = sem(g.name + "_placed_all")
            g.s_cmp = sem(g.name + "_cmp")
            g.s_row = sem(g.name + "_rowps")
            g.s_ready = sem(g.name + "_ready")
        s_deg = sem("s_deg")
        s_degq = sem("s_degq")
        ph = []
        for k in range(3):
            names = ["dv", "xn", "tp", "at", "mm", "ev"]
            names += {0: ["var", "sq", "st"], 1: ["st"],
                      2: ["var", "sq", "x2", "free"]}[k]
            s = {n: sem(f"p{k}_{n}") for n in names}
            if k != 1:
                s["x"] = [sem(f"p{k}_xin{u}") for u in range(U)]
            ph.append(s)
        s_ss = [[sem(f"s_st{a}{u}") for u in range(U)] for a in range(2)]
        cv = []
        for k in range(2):
            cv.append(dict(g=[sem(f"c{k}_gath{j}") for j in range(G)],
                           ix=sem(f"c{k}_ix"),
                           s=sem(f"c{k}_sel"),
                           used=sem(f"c{k}_used"),
                           add=sem(f"c{k}_add")))
        s_ix = sem("s_ix")
        s_rec, s_recst = sem("s_rec"), sem("s_recst")
        s_gr = [sem(f"s_gr{h}") for h in range(2)]
        s_pc = sem("s_pc")
        s_fw, s_ai, s_hm, s_hg, s_ym, s_ye = [sem("e_" + n) for n in ("w", "in", "hm", "hg", "ym", "ye")]
        s_ys = [sem(f"e_ys{j}") for j in range(4)]
        a_z, a_t, a_v, a_m, a_r, a_c, a_d = [sem("a_" + n) for n in ("z", "t", "v", "m", "r", "c", "d")]
        s_adp = sem("s_adp")
        b_s, b_t, b_st, b_sel, b_sc, b_e, b_x, b_p, b_o, b_a, b_c, b_d = [sem("b_" + n) for n in
            ("s", "t", "st", "sel", "sc", "e", "x", "p", "o", "a", "c", "d")]
        s_ex, s_sx, s_gate = sem("s_ex"), sem("s_sx"), sem("s_gate")
        f_in = [sem(f"f_in{u}") for u in range(U)]
        f_c, f_o, f_free = sem("f_c"), sem("f_o"), sem("f_free")
        s_zd, s_lm = sem("s_zd"), sem("s_lm")
        f_st = [sem(f"f_st{u}") for u in range(U)]

        RT = g2.NT // G
        NCONST, NLOADS = 11, 12
        CH = ROWS // 512

        NG = g1.NT // G
        W = -(-g2.T // (2 * NG))
        LEAD = 2
        PLACE_AT = [k * G // W for k in range(W)]
        assert W <= G and NG % 4 == 0
        parts2 = [(0, NG * W), (NG * W, g2.T)]
        assert all(at % 4 == 0 for at, _ in parts2) and NG * W + (NG - 4) * W + LEAD <= g2.T

        def groups(eng, part, group):
            first, last = parts2[part]
            with eng.Fori(0, NG // 4 - 1) as i:
                for h in range(4):
                    group(i * 4 + h, h, i * (4 * W) + (first + h * W), None)
            for h in range(4):
                j = NG - 4 + h
                group(j, h, first + j * W, last)

        def alone(eng):
            eng.sem_inc(s_alone, 1)

        block = ctx.enter_context(nc.Block())

        @block.sync
        def _(sp):
            def load_edges(g):
                sp.dma_start(src_i[0:g.EP, 0:g.T], g.src.rearrange("(p t) -> p t", t=g.T)).then_inc(g.s_in, 16)
                sp.dma_start(dst_i[0:g.EP, 0:g.T], g.dst.rearrange("(p t) -> p t", t=g.T)).then_inc(g.s_in, 16)

            load_edges(g1)
            for k, w in enumerate((gW1, gW2)):
                sp.dma_start(wg[k][:, :, :], w.rearrange("(k p) n -> p k n", p=P)).then_inc(s_w, 16)
            sp.dma_start(wgat[:, :, :], W_gat.rearrange("(k p) n -> p k n", p=P)).then_inc(s_w, 16)
            for k, b in enumerate((gb1, gb2)):
                sp.dma_start(bias[k][:, :], b.partition_broadcast(P)).then_inc(s_w, 16)
            for k, b in enumerate((att_src.rearrange("a b -> (a b)"), att_dst.rearrange("a b -> (a b)"),
                                   b_gat, ln_g, ln_b)):
                sp.dma_start(vecs[:, k, :], b.partition_broadcast(P)).then_inc(s_w, 16)
            sp.dma_start(b2s[:, :], b2.rearrange("e n -> (e n)").partition_broadcast(P)).then_inc(s_w, 16)
            with nc.allow_non_contiguous_dma(reason="bias as a column per hidden chunk"):
                sp.dma_start(b1s[:, :], b1.rearrange("e (c p) -> p (e c)", p=P)).then_inc(s_w, 16)

            def load_x(s, i, tail):
                for u in range(U):
                    sp.wait_ge(s["xn"], i * U + u + 1)
                    rows = LAST if tail and u == 0 else P
                    view = x[(NBIN - 1) * P:N, :] if tail and u == 0 else (
                        x[0:P, :] if tail else x[bass.ds((i * U + u) * P, P), :])
                    sp.dma_start(xt[0:rows, u, :], view).then_inc(s["x"][u], 16)

            with sp.Fori(0, STEPS - 1) as i:
                load_x(ph[0], i, False)
            load_x(ph[0], STEPS - 1, True)
            sp.wait_ge(g1.s_ready, 1)
            load_edges(g2)
            s = ph[2]
            sp.sem_inc(s["free"], U)
            with sp.Fori(0, STEPS) as i:
                for u in range(U):
                    sp.wait_ge(s["x2"], U + i * U + u + 1)
                    sp.dma_start(X2[bass.ds((i * U + u) * P, P), :], x2t[:, u, :]).then_inc(s_ss[0][u], 16)
                    sp.wait_ge(s["at"], 2 + i * U + u + 1)
                    alone(sp)
                    sp.dma_start(AT[:, bass.ds((i * U + u) * P, P)].rearrange("(k p) n -> p k n", p=P),
                                 aT[:, u, :, :]).then_inc(s_ss[1][u], 16)
                for u in range(U):
                    sp.wait_ge(s_ss[0][u], (i + 1) * 16)
                    sp.wait_ge(s_ss[1][u], (i + 1) * 16)
                    sp.sem_inc(s["free"], 1)
            sp.wait_ge(s_rec, 1)
            sp.dma_start(TR.rearrange("(t p) r -> p t r", p=P), tg[:, :, :]).then_inc(s_recst, 16)

            for j in range(4):
                sp.dma_start(y_sb[:, j, :], b2[0, :].partition_broadcast(P)).then_inc(s_ys[j], 16)
            with sp.Fori(0, EXPERTS) as e:
                sp.wait_ge(s_ym, e * (CH * 4) + 1)
                sp.dma_start(w1s[:, :, :], W1[bass.ds(e, 1), :, :].rearrange("o (k p) n -> p (o k) n", p=P)).then_inc(s_fw, 16)
                sp.dma_start(w2s[:, :, :], W2[bass.ds(e, 1), :, :].rearrange("o (k p) n -> p (o k) n", p=P)).then_inc(s_fw, 16)
                with sp.Fori(0, CH) as c:
                    sp.wait_ge(s_hm, (e * CH + c + 1) * HC)
                    sp.dma_start(at_in[:, :, :], AT[:, bass.ds(c * 512, 512)]
                                 .rearrange("(k p) n -> p k n", p=P)).then_inc(s_ai, 16)

            sp.wait_ge(b_a, 1 + RT)
            for j in range(4):
                sp.wait_ge(s_ys[j], 16 * (1 + EXPERTS * CH))

            def final_in(i, us):
                for u in us:
                    sp.wait_ge(f_o, i * U + u + 1)
                    sp.dma_start(x2_in[:, u, :], X2[bass.ds((i * U + u) * P, P), :]).then_inc(f_in[u], 16)
                    sp.dma_start(y_in[:, u, :, :], Y[bass.ds((i * U + u) * P, P), :]
                                 .rearrange("p (e n) -> p e n", e=EXPERTS)).then_inc(f_in[u], 16)

            with sp.Fori(0, STEPS - 1) as i:
                final_in(i, range(U))
            final_in(STEPS - 1, [0])

        @block.gpsimd
        def _(pool):
            pool.iota(iota16[:, :], [[1, TMAX]], base=0, channel_multiplier=0,
                      allow_small_or_imprecise_dtypes=True).then_inc(s_const, 1)
            pool.iota(iota32[:, :], [[1, P]], base=0, channel_multiplier=0,
                      allow_small_or_imprecise_dtypes=True).then_inc(s_const, 1)
            pool.iota(iobin[:, :], [[1, 64]], base=0, channel_multiplier=0,
                      allow_small_or_imprecise_dtypes=True).then_inc(s_const, 1)
            pool.memset(ones[:, :], 1.0).then_inc(s_const, 1)
            pool.memset(onesf16[:, :], 1.0).then_inc(s_const, 1)
            pool.memset(zero16[:, :], 0.0).then_inc(s_const, 1)
            pool.memset(Z[:, :, :], 1.0).then_inc(s_const, 1)
            pool.memset(xt[:, :, :], 0.0).then_inc(s_const, 1)
            pool.memset(dinv[:, :], 1.0).then_inc(s_const, 1)
            pool.wait_ge(s_const, 9)
            pool.affine_select(out=ident[:, :], in_=ones[:, :], compare_op=ALU.is_equal, fill=0.0,
                               base=0, pattern=[[-1, P]], channel_multiplier=1).then_inc(s_const, 1)
            pool.affine_select(out=tri[:, :], in_=ones[:, :], compare_op=ALU.is_gt, fill=0.0,
                               base=0, pattern=[[1, P]], channel_multiplier=-1).then_inc(s_const, 1)

            def conv(c, g, table, s):
                pool.wait_ge(s["st"], 16 * STEPS)
                with pool.Fori(0, g.NT // (2 * G)) as i:
                    for h in range(2):
                        j = i * 2 + h
                        pool.wait_ge(c["used"], j * G + 1)
                        pool.tensor_copy(stage[:, h, :], g.idx[:, bass.ds(j * G, G)]).then_inc(c["ix"], 1)
                        pool.wait_ge(c["ix"], j + 1)
                        for k in range(G):
                            pool.wait_ge(c["used"], j * G + k + 1)
                            alone(pool)
                            pool.indirect_dma_start(
                                out=msg[:, k, :], out_offset=None, in_=table[:, :],
                                in_offset=bass.IndirectOffsetOnAxis(ap=stage[:, h, k:k + 1], axis=0),
                            ).then_inc(c["g"][k], 16)

            pool.wait_ge(g1.s_ready, 1)
            conv(cv[0], g1, G1, ph[0])
            conv(cv[1], g1, G2, ph[1])

            def load_x(s, i, tail):
                for u in range(U):
                    pool.wait_ge(s["x2"], i * U + u + 1)
                    rows = LAST if tail and u == 0 else P
                    view = x[(NBIN - 1) * P:N, :] if tail and u == 0 else (
                        x[0:P, :] if tail else x[bass.ds((i * U + u) * P, P), :])
                    pool.dma_start(xt[0:rows, u, :], view).then_inc(s["x"][u], 16)

            with pool.Fori(0, STEPS - 1) as i:
                load_x(ph[2], i, False)
            load_x(ph[2], STEPS - 1, True)

            pool.memset(LV[:, :, :, :], 0.0).then_inc(s_lm, 1)
            pool.memset(LC[:, :, :], 0.0).then_inc(s_lm, 1)
            for p in range(3):
                pool.wait_ge(s_lm, 2 + p)
                pool.affine_select(out=LV[:, :, :, :], in_=LV[:, :, :, :], compare_op=ALU.not_equal, fill=1.0,
                                   base=-4 * p, pattern=[[-12, G], [-1, HEADS], [0, P]], channel_multiplier=1).then_inc(s_lm, 1)
            for n, (col, row, step, fill) in enumerate(((0, 96, 3, 2.0 * PEN), (1, 97, 3, -128.0 * PEN), (1, 98, 3, -PEN),
                                                        (2, 120, 0, -128.0 * PEN), (3, 121, 0, -PEN))):
                pool.wait_ge(s_lm, 5 + n)
                pool.affine_select(out=LC[:, col, :], in_=LC[:, col, :], compare_op=ALU.not_equal, fill=fill,
                                   base=-row, pattern=[[-step, G]], channel_multiplier=1).then_inc(s_lm, 1)

            pool.wait_ge(s_recst, 16)
            pool.wait_ge(g2.s_ready, 1)

            def gather(j, h):
                pool.tensor_copy(stage[:, h, :], g2.idx[:, bass.ds(j * G, G)]).then_inc(s_ix, 1)
                pool.wait_ge(s_ix, j + 1)
                alone(pool)
                for k in range(G):
                    pool.indirect_dma_start(
                        out=ring[:, h, k * REC:(k + 1) * REC], out_offset=None, in_=TR[:, :],
                        in_offset=bass.IndirectOffsetOnAxis(ap=stage[:, h, k:k + 1], axis=0),
                    ).then_inc(s_gr[h], 16)

            def place(j, h):
                pool.wait_ge(s_gr[h], (j - h + 2) * (G * 8))
                pool.tensor_copy(R[:, bass.ds(j * (G * REC), G * REC)], ring[:, h, :]).then_inc(s_pc, 1)
                pool.wait_ge(s_pc, j + 1)

            gather(0, 0)
            with pool.Fori(0, RT // 2 - 1) as i:
                gather(i * 2 + 1, 1)
                place(i * 2, 0)
                gather(i * 2 + 2, 0)
                place(i * 2 + 1, 1)
            gather(RT - 1, 1)
            place(RT - 2, 0)
            place(RT - 1, 1)

        @block.tensor
        def _(pe):
            mm = nc.tensor.matmul
            pe.wait_ge(s_const, NCONST)
            pe.wait_ge(s_w, 16 * NLOADS)

            def products(g):
                return [(3 * j + c, at, w, j) for j in range(2) for c, (at, w) in enumerate(g.chunks)]

            def edge(g, start, stop):
                for b, _, w, _ in products(g):
                    last = mm(PS[b][:, 0:w], zero16[:, 0:P], zero16[:, 0:w], start=start, stop=stop)
                if g.with_degree:
                    last = mm(PS[6][:, 0:NBIN], zero16[:, 0:P], zero16[:, 0:NBIN], start=start, stop=stop)
                return last

            def sort_open(g):
                pe.sem_inc(g.s_pl, 4)
                pe.wait_ge(g.s_hist, NBIN)
                mm(PS[7][:, 0:NBIN], ones[0:g.EP, :], H[0:g.EP, 0:NBIN], start=True, stop=True)
                mm(PS[7][:, 64:64 + NBIN], tri[0:g.EP, :], H[0:g.EP, 0:NBIN], start=True, stop=True,
                   skip_group_check=True).then_inc(g.s_pre, 1)
                edge(g, True, False)

            def place(g, col, k):
                pe.wait_ge(g.s_oh, col + 1)
                pe.wait_ge(g.s_ab, (col + 1) * 2)
                for b, at, w, j in products(g):
                    last = mm(PS[b][:, 0:w], g.oh_lo[0:g.EP, k, j, :], g.oh_hi[0:g.EP, k, at:at + w],
                              start=False, stop=False)
                if g.with_degree:
                    last = mm(PS[6][:, 0:NBIN], g.oh_lo[0:g.EP, k, 3, :], oh_bin[0:g.EP, k, 0:NBIN],
                              start=False, stop=False)
                last.then_inc(g.s_pl, 1)

            def sort_close(g):
                edge(g, False, True).then_inc(g.s_done, 1)
                pe.wait_ge(g.s_cmp, 1)
                for c, (at, w) in enumerate(g.chunks):
                    last = mm(PS[c][0:1, 0:w], onesf16[0:NBIN, 0:1], g.oh_hi[0:NBIN, 0, at:at + w],
                              start=True, stop=True)
                last.then_inc(g.s_row, 1)

            def phase(s, w, n, banks):
                slots = len(banks) // 2
                pe.sem_inc(s["tp"], U)
                pe.sem_inc(s["mm"], U)
                with pe.Fori(0, STEPS) as i:
                    for pair in range(0, U, 2):
                        for u in (pair, pair + 1):
                            pe.wait_ge(s["xn"], U + i * U + u + 1)
                            pe.wait_ge(s["at"], i * U + u + 1)
                            for c in range(KC):
                                last = nc.tensor.transpose(PS[banks[u % slots]][:, c * P:(c + 1) * P],
                                                           xn[:, u, c * P:(c + 1) * P], ident[:, :])
                            last.then_inc(s["tp"], 1)
                        for u in (pair, pair + 1):
                            pe.wait_ge(s["at"], slots + i * U + u + 1)
                            pe.wait_ge(s["ev"], i * U + u + 1)
                            for c in range(KC):
                                last = mm(PS[banks[slots + u % slots]][:, 0:n], aT[:, u, c, :], w[:, c, :],
                                          start=c == 0, stop=c == KC - 1)
                            last.then_inc(s["mm"], 1)

            def conv(part):
                c = cv[part]
                pe.sem_inc(c["used"], G)

                def group(j, h, col, end):
                    pe.wait_ge(c["s"], j + 1)
                    for k in range(G):
                        pe.wait_ge(c["g"][k], (j + 1) * 16)
                        pe.wait_ge(c["add"], j * G + k + 1)
                        mm(PS[6 + k % 2][:, 0:D], SC[:, h % 2, k, :], msg[:, k, :], start=True, stop=True).then_inc(c["used"], 1)
                        if k in PLACE_AT:
                            q = PLACE_AT.index(k)
                            if end is None or col + q < end:
                                place(g2, col + q, (h * W + q) % 4)

                groups(pe, part, group)

            sort_open(g1)
            with pe.Fori(0, g1.T // 4) as i:
                for k in range(4):
                    place(g1, i * 4 + k, k)
            sort_close(g1)
            phase(ph[0], wg[0], D, (0, 1, 2, 3))
            pe.wait_ge(ph[0]["ev"], 2 + NBP)
            sort_open(g2)
            conv(0)
            phase(ph[1], wg[1], D, (6, 7))
            conv(1)
            sort_close(g2)
            phase(ph[2], wgat, HE, (0, 1, 2, 3))

            def a_front(j, h):
                pe.wait_ge(a_z, j + 1)
                pe.wait_ge(a_v, j + 1)
                mm(PS[4 + h][0:ZR, 0:P], Z[:, h, 0:ZR], ident16[:, :], start=True, stop=True).then_inc(a_t, 1)

            def a_back(j, h):
                pe.wait_ge(a_v, 2 + j + 1)
                rows = VT[0:ZR, h, :]
                for k in range(G):
                    pe.wait_ge(a_r, j * G + k + 1)
                    out_ = PS[6 + k % 2]
                    mm(out_[:, :], LM[0:ZR, k, :], rows.unsqueeze(1).to_broadcast([ZR, HEADS, P]), start=True, stop=False)
                    for hd in range(HEADS):
                        last = mm(out_[:, hd * P:(hd + 1) * P], LV[0:ZR, k, hd, :], rows, start=False, stop=hd == HEADS - 1)
                    last.then_inc(a_m, 1)

            def hidden(n):
                pe.wait_ge(s_ai, (n + 1) * 16)
                for q in range(HC):
                    pe.wait_ge(s_hg, n * HC + q + 1)
                    for k in range(KC):
                        last = mm(PS[q % 2][:, :], w1s[:, k, q * P:(q + 1) * P],
                                  at_in[:, k, :], start=k == 0, stop=k == KC - 1)
                    last.then_inc(s_hm, 1)

            def result(n):
                pe.wait_ge(s_hg, 2 + (n + 1) * HC)
                for j in range(4):
                    pe.wait_ge(s_ye, n * 4 + j + 1)
                    for q in range(HC):
                        last = mm(PS[2 + j % 2][:, 0:D], hid[:, q, j * P:(j + 1) * P], w2s[:, q, :],
                                  start=q == 0, stop=q == HC - 1)
                    last.then_inc(s_ym, 1)

            pe.sem_inc(s_ym, 1)
            pe.sem_inc(s_hm, HC)
            pe.wait_ge(s_zd, 1)
            pe.wait_ge(ph[2]["ev"], 2 + NBP)
            a_front(0, 0)
            with pe.Fori(0, EXPERTS) as e:
                pe.wait_ge(s_fw, (e + 1) * 32)
                alone(pe)
                with pe.Fori(0, CH) as c:
                    i = e * CH + c
                    a_front(i * 2 + 1, 1)
                    a_back(i * 2, 0)
                    hidden(i)
                    a_front(i * 2 + 2, 0)
                    a_back(i * 2 + 1, 1)
                    result(i)
            with pe.Fori(EXPERTS * CH, RT // 2 - 1) as i:
                a_front(i * 2 + 1, 1)
                a_back(i * 2, 0)
                a_front(i * 2 + 2, 0)
                a_back(i * 2 + 1, 1)
            a_front(RT - 1, 1)
            a_back(RT - 2, 0)
            a_back(RT - 1, 1)

            row_regs = [pe.alloc_register(f"pe_bin{k}") for k in range(G)]

            def b_trans(j, h):
                for half in range(2):
                    for k in range(4 * half, 4 * half + 4):
                        if k % 4 == 0:
                            pe.wait_ge(b_s, j + 1)
                            pe.wait_ge(b_st, j * 2 + half + 1)
                        last = nc.tensor.transpose(PS[half][:, (k % 4) * P:(k % 4 + 1) * P], SB[:, h, k, :], ident[:, :])
                    last.then_inc(b_t, 1)

            def b_select(j):
                pe.load(row_regs, g2.row[0:1, bass.ds(j * G, G)])
                offs = [pe.snap(r, min_val=0, max_val=NBIN * SEL) for r in row_regs]
                pe.wait_ge(b_sc, j + 1)
                pe.wait_ge(b_st, 2 + (j + 1) * 2)
                for k in range(G):
                    last = mm(PS[2][:, k * SEL:(k + 1) * SEL], ST[:, k, :], adp[:, bass.ds(offs[k], SEL)],
                              start=True, stop=True, skip_group_check=True)
                last.then_inc(b_sel, 1)

            def b_sum(j, h):
                pe.wait_ge(b_p, j + 1)
                pe.wait_ge(b_a, j + 1)
                for k in range(G):
                    last = mm(PS[3][:, k * REC:(k + 1) * REC], SB[:, h, k, :], pay[:, k, :],
                              start=True, stop=True, skip_group_check=True)
                last.then_inc(b_o, 1)

            pe.wait_ge(s_adp, 1)
            b_trans(0, 0)
            b_select(0)
            with pe.Fori(0, RT // 2 - 1) as i:
                for h in range(2):
                    j = i * 2 + h
                    b_trans(j + 1, 1 - h)
                    b_select(j + 1)
                    b_sum(j, h)
            b_trans(RT - 1, 1)
            b_select(RT - 1)
            b_sum(RT - 2, 0)
            b_sum(RT - 1, 1)

        @block.scalar
        def _(act):
            act.wait_ge(s_const, NCONST)
            copy = lambda o, i: nc.scalar.activation(o, i, ACT.Copy)

            def scale(g, i, k):
                act.wait_ge(g.s_oh, i * 4 + k + 1)
                alone(act)
                for n, val in enumerate((valA, valB)):
                    nc.scalar.activation(g.oh_lo[0:g.EP, k, n, :], g.oh_lo[0:g.EP, k, 2, :], ACT.Copy,
                                         scale=val[0:g.EP, bass.ds(i * 4 + k, 1)]).then_inc(g.s_ab, 1)

            def scale_all(g, first, end):
                with act.Fori(first // 4, end // 4) as i:
                    for k in range(4):
                        scale(g, i, k)

            scale_all(g1, 0, g1.T)
            act.wait_ge(s_deg, 1)
            nc.scalar.activation(one[1][:, 0:NBIN], one[0][:, 0:NBIN], ACT.Sqrt).then_inc(s_degq, 1)

            def phase(k, s, n, table, banks):
                slots = len(banks) // 2
                act.sem_inc(s["at"], slots)
                act.sem_inc(s["ev"], slots)
                with act.Fori(0, STEPS) as i:
                    if k != 1:
                        act.wait_ge(s["var"], i + 1)
                        nc.scalar.activation(mv[:, :, 3], mv[:, :, 2], ACT.Sqrt).then_inc(s["sq"], 1)
                    for pair in range(0, U, 2):
                        for u in (pair, pair + 1):
                            act.wait_ge(s["tp"], U + i * U + u + 1)
                            act.wait_ge(s["mm"], i * U + u + 1)
                            if k == 2:
                                act.wait_ge(s["free"], i * U + u + 1)
                            copy(aT[:, u, :, :], PS[banks[u % slots]][:, 0:D].rearrange("p (k n) -> p k n", k=KC)).then_inc(s["at"], 1)
                        for u in (pair, pair + 1):
                            act.wait_ge(s["mm"], U + i * U + u + 1)
                            alone(act)
                            if k == 2:
                                copy(tg[:, bass.ds(i * U + u, 1), 0:HE],
                                     PS[banks[slots + u % slots]][:, 0:HE].unsqueeze(1)).then_inc(s["ev"], 1)
                            else:
                                nc.scalar.activation(acc[:, bass.ds((i * U + u) * D, D)],
                                                     PS[banks[slots + u % slots]][:, 0:D], ACT.Copy,
                                                     scale=dinv[:, bass.ds(i * U + u, 1)]).then_inc(s["ev"], 1)
                    if table is not None:
                        act.wait_ge(s["ev"], slots + (i + 1) * U)
                        alone(act)
                        act.dma_start(table[bass.ds(i * U * P, U * P), :].rearrange("(u p) n -> p u n", p=P),
                                      acc[:, bass.ds(i * U * D, U * D)].rearrange("p (u n) -> p u n", u=U)).then_inc(s["st"], 16)

            act.wait_ge(g1.s_ready, 1)
            phase(0, ph[0], D, G1, (0, 1, 2, 3))
            scale_all(g2, *parts2[0])
            phase(1, ph[1], D, G2, (6, 7))
            scale_all(g2, *parts2[1])
            phase(2, ph[2], HE, None, (0, 1, 2, 3))

            act.sem_inc(s_hg, 2)

            def gelu(e, c):
                for q in range(HC):
                    act.wait_ge(s_hm, HC + (e * CH + c) * HC + q + 1)
                    alone(act)
                    nc.scalar.activation(hid[:, q, :], PS[q % 2][:, :], ACT.Gelu,
                                         bias=b1s[:, bass.ds(e * HC + q, 1)]).then_inc(s_hg, 1)

            def store_y(e, c):
                for j in range(4):
                    act.wait_ge(s_ye, 2 + (e * CH + c) * 4 + j + 1)
                    act.dma_start(Y[bass.ds((c * 4 + j) * P, P), bass.ds(e * D, D)],
                                  y_sb[:, j, :]).then_inc(s_ys[j], 16)

            def a_rows(j, h):
                act.wait_ge(a_t, j + 1)
                copy(VT[0:ZR, h, :], PS[4 + h][0:ZR, 0:P]).then_inc(a_v, 1)

            act.sem_inc(a_v, 2)
            a_rows(0, 0)
            with act.Fori(0, EXPERTS) as e:
                def pair(c):
                    n = e * CH + c
                    a_rows(n * 2 + 1, 1)
                    gelu(e, c)
                    a_rows(n * 2 + 2, 0)

                pair(0)
                with act.Fori(1, CH) as c:
                    pair(c)
                    store_y(e, c - 1)
                store_y(e, CH - 1)
            with act.Fori(EXPERTS * CH, RT // 2 - 1) as i:
                a_rows(i * 2 + 1, 1)
                a_rows(i * 2 + 2, 0)
            a_rows(RT - 1, 1)

            act.wait_ge(s_ex, 1)
            acc2v = acc2[:, :].rearrange("p (t s) -> p t s", s=SEL)
            nc.scalar.activation(acc2v[:, :, HE:REC], big[:, 1, :, 0:HEADS], ACT.Exp).then_inc(s_sx, 1)
            act.sem_inc(b_st, 2)
            act.sem_inc(b_sc, 1)

            def b_copy(j):
                for half in range(2):
                    act.wait_ge(b_t, j * 2 + half + 1)
                    copy(ST[:, 4 * half:4 * half + 4, :], PS[half][:, :].rearrange("p (k n) -> p k n", k=4)).then_inc(b_st, 1)

            def b_exp(j):
                act.wait_ge(b_e, j + 1)
                nc.scalar.activation(pay[:, :, HE:REC], ee[:, 2, :, :], ACT.Exp).then_inc(b_x, 1)

            def b_values(j):
                act.wait_ge(b_sel, j + 1)
                copy(ssel[:, :, :], PS[2][:, 0:G * SEL].rearrange("p (k n) -> p k n", k=G)).then_inc(b_sc, 1)

            b_copy(0)
            b_values(0)
            b_exp(0)
            b_copy(1)
            b_values(1)
            with act.Fori(1, RT - 1) as j:
                act.wait_ge(b_o, j)
                b_exp(j)
                b_copy(j + 1)
                b_values(j + 1)
            act.wait_ge(b_o, RT - 1)
            b_exp(RT - 1)
            act.wait_ge(s_ex, 2)
            nc.scalar.activation(one[1][:, :], one[0][:, :], ACT.Sqrt).then_inc(s_sx, 1)
            act.wait_ge(s_ex, 3)
            nc.scalar.activation(sc[1][:, :, :], sc[2][:, :, :], ACT.Exp).then_inc(s_sx, 1)

            act.sem_inc(f_free, U)

            def final_out(i, us, rows):
                for u in us:
                    act.wait_ge(f_o, U + i * U + u + 1)
                    act.dma_start(out[bass.ds((i * U + u) * P, rows), :], o_sb[0:rows, u, :]).then_inc(f_st[u], 16)

            with act.Fori(0, STEPS - 1) as i:
                final_out(i, range(U), P)
                for u in range(U):
                    act.wait_ge(f_st[u], (i + 1) * 16)
                    act.sem_inc(f_free, 1)
            final_out(STEPS - 1, [0], LAST)
            act.wait_ge(f_st[0], STEPS * 16)

        @block.vector
        def _(vec):
            v = nc.vector
            ch = Counter(vec, s_vc)
            vec.wait_ge(s_const, NCONST)
            vec.wait_ge(s_w, 16 * NLOADS)
            ch.step(v.tensor_copy(ident16[:, :], ident[:, :]))

            def rank(g):
                p, t = g.EP, g.T
                vec.wait_ge(g.s_in, 32)
                si, di, a_f, b_f = src_i[0:p, 0:t], dst_i[0:p, 0:t], valA[0:p, 0:t], valB[0:p, 0:t]
                lo_f = tmp(0)[0:p, 0:t]
                pos_f, pos_i = pos[0:p, 0:t], tmp(4, I32)[0:p, 0:t]
                run_f, run_i = run[0:p, 0:t], tmp(5, I32)[0:p, 0:t]
                plo_f, plo_i = plo[0:p, 0:t], tmp(6, I32)[0:p, 0:t]
                phi_f = phi[0:p, 0:t]
                b16, mk = bin16[0:p, 0:t], mask[0:p, 0:t]
                ch.step(v.tensor_scalar(si, si, float(N - 1), None, ALU.min))
                ch.step(v.tensor_scalar(plo_i, si, 3, None, ALU.arith_shift_right))
                ch.step(v.tensor_copy(a_f, plo_i))
                ch.step(v.tensor_scalar(plo_i, si, 7, None, ALU.bitwise_and))
                ch.step(v.tensor_scalar(run_i, di, P - 1, None, ALU.bitwise_and))
                ch.step(v.tensor_copy(lo_f, run_i))
                ch.step(v.tensor_scalar(b_f, plo_i, 256.0, 1.0, ALU.mult, ALU.add))
                ch.step(v.tensor_tensor(b_f, b_f, lo_f, ALU.add))
                ch.step(v.tensor_scalar(plo_i, di, 7, None, ALU.arith_shift_right))
                ch.step(v.tensor_scalar(phi_f, di, float(N), 64.0, ALU.is_ge, ALU.mult))
                ch.step(v.tensor_tensor(b16, phi_f, plo_i, ALU.add))
                with v.Fori(0, NBIN) as b:
                    v.tensor_scalar(mk, b16, iobin[0:p, bass.ds(b, 1)], None, ALU.is_equal, ALU.add,
                                    accum_out=H[0:p, bass.ds(b, 1)]).then_inc(g.s_hist, 1)
                    vec.wait_ge(g.s_hist, b + 1)
                vec.wait_ge(g.s_pre, 1)
                nb = slice(0, NBIN)
                ch.step(v.tensor_scalar(bni[:, nb], PS[7][:, nb], float(P - 1), None, ALU.add))
                ch.step(v.tensor_scalar(bni[:, nb], bni[:, nb], 7, None, ALU.arith_shift_right))
                ch.step(v.tensor_copy(bn[:, 0, nb], bni[:, nb]))
                ch.step(v.tensor_tensor_scan(bn[:, 1, nb], bn[:, 0, nb], bn[:, 0, nb], 0.0, ALU.add, ALU.max))
                ch.step(v.tensor_tensor(bn[:, 2, nb], bn[:, 1, nb], bn[:, 0, nb], ALU.subtract))
                ch.step(v.scalar_tensor_tensor(bn[:, 3, nb], bn[:, 2, nb], float(P), PS[7][:, 64:64 + NBIN],
                                               ALU.mult, ALU.add))
                ch.step(v.memset(pos_f, float(1 << 20)))
                with v.Fori(0, NBIN) as b:
                    lc = Counter(vec, g.s_scan, base=b * 3)
                    lc.step(v.tensor_scalar(mk, b16, iobin[0:p, bass.ds(b, 1)], None, ALU.is_equal))
                    lc.step(v.tensor_tensor_scan(run_f, mk, mk, bn[0:p, 3, bass.ds(b, 1)], ALU.add, ALU.max))
                    alone(vec)
                    lc.step(v.copy_predicated(pos_f, mk, run_f))
                ch.step(v.tensor_scalar(run_i, pos_f, -1.0, None, ALU.add))
                ch.step(v.tensor_scalar(pos_i, run_i, 7, None, ALU.arith_shift_right))
                ch.step(v.tensor_copy(phi_f, pos_i))
                ch.step(v.tensor_scalar(pos_i, run_i, P - 1, None, ALU.bitwise_and))
                ch.step(v.tensor_copy(plo_f, pos_i))

            def column(g, col, k):
                p = g.EP
                at = lambda a: a[0:p, bass.ds(col, 1)]
                vec.wait_ge(g.s_pl, col + 1)
                v.tensor_scalar(g.oh_hi[0:p, k, 0:g.NT], iota16[0:p, 0:g.NT], at(phi), None, ALU.is_equal)
                last = v.tensor_scalar(g.oh_lo[0:p, k, 2, :], iota16[0:p, 0:P], at(plo), None, ALU.is_equal)
                if g.with_degree:
                    v.tensor_scalar(g.oh_lo[0:p, k, 3, :], iota16[0:p, 0:P], at(tmp(0)), None, ALU.is_equal)
                    last = v.tensor_scalar(oh_bin[0:p, k, 0:NBIN], iota16[0:p, 0:NBIN], at(bin16), None, ALU.is_equal)
                last.then_inc(g.s_oh, 1)

            def tables(g):
                nb = slice(0, NBIN)
                vec.wait_ge(g.s_done, 1)
                for c, (at, w) in enumerate(g.chunks):
                    bi, hi = tmp(0, I32)[:, at:at + w], tmp(1, I32)[:, at:at + w]
                    ch.step(v.tensor_copy(bi, PS[3 + c][:, 0:w]))
                    ch.step(v.tensor_scalar(hi, bi, 8, None, ALU.arith_shift_right))
                    ch.step(v.scalar_tensor_tensor(g.idx[:, at:at + w], PS[c][:, 0:w], 8.0, hi, ALU.mult, ALU.add))
                    ch.step(v.tensor_scalar(hi, bi, 255, None, ALU.bitwise_and))
                    ch.step(v.tensor_scalar(g.dlo[:, at:at + w], hi, -1.0, None, ALU.add))
                if g is g2:
                    d2, dp = tmp(2, I32)[:, 0:g.NT], tmp(3, I32)[:, 0:g.NT]
                    ch.step(v.tensor_tensor(d2, g.dlo[:, :], g.dlo[:, :], ALU.mult))
                    ch.step(v.tensor_copy(zd[:, :, 0], g.dlo[:, :]))
                    ch.step(v.tensor_scalar(dp, d2, 7, None, ALU.arith_shift_right))
                    ch.step(v.tensor_copy(zd[:, :, 1], dp))
                    ch.step(v.tensor_scalar(dp, d2, P - 1, None, ALU.bitwise_and))
                    ch.step(v.tensor_copy(zd[:, :, 2], dp))
                ch.step(v.tensor_tensor(bn[:, 4, nb], bn[:, 1, nb], ident[:, nb], ALU.mult))
                ch.step(v.reduce_sum(bn[:, 5, 0:1], bn[:, 4, nb], axis=AX.X))
                v.tensor_scalar(g.oh_hi[0:NBIN, 0, 0:g.NT], iota16[0:NBIN, 0:g.NT], bn[0:NBIN, 5, 0:1], None,
                                ALU.is_ge).then_inc(g.s_cmp, 1)
                vec.wait_ge(g.s_row, 1)
                for c, (at, w) in enumerate(g.chunks):
                    last = v.tensor_scalar(g.row[0:1, at:at + w], PS[c][0:1, 0:w], float(g.row_stride), None, ALU.mult)
                ch.step(last)
                if g.with_degree:
                    v.tensor_scalar(one[0][:, nb], PS[6][:, nb], 1.0, None, ALU.add).then_inc(s_deg, 1)
                    vec.wait_ge(s_degq, 1)
                    ch.step(v.reciprocal(dinv[:, nb], one[1][:, nb]))
                vec.sem_inc(g.s_ready, 1)

            def phase(k, s, first):
                vec.sem_inc(s["xn"], U)
                if k == 2:
                    vec.sem_inc(s["x2"], U)
                with v.Fori(0, STEPS) as i:
                    per = 1 if k == 1 else 4
                    lc = Counter(vec, s["dv"], base=i * {0: 10, 1: 4, 2: 14}[k])
                    tile = lambda u: acc[:, bass.ds((i * U + u) * D, D)]
                    dcol = lambda u: dinv[:, bass.ds(i * U + u, 1)]
                    if k == 1:
                        for u in range(U):
                            lc.inc(v.scalar_tensor_tensor(x2t[:, u, :], tile(u), dcol(u), bias[0][:, :], ALU.mult, ALU.add))
                        lc.wait()
                        for u in range(U):
                            vec.wait_ge(s["tp"], i * U + u + 1)
                            v.tensor_scalar(xn[:, u, :], x2t[:, u, :], 0.0, None, ALU.max).then_inc(s["xn"], 1)
                        vec.wait_ge(s["xn"], U + (i + 1) * U)
                    else:
                        srct = xt
                        if k == 2:
                            for u in range(U):
                                vec.wait_ge(s["x"][u], (i + 1) * 16)
                                vec.wait_ge(s["free"], i * U + u + 1)
                                lc.inc(v.scalar_tensor_tensor(x2t[:, u, :], tile(u), dcol(u), xt[:, u, :], ALU.mult, ALU.add))
                            lc.wait()
                            for u in range(U):
                                v.tensor_tensor(x2t[:, u, :], x2t[:, u, :], bias[1][:, :], ALU.add).then_inc(s["x2"], 1)
                            vec.wait_ge(s["x2"], U + (i + 1) * U)
                            srct = x2t
                        for u in range(U):
                            if k == 0:
                                vec.wait_ge(s["x"][u], (i + 1) * 16)
                            lc.inc(v.bn_stats(st6[:, u, :], srct[:, u, :]))
                        lc.wait()
                        alone(vec)
                        for u in range(U):
                            lc.inc(v.bn_aggr(mv[:, u, 0:2], st6[:, u, :]))
                        lc.wait()
                        v.tensor_scalar(mv[:, :, 2], mv[:, :, 1], LN_EPS, None, ALU.add).then_inc(s["var"], 1)
                        vec.wait_ge(s["sq"], i + 1)
                        lc.step(v.reciprocal(mv[:, :, 2], mv[:, :, 3]))
                        for u in range(U):
                            vec.wait_ge(s["tp"], i * U + u + 1)
                            v.tensor_scalar(xn[:, u, :], srct[:, u, :], mv[:, u, 0:1], mv[:, u, 2:3],
                                            ALU.subtract, ALU.mult).then_inc(s["xn"], 1)
                        lc.step(v.tensor_copy(one[0][:, 0:1], mv[:, 0, 0:1]))
                    assert lc.n == {0: 10, 1: 4, 2: 14}[k]

            def one_hots(g, j, out_):
                return v.tensor_tensor(out_, iota32[:, :].unsqueeze(1).to_broadcast([P, G, P]),
                                       g.dlo[:, bass.ds(j * G, G)].unsqueeze(2).to_broadcast([P, G, P]), ALU.is_equal)

            row_regs = [vec.alloc_register(f"dve_bin{k}") for k in range(G)]

            def bins(g, i, top):
                vec.load(row_regs, g.row[0:1, bass.ds(i * G, G)])
                return [vec.snap(r, min_val=0, max_val=top) for r in row_regs]

            def conv(part):
                c, (first, _) = cv[part], parts2[part]

                def hots(j, h):
                    one_hots(g1, j, SC[:, h % 2, :, :]).then_inc(c["s"], 1)

                def group(j, h, col, end):
                    if end is None or j + 1 < NG:
                        hots(j + 1, h + 1)
                    offs = bins(g1, j, NBIN * D)
                    for k in range(G):
                        if k in PLACE_AT:
                            q = PLACE_AT.index(k) + LEAD
                            if end is None or col + q < end:
                                column(g2, col + q, (h * W + q) % 4)
                        vec.wait_ge(c["used"], G + j * G + k + 1)
                        vec.wait_ge(c["add"], 2 + j * G + k)
                        a = acc[:, bass.ds(offs[k], D)]
                        v.tensor_tensor(a, a, PS[6 + k % 2][:, 0:D], ALU.add).then_inc(c["add"], 1)

                vec.sem_inc(c["add"], 2)
                hots(0, 0)
                for q in range(LEAD):
                    column(g2, first + q, q)
                groups(v, part, group)
                vec.wait_ge(c["add"], 2 + g1.NT)

            rank(g1)
            with v.Fori(0, g1.T // 4) as i:
                for k in range(4):
                    column(g1, i * 4 + k, k)
            tables(g1)
            phase(0, ph[0], True)
            rank(g2)
            vec.wait_ge(ph[0]["st"], 16 * STEPS)
            conv(0)
            phase(1, ph[1], False)
            vec.wait_ge(ph[1]["st"], 16 * STEPS)
            conv(1)
            tables(g2)
            phase(2, ph[2], False)

            bc = lambda k: vecs[:, k, :].unsqueeze(1).to_broadcast([P, NBP, HE])
            he = lambda a: a.rearrange("p t (h e) -> p t h e", h=HEADS)
            hb = lambda a: a.unsqueeze(3).to_broadcast([P, NBP, HEADS, EXPERTS])
            w0, w1 = big[:, 0, :, :], big[:, 1, :, :]
            h4 = slice(0, HEADS)
            vec.wait_ge(ph[2]["ev"], 2 + NBP)
            ch.step(v.tensor_tensor(w0, tg[:, :, 0:HE], bc(0), ALU.mult))
            ch.step(v.tensor_tensor(w1, tg[:, :, 0:HE], bc(1), ALU.mult))
            ch.step(v.reduce_sum(adst[:, :, :], he(w1), axis=AX.X))
            v.reduce_sum(tg[:, :, HE:REC], he(w0), axis=AX.X).then_inc(s_rec, 1)
            vec.wait_ge(s_rec, 1)
            mxv = mx[:, :].rearrange("p (t s) -> p t s", s=SEL)
            ch.step(v.tensor_copy(mxv[:, :, 0:HEADS], tg[:, :, HE:REC]))

            def add_bias(e, c):
                n = e * CH + c
                for j in range(4):
                    vec.wait_ge(s_ym, 1 + n * 4 + j + 1)
                    vec.wait_ge(s_ys[j], (n + 1) * 16)
                    v.tensor_tensor(y_sb[:, j, :], PS[2 + j % 2][:, 0:D], b2s[:, bass.ds(e * D, D)],
                                    ALU.add).then_inc(s_ye, 1)

            vec.wait_ge(s_lm, 10)
            sq, sqf, sqi = [tiles[:, at * P:(at + w) * P].rearrange("p (j n) -> p j n", n=P)
                            for at, w in ((0, 1), (1, 2), (3, 2))]
            sq, sqi = sq[:, 0, :], sqi.bitcast(I32)
            ch.step(v.tensor_tensor(sq, iota32[:, :], iota32[:, :], ALU.mult))
            ch.step(v.tensor_copy(sqi[:, 0, :], sq))
            ch.step(v.tensor_scalar(sqi[:, 1, :], sqi[:, 0, :], 7, None, ALU.arith_shift_right))
            ch.step(v.tensor_scalar(sqi[:, 0, :], sqi[:, 0, :], P - 1, None, ALU.bitwise_and))
            ch.step(v.tensor_copy(sqf[:, 0, :], sqi[:, 1, :]))
            ch.step(v.tensor_copy(sqf[:, 1, :], sqi[:, 0, :]))
            for k in range(G):
                ch.step(v.tensor_scalar(sq, iota32[:, :], LC[:, 0, k:k + 1], LC[:, 1, k:k + 1], ALU.mult, ALU.add))
                ch.step(v.scalar_tensor_tensor(sq, sqf[:, 0, :], LC[:, 2, k:k + 1], sq, ALU.mult, ALU.add))
                ch.step(v.scalar_tensor_tensor(LM[:, k, :], sqf[:, 1, :], LC[:, 3, k:k + 1], sq, ALU.mult, ALU.add))
            vec.sem_inc(s_zd, 1)

            def a_front(j, h):
                vec.wait_ge(s_pc, j + 1)
                rec = R[:, bass.ds(j * (G * REC), G * REC)].rearrange("p (k r) -> p k r", k=G)
                a_src = rec[:, :, HE:REC]
                part = [Z[:, h, 0:96].rearrange("p (k q) -> p k q", k=G)[:, :, 4 * p:4 * p + 4] for p in range(3)]
                lc = Counter(vec, a_c, base=j * 5)
                lc.inc(v.tensor_copy(Z[:, h, 96:120].rearrange("p (k q) -> p k q", q=3), zd[:, bass.ds(j * G, G), :]))
                lc.step(v.tensor_copy(part[0], a_src))
                lc.step(v.tensor_tensor(asr[:, 0, :, :], a_src, part[0], ALU.subtract))
                lc.step(v.tensor_copy(part[1], asr[:, 0, :, :]))
                lc.step(v.tensor_tensor(asr[:, 1, :, :], asr[:, 0, :, :], part[1], ALU.subtract))
                assert lc.n == 5
                v.tensor_copy(part[2], asr[:, 1, :, :]).then_inc(a_z, 1)

            def a_back(j, h):
                offs = bins(g2, j, NBIN * SEL)
                lc = Counter(vec, a_d, base=j * G)
                for k in range(G + 1):
                    if k < G:
                        vec.wait_ge(a_m, j * G + k + 1)
                        v.tensor_reduce(red[:, k, :], PS[6 + k % 2][:, :].rearrange("p (h n) -> p h n", h=HEADS),
                                        AX.X, ALU.max).then_inc(a_r, 1)
                    if k > 0:
                        vec.wait_ge(a_r, 2 + j * G + k)
                        if k > 1:
                            lc.wait()
                        m = mx[:, bass.ds(offs[k - 1], HEADS)]
                        lc.inc(v.tensor_tensor(m, m, red[:, k - 1, :], ALU.max))
                lc.wait()

            vec.sem_inc(s_ye, 2)
            vec.sem_inc(a_r, 2)
            a_front(0, 0)
            with v.Fori(0, EXPERTS) as e:
                with v.Fori(0, CH) as c:
                    i = e * CH + c
                    a_front(i * 2 + 1, 1)
                    a_back(i * 2, 0)
                    a_front(i * 2 + 2, 0)
                    a_back(i * 2 + 1, 1)
                    add_bias(e, c)
            with v.Fori(EXPERTS * CH, RT // 2 - 1) as i:
                a_front(i * 2 + 1, 1)
                a_back(i * 2, 0)
                a_front(i * 2 + 2, 0)
                a_back(i * 2 + 1, 1)
            a_front(RT - 1, 1)
            a_back(RT - 2, 0)
            a_back(RT - 1, 1)

            ch.step(v.tensor_copy(v8[:, :, h4], adst[:, :, :]))
            ch.step(v.tensor_tensor(r8[:, :, h4], mxv[:, :, h4], adst[:, :, :], ALU.add))
            ch.step(v.scalar_tensor_tensor(v8[:, :, 4:8], r8[:, :, h4], 0.2, r8[:, :, h4], ALU.mult, ALU.max))
            adpv = adp[:, :].rearrange("p (t s) -> p t s", s=SEL)
            ch.step(v.tensor_copy(adpv[:, :, 0:8], v8[:, :, :]))
            ch.step(v.tensor_tensor(r8[:, :, :], v8[:, :, :], adpv[:, :, 0:8], ALU.subtract))
            ch.step(v.tensor_copy(adpv[:, :, 8:16], r8[:, :, :]))
            ch.step(v.tensor_tensor(r8[:, :, :], r8[:, :, :], adpv[:, :, 8:16], ALU.subtract))
            v.tensor_copy(adpv[:, :, 16:24], r8[:, :, :]).then_inc(s_adp, 1)
            ch.step(v.tensor_tensor(w0[:, :, h4], tg[:, :, HE:REC], adst[:, :, :], ALU.add))
            ch.step(v.scalar_tensor_tensor(w1[:, :, h4], w0[:, :, h4], 0.2, w0[:, :, h4], ALU.mult, ALU.max))
            v.tensor_tensor(w1[:, :, h4], w1[:, :, h4], v8[:, :, 4:8], ALU.subtract).then_inc(s_ex, 1)
            vec.wait_ge(s_sx, 1)
            acc2v = acc2[:, :].rearrange("p (t s) -> p t s", s=SEL)
            ch.step(v.tensor_tensor(he(acc2v[:, :, 0:HE]), he(tg[:, :, 0:HE]), hb(acc2v[:, :, HE:REC]), ALU.mult))

            vec.sem_inc(b_a, 1)

            def b_hot(j, h):
                one_hots(g2, j, SB[:, h, :, :]).then_inc(b_s, 1)

            def b_mid(j):
                lc = Counter(vec, b_c, base=j * 4)
                vec.wait_ge(b_sc, 1 + j + 1)
                lc.step(v.tensor_tensor(q8[:, :, :], ssel[:, :, 0:8], ssel[:, :, 8:16], ALU.add))
                lc.step(v.tensor_tensor(q8[:, :, :], q8[:, :, :], ssel[:, :, 16:24], ALU.add))
                rec = R[:, bass.ds(j * (G * REC), G * REC)].rearrange("p (k r) -> p k r", k=G)
                lc.step(v.tensor_tensor(ee[:, 0, :, :], rec[:, :, HE:REC], q8[:, :, h4], ALU.add))
                lc.step(v.scalar_tensor_tensor(ee[:, 1, :, :], ee[:, 0, :, :], 0.2, ee[:, 0, :, :], ALU.mult, ALU.max))
                v.tensor_tensor(ee[:, 2, :, :], ee[:, 1, :, :], q8[:, :, 4:8], ALU.subtract).then_inc(b_e, 1)

            def b_pay(j):
                rec = R[:, bass.ds(j * (G * REC), G * REC)].rearrange("p (k r) -> p k r", k=G)
                vec.wait_ge(b_x, j + 1)
                v.tensor_tensor(pay[:, :, 0:HE].rearrange("p k (h e) -> p k h e", h=HEADS),
                                rec[:, :, 0:HE].rearrange("p k (h e) -> p k h e", h=HEADS),
                                pay[:, :, HE:REC].unsqueeze(3).to_broadcast([P, G, HEADS, EXPERTS]),
                                ALU.mult).then_inc(b_p, 1)

            def b_add(j):
                offs = bins(g2, j, NBIN * SEL)
                lc = Counter(vec, b_d, base=j * (G - 1))
                vec.wait_ge(b_o, j + 1)
                for k in range(G):
                    a = acc2[:, bass.ds(offs[k], REC)]
                    ins = v.tensor_tensor(a, a, PS[3][:, k * REC:(k + 1) * REC], ALU.add)
                    if k < G - 1:
                        lc.step(ins)
                    else:
                        ins.then_inc(b_a, 1)
                        vec.wait_ge(b_a, 1 + j + 1)

            b_hot(0, 0)
            b_mid(0)
            b_hot(1, 1)
            b_pay(0)
            with v.Fori(0, RT // 2 - 1) as i:
                for h in (1, 0):
                    j = i * 2 + 2 - h
                    b_mid(j)
                    vec.wait_ge(b_o, j)
                    b_hot(j + 1, 1 - h)
                    b_add(j - 1)
                    b_pay(j)
            b_mid(RT - 1)
            b_add(RT - 2)
            b_pay(RT - 1)
            b_add(RT - 1)

            c16 = lambda a: a.unsqueeze(2).to_broadcast([P, NBP, HE])
            c4 = lambda a: a.unsqueeze(2).to_broadcast([P, NBP, EXPERTS])
            o0, o1 = one[0][:, :], one[1][:, :]
            ch.step(v.tensor_scalar(r8[:, :, h4], acc2v[:, :, HE:REC], 1e-16, None, ALU.add))
            ch.step(v.reciprocal(r8[:, :, 4:8], r8[:, :, h4]))
            ch.step(v.tensor_tensor(he(w0), he(acc2v[:, :, 0:HE]), hb(r8[:, :, 4:8]), ALU.mult))
            ch.step(v.tensor_tensor(w0, w0, bc(2), ALU.add))
            ch.step(v.reduce_sum(o0, w0, axis=AX.X))
            ch.step(v.tensor_scalar(o0, o0, 1.0 / HE, None, ALU.mult))
            ch.step(v.tensor_tensor(w0, w0, c16(o0), ALU.subtract))
            ch.step(v.tensor_tensor(w1, w0, w0, ALU.mult))
            ch.step(v.reduce_sum(o0, w1, axis=AX.X))
            v.tensor_scalar(o0, o0, 1.0 / HE, LN_EPS, ALU.mult, ALU.add).then_inc(s_ex, 1)
            vec.wait_ge(s_sx, 2)
            ch.step(v.reciprocal(o0, o1))
            ch.step(v.tensor_tensor(w0, w0, c16(o0), ALU.mult))
            ch.step(v.tensor_tensor(w0, w0, bc(3), ALU.mult))
            ch.step(v.tensor_tensor(w0, w0, bc(4), ALU.add))
            ch.step(v.reduce_sum(sc[0][:, :, :], w0.rearrange("p t (h e) -> p t e h", h=HEADS), axis=AX.X))
            ch.step(v.tensor_scalar(sc[0][:, :, :], sc[0][:, :, :], 1.0 / HEADS, None, ALU.mult))
            ch.step(v.tensor_reduce(o0, sc[0][:, :, :], AX.X, ALU.max))
            v.tensor_tensor(sc[2][:, :, :], sc[0][:, :, :], c4(o0), ALU.subtract).then_inc(s_ex, 1)
            rank, cmpv = w0[:, :, 0:EXPERTS], w1
            n = 0
            for e in range(EXPERTS):
                for j in range(EXPERTS):
                    if j != e:
                        ch.inc(v.tensor_tensor(cmpv[:, :, n:n + 1], sc[0][:, :, j:j + 1], sc[0][:, :, e:e + 1],
                                               ALU.is_ge if j < e else ALU.is_gt))
                        n += 1
            ch.wait()
            ch.step(v.reduce_sum(rank, w1[:, :, 0:12].rearrange("p t (e j) -> p t e j", e=EXPERTS), axis=AX.X))
            vec.wait_ge(s_sx, 3)
            ch.step(v.scalar_tensor_tensor(sc[2][:, :, :], rank, 2.0, sc[1][:, :, :], ALU.is_lt, ALU.mult))
            ch.step(v.reduce_sum(o0, sc[2][:, :, :], axis=AX.X))
            ch.step(v.reciprocal(o1, o0))
            ch.step(v.tensor_tensor(gate[:, :].rearrange("p (t e) -> p t e", e=EXPERTS), sc[2][:, :, :], c4(o1), ALU.mult))

            vec.sem_inc(f_o, U)

            def final(i, us, base):
                lc = Counter(vec, f_c, base=base)
                for u in us:
                    vec.wait_ge(f_in[u], (i + 1) * 32)
                    vec.wait_ge(f_free, i * U + u + 1)
                for e in range(EXPERTS):
                    for u in us:
                        other = x2_in[:, u, :] if e == 0 else o_sb[:, u, :]
                        ins = v.scalar_tensor_tensor(o_sb[:, u, :], y_in[:, u, e, :],
                                                     gate[:, bass.ds((i * U + u) * EXPERTS + e, 1)], other,
                                                     ALU.mult, ALU.add)
                        if e < EXPERTS - 1:
                            lc.inc(ins)
                        else:
                            ins.then_inc(f_o, 1)
                    lc.wait()

            with v.Fori(0, STEPS - 1) as i:
                final(i, range(U), i * (EXPERTS - 1) * U)
            final(STEPS - 1, [0], (STEPS - 1) * (EXPERTS - 1) * U)


_INS = ['x', 'src', 'dst', 'L0_gnn_W1', 'L0_gnn_b1', 'L0_gnn_W2', 'L0_gnn_b2', 'L0_ffn_W_gat',
        'L0_ffn_att_src', 'L0_ffn_att_dst', 'L0_ffn_b_gat', 'L0_ffn_ln_gamma', 'L0_ffn_ln_beta',
        'L0_ffn_W1', 'L0_ffn_b1', 'L0_ffn_W2', 'L0_ffn_b2', 'L0_ffn_edge_index']


def kernel(**inputs):
    import numpy as _np
    import concourse.bacc as _bacc
    from concourse import mybir as _mybir
    from concourse.bass_utils import run_bass_kernel_spmd as _run

    nc = _bacc.Bacc("TRN2", target_bir_lowering=False, num_devices=1)
    arrays, args = {}, []
    for name in _INS:
        a = _np.ascontiguousarray(inputs[name])
        arrays[f"in_{name}_dram"] = a
        args.append(nc.dram_tensor(f"in_{name}_dram", a.shape, _mybir.dt.from_np(a.dtype), kind="ExternalInput").ap())
    args.append(nc.dram_tensor("out_0_dram", (N, D), _mybir.dt.float32, kind="ExternalOutput").ap())
    build(nc, *args)
    r = _run(nc, [arrays], core_ids=[0])
    return r.results[0]["out_0_dram"]
```

```python
import numpy as np
import concourse.bass as bass
from concourse import mybir
from contextlib import ExitStack

F32, I32, F16, BF16 = mybir.dt.float32, mybir.dt.int32, mybir.dt.float16, mybir.dt.bfloat16
U16, I16 = mybir.dt.uint16, mybir.dt.int16
ALU = mybir.AluOpType
ACT = mybir.ActivationFunctionType
AX = mybir.AxisListType

P = 128
N = 6250
D = 256
NBIN = -(-N // P)
LAST = N - (NBIN - 1) * P
U = 4
NBP = -(-NBIN // U) * U
STEPS = NBP // U
ROWS = NBP * P
EXPERTS, HEADS, HID = 4, 4, 512
HE = HEADS * EXPERTS
REC = HE + HEADS
SEL = 24
G = 8
LN_EPS = 1e-5
ZR = 3 * HEADS * G + 3 * G + 2
PEN = float(2.0 ** 110)
KC = D // P
HC = HID // P


def tiles_bound(edges):
    most = (edges + NBIN * (P - 1)) // P
    return -(-most // (2 * G)) * 2 * G


class Counter:

    def __init__(self, eng, sem, base=0):
        self.eng, self.sem, self.base, self.n = eng, sem, base, 0

    def inc(self, ins):
        ins.then_inc(self.sem, 1)
        self.n += 1

    def wait(self):
        self.eng.wait_ge(self.sem, self.base + self.n)

    def step(self, ins):
        self.inc(ins)
        self.wait()


class Graph:
    def __init__(self, name, edges, src, dst, parts, with_degree, row_stride):
        self.name, self.src, self.dst = name, src, dst
        self.EP, self.T = parts, edges // parts
        self.NT = tiles_bound(edges)
        self.with_degree, self.row_stride = with_degree, row_stride
        w = -(-self.NT // 3)
        w += w % 2
        self.chunks = [(c * w, min(w, self.NT - c * w)) for c in range(3)]


def build(nc, x, src, dst, gW1, gb1, gW2, gb2, W_gat, att_src, att_dst, b_gat, ln_g, ln_b,
          W1, b1, W2, b2, edge_index, out):
    E1, E2 = src.shape[0], edge_index.shape[1]
    e1_parts = max(p for p in range(1, P + 1) if E1 % p == 0 and (E1 // p) % 4 == 0)
    g1 = Graph("gcn", E1, src, dst, e1_parts, True, D)
    g2 = Graph("gat", E2, edge_index[0, :], edge_index[1, :], P, False, SEL)
    TMAX = 1088
    assert max(g1.NT, g2.NT, g1.T, g2.T) <= TMAX and g2.T % 4 == 0

    def dram(name, shape, dt):
        return nc.dram_tensor(name, shape, dt, kind="Internal").ap()

    G1 = dram("gcn_table_1", (ROWS, D), F32)
    G2 = dram("gcn_table_2", (ROWS, D), F32)
    X2 = dram("x_after_gcn", (ROWS, D), F32)
    AT = dram("ffn_in_t", (KC * P, ROWS), F32)
    TR = dram("gat_table", (ROWS, REC), F32)
    Y = dram("expert_out", (ROWS, EXPERTS * D), F32)

    with ExitStack() as ctx:
        def sb(name, shape, dt):
            return ctx.enter_context(nc.sbuf_tensor(name, shape, dt))

        def sem(name):
            return ctx.enter_context(nc.semaphore(name))

        ACCF = NBP * D
        R = sb("big", [P, max(ACCF + 9 * TMAX, g2.NT * REC)], F32)
        acc = R[:, 0:ACCF]
        gat_rows = R[:, 0:g2.NT * REC].rearrange("p (t r) -> p t r", r=REC)

        def arrays(base):
            def tmp(k, dt=F32):
                a = R[:, base + k * TMAX:base + (k + 1) * TMAX]
                return a if dt == F32 else a.bitcast(dt)
            return tmp

        assert 9 * TMAX <= ACCF and g2.EP == P
        g1.tmp, g2.tmp = arrays(ACCF), arrays(0)
        zd = R[:, g2.NT * REC:g2.NT * REC + g2.NT * 3 // 2].bitcast(BF16).rearrange("p (t q) -> p t q", q=3)
        assert g2.NT * REC >= ACCF + 6 * TMAX and g2.NT * REC + g2.NT * 3 // 2 <= ACCF + 9 * TMAX

        UN = sb("phase", [P, 6144], F32)
        def onehot_slots(base, n):
            hi = base[:, 0:2 * TMAX].bitcast(F16).rearrange("p (k t) -> p k t", k=4)
            lo = base[:, 2 * TMAX:2 * TMAX + 2 * n * P].bitcast(F16).rearrange("p (k j n) -> p k j n", k=4, j=n)
            return hi, lo

        g1.oh_hi, g1.oh_lo = onehot_slots(UN, 4)
        oh_bin = UN[:, 3328:3328 + 4 * 64 // 2].bitcast(F16).rearrange("p (k n) -> p k n", k=4)
        msg = UN[:, 0:G * D].rearrange("p (k n) -> p k n", k=G)
        SC, SB = [UN[:, at:at + n * G * P].rearrange("p (h k n) -> p h k n", h=n, k=G)
                  for at, n in ((G * D, 2), (0, 4))]
        SB16 = UN[:, 0:4 * G * P].bitcast(BF16).rearrange("p (h k n w) -> p h k n w", h=4, k=G, w=2)
        LV = UN[:, 4096:6144].bitcast(BF16).rearrange("p (k h n) -> p k h n", k=G, h=HEADS)
        at_in = UN[:, 0:KC * 512].rearrange("p (k n) -> p k n", k=KC)
        hid = UN[:, 1024:1024 + HC * 512].rearrange("p (c n) -> p c n", c=HC)
        y_sb = UN[:, 3072:3072 + 4 * D].rearrange("p (s n) -> p s n", s=4)
        y_in = UN[:, 0:U * EXPERTS * D].rearrange("p (u e n) -> p u e n", u=U, e=EXPERTS)
        x2_in = UN[:, 4096:4096 + U * D].rearrange("p (u n) -> p u n", u=U)
        o_sb = UN[:, 5120:5120 + U * D].rearrange("p (u n) -> p u n", u=U)

        for g in (g1, g2):
            g.H = sb(g.name + "_hist_sb", [P, 64], F32)
            g.bn = sb(g.name + "_bins", [P, 6, 64], F32)
            g.at7 = 0 if g is g1 else 128
            g.idx = sb(g.name + "_idx", [P, g.NT], I32)
            g.dlo = sb(g.name + "_dlo", [P, g.NT], F16)
            g.row = sb(g.name + "_row", [1, g.NT], I16)
        stage = sb("stage", [P, 2, G], I32)
        ring = sb("ring", [P, 2, G * REC], F32)
        ST = sb("sel_t", [P, G, P], BF16)
        Z = sb("z", [P, 2, P], BF16)
        VT = sb("z_t", [P, 2, P], BF16)
        LC = sb("mask_factors", [P, 4, G], F32)
        LM = sb("mask_matrix", [P, G, P], BF16)
        tiles = sb("node_tiles", [P, 4 * U * D], F32)
        xt, xn, x2t = [tiles[:, k * U * D:(k + 1) * U * D].rearrange("p (u n) -> p u n", u=U) for k in range(3)]
        aT = tiles[:, 3 * U * D:4 * U * D].rearrange("p (u k n) -> p u k n", u=U, k=KC)
        g2.oh_hi, g2.oh_lo = onehot_slots(tiles[:, U * D:4 * U * D], 3)
        big = tiles[:, 0:2 * NBP * HE].rearrange("p (j t n) -> p j t n", j=2, t=NBP)
        v8 = tiles[:, 2 * NBP * HE:2 * NBP * HE + NBP * 8].rearrange("p (t n) -> p t n", n=8)
        r8 = tiles[:, 2 * NBP * HE + NBP * 8:2 * NBP * HE + NBP * 16].rearrange("p (t n) -> p t n", n=8)
        wg = [sb(f"gcn_w{i}", [P, KC, D], F32) for i in range(2)]
        wgat = sb("gat_w", [P, KC, HE], F32)
        w1s = sb("ffn_w1", [P, KC, HID], F32)
        w2s = sb("ffn_w2", [P, HC, D], F32)
        b1s = sb("ffn_b1", [P, EXPERTS * HC], F32)
        b2s = sb("ffn_b2", [P, EXPERTS * D], F32)
        bias = [sb(f"gcn_b{i}", [P, D], F32) for i in range(2)]
        vecs = sb("gat_vecs", [P, 5, HE], F32)
        st6 = sb("bn", [P, U, 6], F32)
        mv = sb("mean_var", [P, U, 4], F32)
        dinv = sb("dinv", [P, NBP], F32)
        iota16 = sb("iota16", [P, TMAX], F16)
        iota32 = sb("iota32", [P, P], F32)
        iobin = sb("iobin", [P, 64], F32)
        ident = sb("ident", [P, P], F32)
        ident16 = sb("ident16", [P, P], BF16)
        ones = sb("ones", [P, P], F32)
        onesf16 = sb("onesf16", [P, 1], F16)
        zero16 = sb("zero16", [P, 512], F16)
        tri = sb("tri", [P, P], F32)
        bni = sb("bin_small_i", [P, 64], I32)
        tg = sb("gat_rec", [P, NBP, REC], F32)
        adst = sb("a_dst", [P, NBP, HEADS], F32)
        sc = [sb(f"score{k}", [P, NBP, EXPERTS], F32) for k in range(3)]
        one = [sb(f"one{k}", [P, NBP], F32) for k in range(2)]
        mx = sb("max_src", [P, NBP * SEL], F32)
        adp = sb("ad_parts", [P, NBP * SEL], BF16)
        acc2 = sb("gat_acc", [P, NBP * SEL], F32)
        gate = sb("gate", [P, NBP * EXPERTS], F32)
        red = sb("red", [P, G, HEADS], F32)
        asr = sb("as_res", [P, 2, G, HEADS], F32)
        ssel = sb("sel_vals", [P, G, SEL], F32)
        q8 = sb("q8", [P, G, 8], F32)
        ee = sb("ee", [P, 3, G, HEADS], F32)
        pay = sb("payload", [P, 2, G, REC], F32)

        PS = [ctx.enter_context(nc.psum_tensor(f"ps{k}", [P, 512], F32)) for k in range(8)]

        s_const = sem("s_const")
        s_alone = sem("s_alone")
        s_w = sem("s_weights")
        s_vc = sem("s_vec_chain")
        for g in (g1, g2):
            g.s_in = sem(g.name + "_in")
            g.s_hist = sem(g.name + "_hist")
            g.s_scan = sem(g.name + "_scan")
            g.s_oh = sem(g.name + "_onehots")
            g.s_ab = sem(g.name + "_payloads")
            g.s_pl = sem(g.name + "_placed")
            g.s_done = sem(g.name + "_placed_all")
            g.s_cmp = sem(g.name + "_cmp")
            g.s_row = sem(g.name + "_rowps")
            g.s_ready = sem(g.name + "_ready")
        s_pre = sem("s_prefix")
        s_deg = sem("s_deg")
        s_degq = sem("s_degq")
        ph = []
        for k in range(3):
            names = ["dv", "xn", "tp", "at", "mm", "ev"]
            names += {0: ["var", "sq", "st"], 1: ["st"],
                      2: ["var", "sq", "x2", "free"]}[k]
            s = {n: sem(f"p{k}_{n}") for n in names}
            if k != 1:
                s["x"] = [sem(f"p{k}_xin{u}") for u in range(U)]
            ph.append(s)
        s_ss = [[sem(f"s_st{a}{u}") for u in range(U)] for a in range(2)]
        cv = []
        for k in range(2):
            cv.append(dict(g=[sem(f"c{k}_gath{j}") for j in range(G)],
                           ix=sem(f"c{k}_ix"),
                           s=sem(f"c{k}_sel"),
                           used=sem(f"c{k}_used"),
                           add=sem(f"c{k}_add")))
        s_ix = sem("s_ix")
        s_rec, s_recst = sem("s_rec"), sem("s_recst")
        s_gr = [sem(f"s_gr{h}") for h in range(2)]
        s_pc = sem("s_pc")
        s_fw, s_ai, s_hm, s_hg, s_ym, s_ye = [sem("e_" + n) for n in ("w", "in", "hm", "hg", "ym", "ye")]
        s_ys = [sem(f"e_ys{j}") for j in range(4)]
        a_z, a_t, a_v, a_m, a_r, a_c, a_d = [sem("a_" + n) for n in ("z", "t", "v", "m", "r", "c", "d")]
        s_adp = sem("s_adp")
        b_s, b_t, b_st, b_sel, b_sc, b_e, b_x, b_p, b_o, b_a, b_c, b_d = [sem("b_" + n) for n in
            ("s", "t", "st", "sel", "sc", "e", "x", "p", "o", "a", "c", "d")]
        s_ex, s_sx, s_gate = sem("s_ex"), sem("s_sx"), sem("s_gate")
        f_in = [sem(f"f_in{u}") for u in range(U)]
        f_c, f_o = sem("f_c"), sem("f_o")
        s_zd, s_lm = sem("s_zd"), sem("s_lm")
        f_st = [sem(f"f_st{u}") for u in range(U)]

        RT = g2.NT // G
        NCONST, NLOADS = 11, 12
        CH = ROWS // 512

        NG = g1.NT // G
        W = -(-g2.T // (2 * NG))
        LEAD = 2
        PLACE_AT = [k * G // W for k in range(W)]
        assert W <= G and NG % 4 == 0
        parts2 = [(0, NG * W), (NG * W, g2.T)]
        assert all(at % 4 == 0 for at, _ in parts2) and NG * W + (NG - 4) * W + LEAD <= g2.T

        def groups(eng, part, group):
            first, last = parts2[part]
            with eng.Fori(0, NG // 4 - 1) as i:
                for h in range(4):
                    group(i * 4 + h, h, i * (4 * W) + (first + h * W), None)
            for h in range(4):
                j = NG - 4 + h
                group(j, h, first + j * W, last)

        def alone(eng):
            eng.sem_inc(s_alone, 1)

        block = ctx.enter_context(nc.Block())

        @block.sync
        def _(sp):
            def load_edges(g):
                sp.dma_start(g.tmp(0, I32)[0:g.EP, 0:g.T], g.src.rearrange("(p t) -> p t", t=g.T)).then_inc(g.s_in, 16)
                sp.dma_start(g.tmp(1, I32)[0:g.EP, 0:g.T], g.dst.rearrange("(p t) -> p t", t=g.T)).then_inc(g.s_in, 16)

            load_edges(g1)
            load_edges(g2)
            for k, w in enumerate((gW1, gW2)):
                sp.dma_start(wg[k][:, :, :], w.rearrange("(k p) n -> p k n", p=P)).then_inc(s_w, 16)
            sp.dma_start(wgat[:, :, :], W_gat.rearrange("(k p) n -> p k n", p=P)).then_inc(s_w, 16)
            for k, b in enumerate((gb1, gb2)):
                sp.dma_start(bias[k][:, :], b.partition_broadcast(P)).then_inc(s_w, 16)
            for k, b in enumerate((att_src.rearrange("a b -> (a b)"), att_dst.rearrange("a b -> (a b)"),
                                   b_gat, ln_g, ln_b)):
                sp.dma_start(vecs[:, k, :], b.partition_broadcast(P)).then_inc(s_w, 16)
            sp.dma_start(b2s[:, :], b2.rearrange("e n -> (e n)").partition_broadcast(P)).then_inc(s_w, 16)
            with nc.allow_non_contiguous_dma(reason="bias as a column per hidden chunk"):
                sp.dma_start(b1s[:, :], b1.rearrange("e (c p) -> p (e c)", p=P)).then_inc(s_w, 16)

            def load_x(s, i, tail):
                for u in range(U):
                    sp.wait_ge(s["xn"], i * U + u + 1)
                    rows = LAST if tail and u == 0 else P
                    view = x[(NBIN - 1) * P:N, :] if tail and u == 0 else (
                        x[0:P, :] if tail else x[bass.ds((i * U + u) * P, P), :])
                    sp.dma_start(xt[0:rows, u, :], view).then_inc(s["x"][u], 16)

            with sp.Fori(0, STEPS - 1) as i:
                load_x(ph[0], i, False)
            load_x(ph[0], STEPS - 1, True)
            s = ph[2]
            sp.sem_inc(s["free"], U)
            with sp.Fori(0, STEPS) as i:
                for u in range(U):
                    sp.wait_ge(s["x2"], U + i * U + u + 1)
                    sp.dma_start(X2[bass.ds((i * U + u) * P, P), :], x2t[:, u, :]).then_inc(s_ss[0][u], 16)
                    sp.wait_ge(s["at"], 2 + i * U + u + 1)
                    alone(sp)
                    sp.dma_start(AT[:, bass.ds((i * U + u) * P, P)].rearrange("(k p) n -> p k n", p=P),
                                 aT[:, u, :, :]).then_inc(s_ss[1][u], 16)
                for u in range(U):
                    sp.wait_ge(s_ss[0][u], (i + 1) * 16)
                    sp.wait_ge(s_ss[1][u], (i + 1) * 16)
                    sp.sem_inc(s["free"], 1)
            sp.wait_ge(s_rec, 1)
            sp.dma_start(TR.rearrange("(t p) r -> p t r", p=P), tg[:, :, :]).then_inc(s_recst, 16)

            for j in range(4):
                sp.dma_start(y_sb[:, j, :], b2[0, :].partition_broadcast(P)).then_inc(s_ys[j], 16)
            with sp.Fori(0, EXPERTS) as e:
                sp.wait_ge(s_ym, e * (CH * 4) + 1)
                sp.dma_start(w1s[:, :, :], W1[bass.ds(e, 1), :, :].rearrange("o (k p) n -> p (o k) n", p=P)).then_inc(s_fw, 16)
                sp.dma_start(w2s[:, :, :], W2[bass.ds(e, 1), :, :].rearrange("o (k p) n -> p (o k) n", p=P)).then_inc(s_fw, 16)
                with sp.Fori(0, CH) as c:
                    sp.wait_ge(s_hm, (e * CH + c + 1) * HC)
                    sp.dma_start(at_in[:, :, :], AT[:, bass.ds(c * 512, 512)]
                                 .rearrange("(k p) n -> p k n", p=P)).then_inc(s_ai, 16)

            sp.wait_ge(b_a, 2 + RT)
            for j in range(4):
                sp.wait_ge(s_ys[j], 16 * (1 + EXPERTS * CH))

            def final_in(i, us):
                for u in us:
                    sp.wait_ge(f_o, i * U + u + 1)
                    sp.dma_start(x2_in[:, u, :], X2[bass.ds((i * U + u) * P, P), :]).then_inc(f_in[u], 16)
                    sp.dma_start(y_in[:, u, :, :], Y[bass.ds((i * U + u) * P, P), :]
                                 .rearrange("p (e n) -> p e n", e=EXPERTS)).then_inc(f_in[u], 16)

            with sp.Fori(0, STEPS - 1) as i:
                final_in(i, range(U))
            final_in(STEPS - 1, [0])

        @block.gpsimd
        def _(pool):
            pool.iota(iota16[:, :], [[1, TMAX]], base=0, channel_multiplier=0,
                      allow_small_or_imprecise_dtypes=True).then_inc(s_const, 1)
            pool.iota(iota32[:, :], [[1, P]], base=0, channel_multiplier=0,
                      allow_small_or_imprecise_dtypes=True).then_inc(s_const, 1)
            pool.iota(iobin[:, :], [[1, 64]], base=0, channel_multiplier=0,
                      allow_small_or_imprecise_dtypes=True).then_inc(s_const, 1)
            pool.memset(ones[:, :], 1.0).then_inc(s_const, 1)
            pool.memset(onesf16[:, :], 1.0).then_inc(s_const, 1)
            pool.memset(zero16[:, :], 0.0).then_inc(s_const, 1)
            pool.memset(Z[:, :, :], 1.0).then_inc(s_const, 1)
            pool.memset(xt[:, :, :], 0.0).then_inc(s_const, 1)
            pool.memset(dinv[:, :], 1.0).then_inc(s_const, 1)
            pool.wait_ge(s_const, 9)
            pool.affine_select(out=ident[:, :], in_=ones[:, :], compare_op=ALU.is_equal, fill=0.0,
                               base=0, pattern=[[-1, P]], channel_multiplier=1).then_inc(s_const, 1)
            pool.affine_select(out=tri[:, :], in_=ones[:, :], compare_op=ALU.is_gt, fill=0.0,
                               base=0, pattern=[[1, P]], channel_multiplier=-1).then_inc(s_const, 1)

            def conv(c, g, table, s):
                pool.wait_ge(s["st"], 16 * STEPS)
                with pool.Fori(0, g.NT // (2 * G)) as i:
                    for h in range(2):
                        j = i * 2 + h
                        pool.wait_ge(c["used"], j * G + 1)
                        pool.tensor_copy(stage[:, h, :], g.idx[:, bass.ds(j * G, G)]).then_inc(c["ix"], 1)
                        pool.wait_ge(c["ix"], j + 1)
                        for k in range(G):
                            pool.wait_ge(c["used"], j * G + k + 1)
                            alone(pool)
                            pool.indirect_dma_start(
                                out=msg[:, k, :], out_offset=None, in_=table[:, :],
                                in_offset=bass.IndirectOffsetOnAxis(ap=stage[:, h, k:k + 1], axis=0),
                            ).then_inc(c["g"][k], 16)

            pool.wait_ge(g1.s_ready, 1)
            conv(cv[0], g1, G1, ph[0])
            conv(cv[1], g1, G2, ph[1])

            def load_x(s, i, tail):
                for u in range(U):
                    pool.wait_ge(s["x2"], i * U + u + 1)
                    rows = LAST if tail and u == 0 else P
                    view = x[(NBIN - 1) * P:N, :] if tail and u == 0 else (
                        x[0:P, :] if tail else x[bass.ds((i * U + u) * P, P), :])
                    pool.dma_start(xt[0:rows, u, :], view).then_inc(s["x"][u], 16)

            with pool.Fori(0, STEPS - 1) as i:
                load_x(ph[2], i, False)
            load_x(ph[2], STEPS - 1, True)

            pool.memset(LV[:, :, :, :], 0.0).then_inc(s_lm, 1)
            pool.memset(LC[:, :, :], 0.0).then_inc(s_lm, 1)
            for p in range(3):
                pool.wait_ge(s_lm, 2 + p)
                pool.affine_select(out=LV[:, :, :, :], in_=LV[:, :, :, :], compare_op=ALU.not_equal, fill=1.0,
                                   base=-4 * p, pattern=[[-12, G], [-1, HEADS], [0, P]], channel_multiplier=1).then_inc(s_lm, 1)
            for n, (col, row, step, fill) in enumerate(((0, 96, 3, 2.0 * PEN), (1, 97, 3, -128.0 * PEN), (1, 98, 3, -PEN),
                                                        (2, 120, 0, -128.0 * PEN), (3, 121, 0, -PEN))):
                pool.wait_ge(s_lm, 5 + n)
                pool.affine_select(out=LC[:, col, :], in_=LC[:, col, :], compare_op=ALU.not_equal, fill=fill,
                                   base=-row, pattern=[[-step, G]], channel_multiplier=1).then_inc(s_lm, 1)

            pool.wait_ge(s_recst, 16)
            pool.wait_ge(g2.s_ready, 1)

            def gather(j, h):
                pool.tensor_copy(stage[:, h, :], g2.idx[:, bass.ds(j * G, G)]).then_inc(s_ix, 1)
                pool.wait_ge(s_ix, j + 1)
                alone(pool)
                for k in range(G):
                    pool.indirect_dma_start(
                        out=ring[:, h, k * REC:(k + 1) * REC], out_offset=None, in_=TR[:, :],
                        in_offset=bass.IndirectOffsetOnAxis(ap=stage[:, h, k:k + 1], axis=0),
                    ).then_inc(s_gr[h], 16)

            def place(j, h):
                pool.wait_ge(s_gr[h], (j - h + 2) * (G * 8))
                pool.tensor_copy(R[:, bass.ds(j * (G * REC), G * REC)], ring[:, h, :]).then_inc(s_pc, 1)
                pool.wait_ge(s_pc, j + 1)

            gather(0, 0)
            with pool.Fori(0, RT // 2 - 1) as i:
                gather(i * 2 + 1, 1)
                place(i * 2, 0)
                gather(i * 2 + 2, 0)
                place(i * 2 + 1, 1)
            gather(RT - 1, 1)
            place(RT - 2, 0)
            place(RT - 1, 1)

        @block.tensor
        def _(pe):
            mm = nc.tensor.matmul
            pe.wait_ge(s_const, NCONST)
            pe.wait_ge(s_w, 16 * NLOADS)

            def products(g):
                return [(3 * j + c, at, w, j) for j in range(2) for c, (at, w) in enumerate(g.chunks)]

            def edge(g, start, stop):
                for b, _, w, _ in products(g):
                    last = mm(PS[b][:, 0:w], zero16[:, 0:P], zero16[:, 0:w], start=start, stop=stop)
                if g.with_degree:
                    last = mm(PS[6][:, 0:NBIN], zero16[:, 0:P], zero16[:, 0:NBIN], start=start, stop=stop)
                return last

            def prefixes():
                for g in (g1, g2):
                    pe.wait_ge(g.s_hist, NBIN)
                    for at, m in ((0, ones), (64, tri)):
                        last = mm(PS[7][:, g.at7 + at:g.at7 + at + NBIN], m[0:g.EP, :], g.H[0:g.EP, 0:NBIN],
                                  start=True, stop=True, skip_group_check=True)
                last.then_inc(s_pre, 1)

            def sort_open(g):
                pe.sem_inc(g.s_pl, 4)
                edge(g, True, False)

            def place(g, col, k):
                pe.wait_ge(g.s_oh, col + 1)
                pe.wait_ge(g.s_ab, (col + 1) * 2)
                for b, at, w, j in products(g):
                    last = mm(PS[b][:, 0:w], g.oh_lo[0:g.EP, k, j, :], g.oh_hi[0:g.EP, k, at:at + w],
                              start=False, stop=False)
                if g.with_degree:
                    last = mm(PS[6][:, 0:NBIN], g.oh_lo[0:g.EP, k, 3, :], oh_bin[0:g.EP, k, 0:NBIN],
                              start=False, stop=False)
                last.then_inc(g.s_pl, 1)

            def sort_close(g):
                edge(g, False, True).then_inc(g.s_done, 1)
                pe.wait_ge(g.s_cmp, 1)
                for c, (at, w) in enumerate(g.chunks):
                    last = mm(PS[c][0:1, 0:w], onesf16[0:NBIN, 0:1], g.oh_hi[0:NBIN, 0, at:at + w],
                              start=True, stop=True)
                last.then_inc(g.s_row, 1)

            def phase(s, w, n, banks):
                slots = len(banks) // 2
                pe.sem_inc(s["tp"], U)
                pe.sem_inc(s["mm"], U)
                with pe.Fori(0, STEPS) as i:
                    for pair in range(0, U, 2):
                        for u in (pair, pair + 1):
                            pe.wait_ge(s["xn"], U + i * U + u + 1)
                            pe.wait_ge(s["at"], i * U + u + 1)
                            for c in range(KC):
                                last = nc.tensor.transpose(PS[banks[u % slots]][:, c * P:(c + 1) * P],
                                                           xn[:, u, c * P:(c + 1) * P], ident[:, :])
                            last.then_inc(s["tp"], 1)
                        for u in (pair, pair + 1):
                            pe.wait_ge(s["at"], slots + i * U + u + 1)
                            pe.wait_ge(s["ev"], i * U + u + 1)
                            for c in range(KC):
                                last = mm(PS[banks[slots + u % slots]][:, 0:n], aT[:, u, c, :], w[:, c, :],
                                          start=c == 0, stop=c == KC - 1)
                            last.then_inc(s["mm"], 1)

            def conv(part):
                c = cv[part]
                pe.sem_inc(c["used"], G)

                def group(j, h, col, end):
                    pe.wait_ge(c["s"], j + 1)
                    for k in range(G):
                        pe.wait_ge(c["g"][k], (j + 1) * 16)
                        pe.wait_ge(c["add"], j * G + k + 1)
                        mm(PS[6 + k % 2][:, 0:D], SC[:, h % 2, k, :], msg[:, k, :], start=True, stop=True).then_inc(c["used"], 1)
                        if k in PLACE_AT:
                            q = PLACE_AT.index(k)
                            if end is None or col + q < end:
                                place(g2, col + q, (h * W + q) % 4)

                groups(pe, part, group)

            prefixes()
            sort_open(g1)
            with pe.Fori(0, g1.T // 4) as i:
                for k in range(4):
                    place(g1, i * 4 + k, k)
            sort_close(g1)
            phase(ph[0], wg[0], D, (0, 1, 2, 3))
            pe.wait_ge(ph[0]["ev"], 2 + NBP)
            sort_open(g2)
            conv(0)
            phase(ph[1], wg[1], D, (6, 7))
            conv(1)
            sort_close(g2)
            phase(ph[2], wgat, HE, (0, 1, 2, 3))

            def a_front(j, h):
                pe.wait_ge(a_z, j + 1)
                pe.wait_ge(a_v, j + 1)
                mm(PS[4 + h][0:ZR, 0:P], Z[:, h, 0:ZR], ident16[:, :], start=True, stop=True).then_inc(a_t, 1)

            def a_back(j, h, banks=(6, 7), front=None, piece=None, odd=1):
                pe.wait_ge(a_v, 2 + j + 1)
                rows = VT[0:ZR, h, :]
                for k in range(G):
                    pe.wait_ge(a_r, j * G + k + 1)
                    out_ = PS[banks[k % len(banks)]]
                    mm(out_[:, :], LM[0:ZR, k, :], rows.unsqueeze(1).to_broadcast([ZR, HEADS, P]), start=True, stop=False)
                    for hd in range(HEADS):
                        last = mm(out_[:, hd * P:(hd + 1) * P], LV[0:ZR, k, hd, :], rows, start=False, stop=hd == HEADS - 1)
                    last.then_inc(a_m, 1)
                    if k == 1 and front is not None:
                        a_front(*front)
                    if piece is not None and k % 2 == odd:
                        piece(k // 2)

            def hidden(n, q):
                if q == 0:
                    pe.wait_ge(s_ai, (n + 1) * 16)
                pe.wait_ge(s_hg, n * HC + q + 1)
                for k in range(KC):
                    last = mm(PS[q % 2][:, :], w1s[:, k, q * P:(q + 1) * P],
                              at_in[:, k, :], start=k == 0, stop=k == KC - 1)
                last.then_inc(s_hm, 1)

            def result(n, j):
                if j == 0:
                    pe.wait_ge(s_hg, 2 + (n + 1) * HC)
                pe.wait_ge(s_ye, n * 4 + j + 1)
                for q in range(HC):
                    last = mm(PS[2 + j % 2][:, 0:D], hid[:, q, j * P:(j + 1) * P], w2s[:, q, :],
                              start=q == 0, stop=q == HC - 1)
                last.then_inc(s_ym, 1)

            assert HC == G // 2 == 4
            pe.sem_inc(s_ym, 1)
            pe.sem_inc(s_hm, HC)
            pe.wait_ge(s_zd, 1)
            pe.wait_ge(ph[2]["ev"], 2 + NBP)
            a_front(0, 0)
            with pe.Fori(0, EXPERTS) as e:
                pe.wait_ge(s_fw, (e + 1) * 32)
                alone(pe)
                with pe.Fori(0, CH) as c:
                    i = e * CH + c
                    a_back(i * 2, 0, front=(i * 2 + 1, 1), piece=lambda q: hidden(i, q), odd=0)
                    a_back(i * 2 + 1, 1, front=(i * 2 + 2, 0), piece=lambda j: result(i, j))
            pe.wait_ge(a_r, 4 + EXPERTS * CH * 2 * G)
            with pe.Fori(EXPERTS * CH, RT // 2 - 1) as i:
                a_back(i * 2, 0, (6, 7, 0, 1), (i * 2 + 1, 1))
                a_back(i * 2 + 1, 1, (6, 7, 0, 1), (i * 2 + 2, 0))
            a_back(RT - 2, 0, (6, 7, 0, 1), (RT - 1, 1))
            a_back(RT - 1, 1, (6, 7, 0, 1))

            row_regs = [pe.alloc_register(f"pe_bin{k}") for k in range(G)]

            def b_trans(j, h):
                for half in range(2):
                    for k in range(4 * half, 4 * half + 4):
                        if k % 4 == 0:
                            pe.wait_ge(b_s, j + 1)
                            pe.wait_ge(b_st, j * 2 + half + 1)
                        last = mm(PS[half][:, (k % 4) * P:(k % 4 + 1) * P], SB16[:, h, k, :, 1], ident16[:, :],
                                  start=True, stop=True, skip_group_check=True)
                    last.then_inc(b_t, 1)

            def b_select(j):
                pe.load(row_regs, g2.row[0:1, bass.ds(j * G, G)])
                offs = [pe.snap(r, min_val=0, max_val=NBIN * SEL) for r in row_regs]
                pe.wait_ge(b_sc, j + 1)
                pe.wait_ge(b_st, 2 + (j + 1) * 2)
                for k in range(G):
                    last = mm(PS[2][:, k * SEL:(k + 1) * SEL], ST[:, k, :], adp[:, bass.ds(offs[k], SEL)],
                              start=True, stop=True, skip_group_check=True)
                last.then_inc(b_sel, 1)

            def b_sum(j, q):
                pe.wait_ge(b_p, j + 1)
                pe.wait_ge(b_a, j + 1)
                for k in range(G):
                    last = mm(PS[3 + q % 2][:, k * REC:(k + 1) * REC], SB[:, q, k, :], pay[:, q % 2, k, :],
                              start=True, stop=True, skip_group_check=True)
                last.then_inc(b_o, 1)

            def b_group(j, q):
                b_trans(j + 1, (q + 1) % 4)
                b_select(j + 1)
                b_sum(j, q)

            pe.wait_ge(s_adp, 1)
            b_trans(0, 0)
            b_select(0)
            with pe.Fori(0, (RT - 1) // 4) as i:
                for q in range(4):
                    b_group(i * 4 + q, q)
            for j in range((RT - 1) // 4 * 4, RT - 1):
                b_group(j, j % 4)
            b_sum(RT - 1, (RT - 1) % 4)

        @block.scalar
        def _(act):
            act.wait_ge(s_const, NCONST)
            copy = lambda o, i: nc.scalar.activation(o, i, ACT.Copy)

            def scale(g, i, k):
                act.wait_ge(g.s_oh, i * 4 + k + 1)
                alone(act)
                for n, val in enumerate((g1.tmp(2), g1.tmp(3))):
                    nc.scalar.activation(g.oh_lo[0:g.EP, k, n, :], g.oh_lo[0:g.EP, k, 2, :], ACT.Copy,
                                         scale=val[0:g.EP, bass.ds(i * 4 + k, 1)]).then_inc(g.s_ab, 1)

            def scale_all(g, first, end):
                with act.Fori(first // 4, end // 4) as i:
                    for k in range(4):
                        scale(g, i, k)

            scale_all(g1, 0, g1.T)
            act.wait_ge(s_deg, 1)
            nc.scalar.activation(one[1][:, 0:NBIN], one[0][:, 0:NBIN], ACT.Sqrt).then_inc(s_degq, 1)

            def phase(k, s, n, table, banks):
                slots = len(banks) // 2
                act.sem_inc(s["at"], slots)
                act.sem_inc(s["ev"], slots)
                with act.Fori(0, STEPS) as i:
                    if k != 1:
                        act.wait_ge(s["var"], i + 1)
                        nc.scalar.activation(mv[:, :, 3], mv[:, :, 2], ACT.Sqrt).then_inc(s["sq"], 1)
                    for pair in range(0, U, 2):
                        for u in (pair, pair + 1):
                            act.wait_ge(s["tp"], U + i * U + u + 1)
                            act.wait_ge(s["mm"], i * U + u + 1)
                            if k == 2:
                                act.wait_ge(s["free"], i * U + u + 1)
                            copy(aT[:, u, :, :], PS[banks[u % slots]][:, 0:D].rearrange("p (k n) -> p k n", k=KC)).then_inc(s["at"], 1)
                        for u in (pair, pair + 1):
                            act.wait_ge(s["mm"], U + i * U + u + 1)
                            alone(act)
                            if k == 2:
                                copy(tg[:, bass.ds(i * U + u, 1), 0:HE],
                                     PS[banks[slots + u % slots]][:, 0:HE].unsqueeze(1)).then_inc(s["ev"], 1)
                            else:
                                nc.scalar.activation(acc[:, bass.ds((i * U + u) * D, D)],
                                                     PS[banks[slots + u % slots]][:, 0:D], ACT.Copy,
                                                     scale=dinv[:, bass.ds(i * U + u, 1)]).then_inc(s["ev"], 1)
                    if table is not None:
                        act.wait_ge(s["ev"], slots + (i + 1) * U)
                        alone(act)
                        act.dma_start(table[bass.ds(i * U * P, U * P), :].rearrange("(u p) n -> p u n", p=P),
                                      acc[:, bass.ds(i * U * D, U * D)].rearrange("p (u n) -> p u n", u=U)).then_inc(s["st"], 16)

            act.wait_ge(g1.s_ready, 1)
            phase(0, ph[0], D, G1, (0, 1, 2, 3))
            scale_all(g2, *parts2[0])
            phase(1, ph[1], D, G2, (6, 7))
            scale_all(g2, *parts2[1])
            phase(2, ph[2], HE, None, (0, 1, 2, 3))

            act.sem_inc(s_hg, 2)

            def gelu(e, c):
                for q in range(HC):
                    act.wait_ge(s_hm, HC + (e * CH + c) * HC + q + 1)
                    alone(act)
                    nc.scalar.activation(hid[:, q, :], PS[q % 2][:, :], ACT.Gelu,
                                         bias=b1s[:, bass.ds(e * HC + q, 1)]).then_inc(s_hg, 1)

            def store_y(e, c):
                for j in range(4):
                    act.wait_ge(s_ye, 2 + (e * CH + c) * 4 + j + 1)
                    act.dma_start(Y[bass.ds((c * 4 + j) * P, P), bass.ds(e * D, D)],
                                  y_sb[:, j, :]).then_inc(s_ys[j], 16)

            def a_rows(j, h):
                act.wait_ge(a_t, j + 1)
                copy(VT[0:ZR, h, :], PS[4 + h][0:ZR, 0:P]).then_inc(a_v, 1)

            act.sem_inc(a_v, 2)
            a_rows(0, 0)
            with act.Fori(0, EXPERTS) as e:
                def pair(c, store):
                    n = e * CH + c
                    a_rows(n * 2 + 1, 1)
                    if store:
                        store_y(e, c - 1)
                    gelu(e, c)
                    a_rows(n * 2 + 2, 0)

                pair(0, False)
                with act.Fori(1, CH) as c:
                    pair(c, True)
                store_y(e, CH - 1)
            with act.Fori(EXPERTS * CH, RT // 2 - 1) as i:
                a_rows(i * 2 + 1, 1)
                a_rows(i * 2 + 2, 0)
            a_rows(RT - 1, 1)

            act.wait_ge(s_ex, 1)
            acc2v = acc2[:, :].rearrange("p (t s) -> p t s", s=SEL)
            nc.scalar.activation(acc2v[:, :, HE:REC], big[:, 1, :, 0:HEADS], ACT.Exp).then_inc(s_sx, 1)
            act.sem_inc(b_st, 2)
            act.sem_inc(b_sc, 1)

            def b_copy(j):
                for half in range(2):
                    act.wait_ge(b_t, j * 2 + half + 1)
                    copy(ST[:, 4 * half:4 * half + 4, :], PS[half][:, :].rearrange("p (k n) -> p k n", k=4)).then_inc(b_st, 1)

            def b_exp(j, h):
                act.wait_ge(b_e, j + 1)
                nc.scalar.activation(pay[:, h, :, HE:REC], ee[:, 2, :, :], ACT.Exp).then_inc(b_x, 1)

            def b_values(j):
                act.wait_ge(b_sel, j + 1)
                copy(ssel[:, :, :], PS[2][:, 0:G * SEL].rearrange("p (k n) -> p k n", k=G)).then_inc(b_sc, 1)

            def b_group(j, h):
                b_exp(j, h)
                b_copy(j + 1)
                b_values(j + 1)

            b_copy(0)
            b_values(0)
            with act.Fori(0, (RT - 1) // 2) as i:
                for h in range(2):
                    b_group(i * 2 + h, h)
            for j in range((RT - 1) // 2 * 2, RT - 1):
                b_group(j, j % 2)
            b_exp(RT - 1, (RT - 1) % 2)
            act.wait_ge(s_ex, 2)
            nc.scalar.activation(one[1][:, :], one[0][:, :], ACT.Sqrt).then_inc(s_sx, 1)
            act.wait_ge(s_ex, 3)
            nc.scalar.activation(sc[1][:, :, :], sc[2][:, :, :], ACT.Exp).then_inc(s_sx, 1)

            def final_out(i, us, rows):
                for u in us:
                    act.wait_ge(f_o, U + i * U + u + 1)
                    act.dma_start(out[bass.ds((i * U + u) * P, rows), :], o_sb[0:rows, u, :]).then_inc(f_st[u], 16)

            with act.Fori(0, STEPS - 1) as i:
                final_out(i, range(U), P)
            final_out(STEPS - 1, [0], LAST)
            for u in range(U):
                act.wait_ge(f_st[u], (STEPS if u == 0 else STEPS - 1) * 16)

        @block.vector
        def _(vec):
            v = nc.vector
            ch = Counter(vec, s_vc)
            vec.wait_ge(s_const, NCONST)
            vec.wait_ge(s_w, 16 * NLOADS)
            ch.step(v.tensor_copy(ident16[:, :], ident[:, :]))

            nb = slice(0, NBIN)

            def views(g):
                p, t = g.EP, g.T
                f = lambda k: g.tmp(k)[0:p, 0:t]
                n = lambda k: g.tmp(k, I32)[0:p, 0:t]
                b16 = g.tmp(8, F16)[0:p, 0:t]
                mk = g.tmp(8, U16)[0:p, TMAX:TMAX + t]
                return f, n, b16, mk

            def payloads(g):
                f, n, b16, mk = views(g)
                p = g.EP
                si, di, a_f, b_f, lo_f, run_i, plo_i, phi_f = n(0), n(1), f(2), f(3), f(0), n(5), n(6), f(7)
                vec.wait_ge(g.s_in, 32)
                ch.step(v.tensor_scalar(si, si, float(N - 1), None, ALU.min))
                ch.step(v.tensor_scalar(plo_i, si, 3, None, ALU.arith_shift_right))
                ch.step(v.tensor_copy(a_f, plo_i))
                ch.step(v.tensor_scalar(plo_i, si, 7, None, ALU.bitwise_and))
                ch.step(v.tensor_scalar(run_i, di, P - 1, None, ALU.bitwise_and))
                ch.step(v.tensor_copy(lo_f, run_i))
                ch.step(v.tensor_scalar(b_f, plo_i, 256.0, 1.0, ALU.mult, ALU.add))
                ch.step(v.tensor_tensor(b_f, b_f, lo_f, ALU.add))
                ch.step(v.tensor_scalar(plo_i, di, 7, None, ALU.arith_shift_right))
                ch.step(v.tensor_scalar(phi_f, di, float(N), 64.0, ALU.is_ge, ALU.mult))
                ch.step(v.tensor_tensor(b16, phi_f, plo_i, ALU.add))
                with v.Fori(0, NBIN) as b:
                    v.tensor_scalar(mk, b16, iobin[0:p, bass.ds(b, 1)], None, ALU.is_equal, ALU.add,
                                    accum_out=g.H[0:p, bass.ds(b, 1)]).then_inc(g.s_hist, 1)
                    vec.wait_ge(g.s_hist, b + 1)

            def starts(g):
                bn, at = g.bn, g.at7
                ch.step(v.tensor_scalar(bni[:, nb], PS[7][:, at:at + NBIN], float(P - 1), None, ALU.add))
                ch.step(v.tensor_scalar(bni[:, nb], bni[:, nb], 7, None, ALU.arith_shift_right))
                ch.step(v.tensor_copy(bn[:, 0, nb], bni[:, nb]))
                ch.step(v.tensor_tensor_scan(bn[:, 1, nb], bn[:, 0, nb], bn[:, 0, nb], 0.0, ALU.add, ALU.max))
                ch.step(v.tensor_tensor(bn[:, 2, nb], bn[:, 1, nb], bn[:, 0, nb], ALU.subtract))
                ch.step(v.scalar_tensor_tensor(bn[:, 3, nb], bn[:, 2, nb], float(P), PS[7][:, at + 64:at + 64 + NBIN],
                                               ALU.mult, ALU.add))
                f, _, _, _ = views(g)
                ch.step(v.memset(f(4), float(1 << 20)))

            def rank_steps(g, b):
                f, _, b16, mk = views(g)
                lc = Counter(vec, g.s_scan, base=b * 3)
                yield lc.step(v.tensor_scalar(mk, b16, iobin[0:g.EP, bass.ds(b, 1)], None, ALU.is_equal))
                yield lc.step(v.tensor_tensor_scan(f(5), mk, mk, g.bn[0:g.EP, 3, bass.ds(b, 1)], ALU.add, ALU.max))
                alone(vec)
                yield lc.step(v.copy_predicated(f(4), mk, f(5)))

            def ranked(g):
                f, n, _, _ = views(g)
                ch.step(v.tensor_scalar(n(5), f(4), -1.0, None, ALU.add))
                ch.step(v.tensor_scalar(n(4), n(5), 7, None, ALU.arith_shift_right))
                ch.step(v.tensor_copy(f(7), n(4)))
                ch.step(v.tensor_scalar(n(4), n(5), P - 1, None, ALU.bitwise_and))
                ch.step(v.tensor_copy(f(6), n(4)))

            def column(g, col, k):
                p = g.EP
                at = lambda a: a[0:p, bass.ds(col, 1)]
                vec.wait_ge(g.s_pl, col + 1)
                v.tensor_scalar(g.oh_hi[0:p, k, 0:g.NT], iota16[0:p, 0:g.NT], at(g1.tmp(7)), None, ALU.is_equal)
                last = v.tensor_scalar(g.oh_lo[0:p, k, 2, :], iota16[0:p, 0:P], at(g1.tmp(6)), None, ALU.is_equal)
                if g.with_degree:
                    v.tensor_scalar(g.oh_lo[0:p, k, 3, :], iota16[0:p, 0:P], at(g1.tmp(0)), None, ALU.is_equal)
                    last = v.tensor_scalar(oh_bin[0:p, k, 0:NBIN], iota16[0:p, 0:NBIN], at(g1.tmp(8, F16)), None, ALU.is_equal)
                last.then_inc(g.s_oh, 1)

            def tables(g):
                bn, tmp = g.bn, g1.tmp
                vec.wait_ge(g.s_done, 1)
                for c, (at, w) in enumerate(g.chunks):
                    bi, hi = tmp(0, I32)[:, at:at + w], tmp(1, I32)[:, at:at + w]
                    ch.step(v.tensor_copy(bi, PS[3 + c][:, 0:w]))
                    ch.step(v.tensor_scalar(hi, bi, 8, None, ALU.arith_shift_right))
                    ch.step(v.scalar_tensor_tensor(g.idx[:, at:at + w], PS[c][:, 0:w], 8.0, hi, ALU.mult, ALU.add))
                    ch.step(v.tensor_scalar(hi, bi, 255, None, ALU.bitwise_and))
                    ch.step(v.tensor_scalar(g.dlo[:, at:at + w], hi, -1.0, None, ALU.add))
                if g is g2:
                    d2, dp = tmp(2, I32)[:, 0:g.NT], tmp(3, I32)[:, 0:g.NT]
                    ch.step(v.tensor_tensor(d2, g.dlo[:, :], g.dlo[:, :], ALU.mult))
                    ch.step(v.tensor_copy(zd[:, :, 0], g.dlo[:, :]))
                    ch.step(v.tensor_scalar(dp, d2, 7, None, ALU.arith_shift_right))
                    ch.step(v.tensor_copy(zd[:, :, 1], dp))
                    ch.step(v.tensor_scalar(dp, d2, P - 1, None, ALU.bitwise_and))
                    ch.step(v.tensor_copy(zd[:, :, 2], dp))
                ch.step(v.tensor_tensor(bn[:, 4, nb], bn[:, 1, nb], ident[:, nb], ALU.mult))
                ch.step(v.reduce_sum(bn[:, 5, 0:1], bn[:, 4, nb], axis=AX.X))
                v.tensor_scalar(g.oh_hi[0:NBIN, 0, 0:g.NT], iota16[0:NBIN, 0:g.NT], bn[0:NBIN, 5, 0:1], None,
                                ALU.is_ge).then_inc(g.s_cmp, 1)
                vec.wait_ge(g.s_row, 1)
                for c, (at, w) in enumerate(g.chunks):
                    last = v.tensor_scalar(g.row[0:1, at:at + w], PS[c][0:1, 0:w], float(g.row_stride), None, ALU.mult)
                ch.step(last)
                if g.with_degree:
                    v.tensor_scalar(one[0][:, nb], PS[6][:, nb], 1.0, None, ALU.add).then_inc(s_deg, 1)
                    vec.wait_ge(s_degq, 1)
                    ch.step(v.reciprocal(dinv[:, nb], one[1][:, nb]))
                vec.sem_inc(g.s_ready, 1)

            def phase(k, s, first):
                vec.sem_inc(s["xn"], U)
                if k == 2:
                    vec.sem_inc(s["x2"], U)
                with v.Fori(0, STEPS) as i:
                    per = 1 if k == 1 else 4
                    lc = Counter(vec, s["dv"], base=i * {0: 10, 1: 4, 2: 14}[k])
                    tile = lambda u: acc[:, bass.ds((i * U + u) * D, D)]
                    dcol = lambda u: dinv[:, bass.ds(i * U + u, 1)]
                    if k == 1:
                        for u in range(U):
                            lc.inc(v.scalar_tensor_tensor(x2t[:, u, :], tile(u), dcol(u), bias[0][:, :], ALU.mult, ALU.add))
                        lc.wait()
                        for u in range(U):
                            vec.wait_ge(s["tp"], i * U + u + 1)
                            v.tensor_scalar(xn[:, u, :], x2t[:, u, :], 0.0, None, ALU.max).then_inc(s["xn"], 1)
                        vec.wait_ge(s["xn"], U + (i + 1) * U)
                    else:
                        srct = xt
                        if k == 2:
                            for u in range(U):
                                vec.wait_ge(s["x"][u], (i + 1) * 16)
                                vec.wait_ge(s["free"], i * U + u + 1)
                                lc.inc(v.scalar_tensor_tensor(x2t[:, u, :], tile(u), dcol(u), xt[:, u, :], ALU.mult, ALU.add))
                            lc.wait()
                            for u in range(U):
                                v.tensor_tensor(x2t[:, u, :], x2t[:, u, :], bias[1][:, :], ALU.add).then_inc(s["x2"], 1)
                            vec.wait_ge(s["x2"], U + (i + 1) * U)
                            srct = x2t
                        for u in range(U):
                            if k == 0:
                                vec.wait_ge(s["x"][u], (i + 1) * 16)
                            lc.inc(v.bn_stats(st6[:, u, :], srct[:, u, :]))
                        lc.wait()
                        alone(vec)
                        for u in range(U):
                            lc.inc(v.bn_aggr(mv[:, u, 0:2], st6[:, u, :]))
                        lc.wait()
                        v.tensor_scalar(mv[:, :, 2], mv[:, :, 1], LN_EPS, None, ALU.add).then_inc(s["var"], 1)
                        vec.wait_ge(s["sq"], i + 1)
                        lc.step(v.reciprocal(mv[:, :, 2], mv[:, :, 3]))
                        for u in range(U):
                            vec.wait_ge(s["tp"], i * U + u + 1)
                            v.tensor_scalar(xn[:, u, :], srct[:, u, :], mv[:, u, 0:1], mv[:, u, 2:3],
                                            ALU.subtract, ALU.mult).then_inc(s["xn"], 1)
                        lc.step(v.tensor_copy(one[0][:, 0:1], mv[:, 0, 0:1]))
                    assert lc.n == {0: 10, 1: 4, 2: 14}[k]

            def one_hots(g, j, out_):
                return v.tensor_tensor(out_, iota32[:, :].unsqueeze(1).to_broadcast([P, G, P]),
                                       g.dlo[:, bass.ds(j * G, G)].unsqueeze(2).to_broadcast([P, G, P]), ALU.is_equal)

            row_regs = [vec.alloc_register(f"dve_bin{k}") for k in range(G)]

            def bins(g, i, top):
                vec.load(row_regs, g.row[0:1, bass.ds(i * G, G)])
                return [vec.snap(r, min_val=0, max_val=top) for r in row_regs]

            def conv(part):
                c, (first, _) = cv[part], parts2[part]

                def hots(j, h):
                    one_hots(g1, j, SC[:, h % 2, :, :]).then_inc(c["s"], 1)

                def group(j, h, col, end):
                    if end is None or j + 1 < NG:
                        hots(j + 1, h + 1)
                    offs = bins(g1, j, NBIN * D)
                    for k in range(G):
                        if k in PLACE_AT:
                            q = PLACE_AT.index(k) + LEAD
                            if end is None or col + q < end:
                                column(g2, col + q, (h * W + q) % 4)
                        vec.wait_ge(c["used"], G + j * G + k + 1)
                        vec.wait_ge(c["add"], 2 + j * G + k)
                        a = acc[:, bass.ds(offs[k], D)]
                        v.tensor_tensor(a, a, PS[6 + k % 2][:, 0:D], ALU.add).then_inc(c["add"], 1)

                vec.sem_inc(c["add"], 2)
                hots(0, 0)
                for q in range(LEAD):
                    column(g2, first + q, q)
                groups(v, part, group)
                vec.wait_ge(c["add"], 2 + g1.NT)

            payloads(g1)
            payloads(g2)
            vec.wait_ge(s_pre, 1)
            starts(g1)
            starts(g2)
            with v.Fori(0, NBIN) as b:
                for _ in rank_steps(g1, b):
                    pass
            ranked(g1)

            def quad(i):
                for k in range(4):
                    column(g1, i * 4 + k, k)

            quads = g1.T // 4
            per_bin = quads // NBIN
            assert per_bin >= 3
            with v.Fori(0, NBIN) as b:
                steps = rank_steps(g2, b)
                for q in range(per_bin):
                    quad(b * per_bin + q)
                    if q < 3:
                        next(steps)
            with v.Fori(NBIN * per_bin, quads) as i:
                quad(i)
            ranked(g2)
            vec.wait_ge(g1.s_done, 1)
            for k in (2, 3, 6, 7):
                ch.step(v.tensor_copy(g1.tmp(k)[:, 0:g2.T], g2.tmp(k)[:, 0:g2.T]))
            tables(g1)
            phase(0, ph[0], True)
            vec.wait_ge(ph[0]["st"], 16 * STEPS)
            conv(0)
            phase(1, ph[1], False)
            vec.wait_ge(ph[1]["st"], 16 * STEPS)
            conv(1)
            tables(g2)
            phase(2, ph[2], False)

            bc = lambda k: vecs[:, k, :].unsqueeze(1).to_broadcast([P, NBP, HE])
            he = lambda a: a.rearrange("p t (h e) -> p t h e", h=HEADS)
            hb = lambda a: a.unsqueeze(3).to_broadcast([P, NBP, HEADS, EXPERTS])
            w0, w1 = big[:, 0, :, :], big[:, 1, :, :]
            h4 = slice(0, HEADS)
            vec.wait_ge(ph[2]["ev"], 2 + NBP)
            ch.step(v.tensor_tensor(w0, tg[:, :, 0:HE], bc(0), ALU.mult))
            ch.step(v.tensor_tensor(w1, tg[:, :, 0:HE], bc(1), ALU.mult))
            ch.step(v.reduce_sum(adst[:, :, :], he(w1), axis=AX.X))
            v.reduce_sum(tg[:, :, HE:REC], he(w0), axis=AX.X).then_inc(s_rec, 1)
            vec.wait_ge(s_rec, 1)
            mxv = mx[:, :].rearrange("p (t s) -> p t s", s=SEL)
            ch.step(v.tensor_copy(mxv[:, :, 0:HEADS], tg[:, :, HE:REC]))

            def add_bias(e, c, j):
                n = e * CH + c
                vec.wait_ge(s_ym, 1 + n * 4 + j + 1)
                vec.wait_ge(s_ys[j], (n + 1) * 16)
                v.tensor_tensor(y_sb[:, j, :], PS[2 + j % 2][:, 0:D], b2s[:, bass.ds(e * D, D)],
                                ALU.add).then_inc(s_ye, 1)

            vec.wait_ge(s_lm, 10)
            sq, sqf, sqi = [tiles[:, at * P:(at + w) * P].rearrange("p (j n) -> p j n", n=P)
                            for at, w in ((0, 1), (1, 2), (3, 2))]
            sq, sqi = sq[:, 0, :], sqi.bitcast(I32)
            ch.step(v.tensor_tensor(sq, iota32[:, :], iota32[:, :], ALU.mult))
            ch.step(v.tensor_copy(sqi[:, 0, :], sq))
            ch.step(v.tensor_scalar(sqi[:, 1, :], sqi[:, 0, :], 7, None, ALU.arith_shift_right))
            ch.step(v.tensor_scalar(sqi[:, 0, :], sqi[:, 0, :], P - 1, None, ALU.bitwise_and))
            ch.step(v.tensor_copy(sqf[:, 0, :], sqi[:, 1, :]))
            ch.step(v.tensor_copy(sqf[:, 1, :], sqi[:, 0, :]))
            for k in range(G):
                ch.step(v.tensor_scalar(sq, iota32[:, :], LC[:, 0, k:k + 1], LC[:, 1, k:k + 1], ALU.mult, ALU.add))
                ch.step(v.scalar_tensor_tensor(sq, sqf[:, 0, :], LC[:, 2, k:k + 1], sq, ALU.mult, ALU.add))
                ch.step(v.scalar_tensor_tensor(LM[:, k, :], sqf[:, 1, :], LC[:, 3, k:k + 1], sq, ALU.mult, ALU.add))
            vec.sem_inc(s_zd, 1)

            def a_front(j, h):
                vec.wait_ge(s_pc, j + 1)
                rec = R[:, bass.ds(j * (G * REC), G * REC)].rearrange("p (k r) -> p k r", k=G)
                a_src = rec[:, :, HE:REC]
                part = [Z[:, h, 0:96].rearrange("p (k q) -> p k q", k=G)[:, :, 4 * p:4 * p + 4] for p in range(3)]
                lc = Counter(vec, a_c, base=j * 5)
                lc.inc(v.tensor_copy(Z[:, h, 96:120].rearrange("p (k q) -> p k q", q=3), zd[:, bass.ds(j * G, G), :]))
                lc.step(v.tensor_copy(part[0], a_src))
                lc.step(v.tensor_tensor(asr[:, 0, :, :], a_src, part[0], ALU.subtract))
                lc.step(v.tensor_copy(part[1], asr[:, 0, :, :]))
                lc.step(v.tensor_tensor(asr[:, 1, :, :], asr[:, 0, :, :], part[1], ALU.subtract))
                assert lc.n == 5
                v.tensor_copy(part[2], asr[:, 1, :, :]).then_inc(a_z, 1)

            def a_back(j, banks=(6, 7), piece=None):
                offs = bins(g2, j, NBIN * SEL)
                lc = Counter(vec, a_d, base=j * G)
                for k in range(G + 1):
                    if k < G:
                        vec.wait_ge(a_m, j * G + k + 1)
                        v.tensor_reduce(red[:, k, :], PS[banks[k % len(banks)]][:, :].rearrange("p (h n) -> p h n", h=HEADS),
                                        AX.X, ALU.max).then_inc(a_r, 1)
                    if k > 0:
                        vec.wait_ge(a_r, len(banks) + j * G + k)
                        if k > 1:
                            lc.wait()
                        m = mx[:, bass.ds(offs[k - 1], HEADS)]
                        lc.inc(v.tensor_tensor(m, m, red[:, k - 1, :], ALU.max))
                        if piece is not None and k % 2 == 0:
                            piece(k // 2 - 1)
                lc.wait()

            vec.sem_inc(s_ye, 2)
            vec.sem_inc(a_r, 2)
            a_front(0, 0)
            with v.Fori(0, EXPERTS) as e:
                with v.Fori(0, CH) as c:
                    i = e * CH + c
                    a_front(i * 2 + 1, 1)
                    a_back(i * 2)
                    a_front(i * 2 + 2, 0)
                    a_back(i * 2 + 1, piece=lambda j: add_bias(e, c, j))
            vec.sem_inc(a_r, 2)
            with v.Fori(EXPERTS * CH, RT // 2 - 1) as i:
                a_front(i * 2 + 1, 1)
                a_back(i * 2, (6, 7, 0, 1))
                a_front(i * 2 + 2, 0)
                a_back(i * 2 + 1, (6, 7, 0, 1))
            a_front(RT - 1, 1)
            a_back(RT - 2, (6, 7, 0, 1))
            a_back(RT - 1, (6, 7, 0, 1))

            ch.step(v.tensor_copy(v8[:, :, h4], adst[:, :, :]))
            ch.step(v.tensor_tensor(r8[:, :, h4], mxv[:, :, h4], adst[:, :, :], ALU.add))
            ch.step(v.scalar_tensor_tensor(v8[:, :, 4:8], r8[:, :, h4], 0.2, r8[:, :, h4], ALU.mult, ALU.max))
            adpv = adp[:, :].rearrange("p (t s) -> p t s", s=SEL)
            ch.step(v.tensor_copy(adpv[:, :, 0:8], v8[:, :, :]))
            ch.step(v.tensor_tensor(r8[:, :, :], v8[:, :, :], adpv[:, :, 0:8], ALU.subtract))
            ch.step(v.tensor_copy(adpv[:, :, 8:16], r8[:, :, :]))
            ch.step(v.tensor_tensor(r8[:, :, :], r8[:, :, :], adpv[:, :, 8:16], ALU.subtract))
            v.tensor_copy(adpv[:, :, 16:24], r8[:, :, :]).then_inc(s_adp, 1)
            ch.step(v.tensor_tensor(w0[:, :, h4], tg[:, :, HE:REC], adst[:, :, :], ALU.add))
            ch.step(v.scalar_tensor_tensor(w1[:, :, h4], w0[:, :, h4], 0.2, w0[:, :, h4], ALU.mult, ALU.max))
            v.tensor_tensor(w1[:, :, h4], w1[:, :, h4], v8[:, :, 4:8], ALU.subtract).then_inc(s_ex, 1)
            vec.wait_ge(s_sx, 1)
            acc2v = acc2[:, :].rearrange("p (t s) -> p t s", s=SEL)
            ch.step(v.tensor_tensor(he(acc2v[:, :, 0:HE]), he(tg[:, :, 0:HE]), hb(acc2v[:, :, HE:REC]), ALU.mult))

            vec.sem_inc(b_a, 2)
            for j in range(4):
                vec.wait_ge(s_ys[j], 16 * (1 + EXPERTS * CH))

            def b_hot(j, h):
                one_hots(g2, j, SB[:, h, :, :]).then_inc(b_s, 1)

            def b_mid(j):
                lc = Counter(vec, b_c, base=j * 4)
                vec.wait_ge(b_sc, 1 + j + 1)
                lc.step(v.tensor_tensor(q8[:, :, :], ssel[:, :, 0:8], ssel[:, :, 8:16], ALU.add))
                lc.step(v.tensor_tensor(q8[:, :, :], q8[:, :, :], ssel[:, :, 16:24], ALU.add))
                rec = R[:, bass.ds(j * (G * REC), G * REC)].rearrange("p (k r) -> p k r", k=G)
                lc.step(v.tensor_tensor(ee[:, 0, :, :], rec[:, :, HE:REC], q8[:, :, h4], ALU.add))
                lc.step(v.scalar_tensor_tensor(ee[:, 1, :, :], ee[:, 0, :, :], 0.2, ee[:, 0, :, :], ALU.mult, ALU.max))
                v.tensor_tensor(ee[:, 2, :, :], ee[:, 1, :, :], q8[:, :, 4:8], ALU.subtract).then_inc(b_e, 1)

            def b_pay(j, h):
                rec = R[:, bass.ds(j * (G * REC), G * REC)].rearrange("p (k r) -> p k r", k=G)
                vec.wait_ge(b_x, j + 1)
                v.tensor_tensor(pay[:, h, :, 0:HE].rearrange("p k (h e) -> p k h e", h=HEADS),
                                rec[:, :, 0:HE].rearrange("p k (h e) -> p k h e", h=HEADS),
                                pay[:, h, :, HE:REC].unsqueeze(3).to_broadcast([P, G, HEADS, EXPERTS]),
                                ALU.mult).then_inc(b_p, 1)

            def b_add(j, h):
                offs = bins(g2, j, NBIN * SEL)
                lc = Counter(vec, b_d, base=j * (G - 1))
                vec.wait_ge(b_o, j + 1)
                for k in range(G):
                    a = acc2[:, bass.ds(offs[k], REC)]
                    ins = v.tensor_tensor(a, a, PS[3 + h][:, k * REC:(k + 1) * REC], ALU.add)
                    if k < G - 1:
                        lc.step(ins)
                    else:
                        ins.then_inc(b_a, 1)
                        vec.wait_ge(b_a, 2 + j + 1)

            def b_group(j, q, hot=True):
                b_mid(j)
                if hot:
                    b_hot(j + 2, (q + 2) % 4)
                b_pay(j, q % 2)
                b_add(j - 1, (q + 1) % 2)

            b_hot(0, 0)
            b_hot(1, 1)
            b_mid(0)
            b_hot(2, 2)
            b_pay(0, 0)
            loops = (RT - 3) // 4
            with v.Fori(0, loops) as i:
                for q in range(4):
                    b_group(i * 4 + (q + 1), (q + 1) % 4)
            for j in range(loops * 4 + 1, RT):
                b_group(j, j % 4, j + 2 < RT)
            b_add(RT - 1, (RT - 1) % 2)

            c16 = lambda a: a.unsqueeze(2).to_broadcast([P, NBP, HE])
            c4 = lambda a: a.unsqueeze(2).to_broadcast([P, NBP, EXPERTS])
            o0, o1 = one[0][:, :], one[1][:, :]
            ch.step(v.tensor_scalar(r8[:, :, h4], acc2v[:, :, HE:REC], 1e-16, None, ALU.add))
            ch.step(v.reciprocal(r8[:, :, 4:8], r8[:, :, h4]))
            ch.step(v.tensor_tensor(he(w0), he(acc2v[:, :, 0:HE]), hb(r8[:, :, 4:8]), ALU.mult))
            ch.step(v.tensor_tensor(w0, w0, bc(2), ALU.add))
            ch.step(v.reduce_sum(o0, w0, axis=AX.X))
            ch.step(v.tensor_scalar(o0, o0, 1.0 / HE, None, ALU.mult))
            ch.step(v.tensor_tensor(w0, w0, c16(o0), ALU.subtract))
            ch.step(v.tensor_tensor(w1, w0, w0, ALU.mult))
            ch.step(v.reduce_sum(o0, w1, axis=AX.X))
            v.tensor_scalar(o0, o0, 1.0 / HE, LN_EPS, ALU.mult, ALU.add).then_inc(s_ex, 1)
            vec.wait_ge(s_sx, 2)
            ch.step(v.reciprocal(o0, o1))
            ch.step(v.tensor_tensor(w0, w0, c16(o0), ALU.mult))
            ch.step(v.tensor_tensor(w0, w0, bc(3), ALU.mult))
            ch.step(v.tensor_tensor(w0, w0, bc(4), ALU.add))
            ch.step(v.reduce_sum(sc[0][:, :, :], w0.rearrange("p t (h e) -> p t e h", h=HEADS), axis=AX.X))
            ch.step(v.tensor_scalar(sc[0][:, :, :], sc[0][:, :, :], 1.0 / HEADS, None, ALU.mult))
            ch.step(v.tensor_reduce(o0, sc[0][:, :, :], AX.X, ALU.max))
            v.tensor_tensor(sc[2][:, :, :], sc[0][:, :, :], c4(o0), ALU.subtract).then_inc(s_ex, 1)
            rank, cmpv = w0[:, :, 0:EXPERTS], w1
            n = 0
            for e in range(EXPERTS):
                for j in range(EXPERTS):
                    if j != e:
                        ch.inc(v.tensor_tensor(cmpv[:, :, n:n + 1], sc[0][:, :, j:j + 1], sc[0][:, :, e:e + 1],
                                               ALU.is_ge if j < e else ALU.is_gt))
                        n += 1
            ch.wait()
            ch.step(v.reduce_sum(rank, w1[:, :, 0:12].rearrange("p t (e j) -> p t e j", e=EXPERTS), axis=AX.X))
            vec.wait_ge(s_sx, 3)
            ch.step(v.scalar_tensor_tensor(sc[2][:, :, :], rank, 2.0, sc[1][:, :, :], ALU.is_lt, ALU.mult))
            ch.step(v.reduce_sum(o0, sc[2][:, :, :], axis=AX.X))
            ch.step(v.reciprocal(o1, o0))
            ch.step(v.tensor_tensor(gate[:, :].rearrange("p (t e) -> p t e", e=EXPERTS), sc[2][:, :, :], c4(o1), ALU.mult))

            vec.sem_inc(f_o, U)

            def final(i, pair, base, first=False):
                lc = Counter(vec, f_c, base=base)
                for u in pair:
                    vec.wait_ge(f_in[u], (i + 1) * 32)
                    if not first:
                        vec.wait_ge(f_st[u], i * 16)
                for e in range(EXPERTS):
                    for u in pair:
                        other = x2_in[:, u, :] if e == 0 else o_sb[:, u, :]
                        ins = v.scalar_tensor_tensor(o_sb[:, u, :], y_in[:, u, e, :],
                                                     gate[:, bass.ds((i * U + u) * EXPERTS + e, 1)], other,
                                                     ALU.mult, ALU.add)
                        if e < EXPERTS - 1:
                            lc.inc(ins)
                        else:
                            ins.then_inc(f_o, 1)
                    lc.wait()

            per = (EXPERTS - 1) * U
            final(0, (0, 1), 0, True)
            final(0, (2, 3), per // 2, True)
            with v.Fori(1, STEPS - 1) as i:
                final(i, (0, 1), i * per)
                final(i, (2, 3), i * per + per // 2)
            final(STEPS - 1, [0], (STEPS - 1) * per)


_INS = ['x', 'src', 'dst', 'L0_gnn_W1', 'L0_gnn_b1', 'L0_gnn_W2', 'L0_gnn_b2', 'L0_ffn_W_gat',
        'L0_ffn_att_src', 'L0_ffn_att_dst', 'L0_ffn_b_gat', 'L0_ffn_ln_gamma', 'L0_ffn_ln_beta',
        'L0_ffn_W1', 'L0_ffn_b1', 'L0_ffn_W2', 'L0_ffn_b2', 'L0_ffn_edge_index']


def kernel(**inputs):
    import numpy as _np
    import concourse.bacc as _bacc
    from concourse import mybir as _mybir
    from concourse.bass_utils import run_bass_kernel_spmd as _run

    nc = _bacc.Bacc("TRN2", target_bir_lowering=False, num_devices=1)
    arrays, args = {}, []
    for name in _INS:
        a = _np.ascontiguousarray(inputs[name])
        arrays[f"in_{name}_dram"] = a
        args.append(nc.dram_tensor(f"in_{name}_dram", a.shape, _mybir.dt.from_np(a.dtype), kind="ExternalInput").ap())
    args.append(nc.dram_tensor("out_0_dram", (N, D), _mybir.dt.float32, kind="ExternalOutput").ap())
    build(nc, *args)
    r = _run(nc, [arrays], core_ids=[0])
    return r.results[0]["out_0_dram"]
```
